# Optimizing a Trainium2 kernel written in Bass

```python
import numpy as np
import jax
import jax.numpy as jnp

def _softmax(x, axis=-1):
    return jax.nn.softmax(x, axis=axis)

def _gelu(x):
    return jax.nn.gelu(x, approximate=True)

def _silu(x):
    return jax.nn.silu(x)

def _sigmoid(x):
    return jax.nn.sigmoid(x)

def _layernorm(x, axis=-1, eps=1e-05):
    m = jnp.mean(x, axis=axis, keepdims=True)
    v = jnp.var(x, axis=axis, keepdims=True)
    return (x - m) / jnp.sqrt(v + eps)

def _scatter_add(tgt, idx, src, axis=0):
    return tgt.at[idx].add(src)

def _segment_sum(src, seg, n):
    return jax.ops.segment_sum(src, seg, n)
kernel_name = 'mk_adaln_d2_jaxref_r4_b19291'

def setup_inputs(seed: int=0):
    np.random.seed(seed)
    _w = jnp.asarray

    def _L0_attn_setup():
        import jax, jax.numpy as jnp
        import numpy as np
        D_MODEL = 256
        N_HEADS = 16
        HEAD_DIM = D_MODEL // N_HEADS
        MAX_SHIFT = HEAD_DIM // 2
        BATCH, SEQ = (2, 512)

        def _forward(x, Wq, bq, Wk, bk, Wv, bv, Wo, bo, W_cross, shift_weights, gate):
            b, s, _ = x.shape
            H, hd = (W_cross.shape[0], W_cross.shape[1])
            ms = shift_weights.shape[1]
            Q = (x @ Wq.T + bq).reshape(b, s, H, hd)
            K = (x @ Wk.T + bk).reshape(b, s, H, hd)
            V = (x @ Wv.T + bv).reshape(b, s, H, hd)
            Qt = jnp.einsum('bqhf,hfg->bqhg', Q, W_cross)
            scores_cross = jnp.einsum('bqhd,bkhd->bhqk', Qt, K)
            f = jnp.arange(hd)[:, None]
            g = jnp.arange(hd)[None, :]
            tau = g - f
            valid = (tau >= 0) & (tau < ms)
            M = jnp.where(valid[None], shift_weights[:, jnp.clip(tau, 0, ms - 1)], 0.0)
            K_mixed = jnp.einsum('hfg,bkhg->bkhf', M, K)
            scores_conv = jnp.einsum('bqhf,bkhf->bhqk', Q, K_mixed)
            gt = jax.nn.sigmoid(gate).reshape(1, H, 1, 1)
            scale = hd ** (-0.5)
            scores = (gt * scores_cross + (1.0 - gt) * scores_conv) * scale
            causal = jnp.tril(jnp.ones((s, s), dtype=bool))
            scores = jnp.where(causal[None, None], scores, -jnp.inf)
            attn = jax.nn.softmax(scores, axis=-1)
            out = jnp.einsum('bhqk,bkhd->bqhd', attn, V).reshape(b, s, H * hd)
            return out @ Wo.T + bo
        key = jax.random.key(seed)
        ks = jax.random.split(key, 12)
        s = 0.02
        x = jax.random.normal(ks[0], (BATCH, SEQ, D_MODEL), dtype=jnp.float32)
        Wq = jax.random.normal(ks[1], (D_MODEL, D_MODEL), dtype=jnp.float32) * s
        bq = jnp.zeros((D_MODEL,), jnp.float32)
        Wk = jax.random.normal(ks[2], (D_MODEL, D_MODEL), dtype=jnp.float32) * s
        bk = jnp.zeros((D_MODEL,), jnp.float32)
        Wv = jax.random.normal(ks[3], (D_MODEL, D_MODEL), dtype=jnp.float32) * s
        bv = jnp.zeros((D_MODEL,), jnp.float32)
        Wo = jax.random.normal(ks[4], (D_MODEL, D_MODEL), dtype=jnp.float32) * s
        bo = jnp.zeros((D_MODEL,), jnp.float32)
        eye = jnp.broadcast_to(jnp.eye(HEAD_DIM, dtype=jnp.float32), (N_HEADS, HEAD_DIM, HEAD_DIM))
        W_cross = eye + 0.01 * jax.random.normal(ks[5], (N_HEADS, HEAD_DIM, HEAD_DIM), dtype=jnp.float32)
        decay = jnp.exp(-jnp.arange(MAX_SHIFT, dtype=jnp.float32) / (MAX_SHIFT / 4.0))
        shift_weights = jnp.broadcast_to(decay, (N_HEADS, MAX_SHIFT)).copy()
        gate = jnp.zeros((N_HEADS,), jnp.float32)
        return {'x': x, 'Wq': Wq, 'bq': bq, 'Wk': Wk, 'bk': bk, 'Wv': Wv, 'bv': bv, 'Wo': Wo, 'bo': bo, 'W_cross': W_cross, 'shift_weights': shift_weights, 'gate': gate}
    _L0_attn_in = _L0_attn_setup()

    def _L0_ffn_setup():
        import jax, jax.numpy as jnp
        import numpy as np
        D_IN, D_HID = (256, 1024)

        def _ternary(key, shape):
            return jax.random.randint(key, shape, -1, 2).astype(jnp.float32)

        def _tlin(x, w, s):
            return jnp.einsum('bsi,oi->bso', x, w) * s
        key = jax.random.key(seed)
        ks = jax.random.split(key, 12)
        inv = lambda fan: 1.0 / np.sqrt(fan).astype(np.float32)
        return {'x': jax.random.normal(ks[0], (4, 512, D_IN), dtype=jnp.float32), 'w1_w': _ternary(ks[1], (D_HID, D_IN)), 'w1_s': jax.random.uniform(ks[2], (D_HID,), dtype=jnp.float32) * inv(D_IN), 'w2_w': _ternary(ks[3], (D_HID, D_IN)), 'w2_s': jax.random.uniform(ks[4], (D_HID,), dtype=jnp.float32) * inv(D_IN), 'h1_w': _ternary(ks[5], (D_HID, D_HID)), 'h1_s': jax.random.uniform(ks[6], (D_HID,), dtype=jnp.float32) * inv(D_HID), 'h2_w': _ternary(ks[7], (D_HID, D_HID)), 'h2_s': jax.random.uniform(ks[8], (D_HID,), dtype=jnp.float32) * inv(D_HID), 'w3_w': _ternary(ks[9], (D_IN, D_HID)), 'w3_s': jax.random.uniform(ks[10], (D_IN,), dtype=jnp.float32) * inv(D_HID)}
    _L0_ffn_in = _L0_ffn_setup()
    _L0_c = _w((lambda *s: np.random.randn(*s).astype(np.float32) * 0.05)(2, 256))
    _L0_wmod = _w((lambda *s: np.random.randn(*s).astype(np.float32) * 0.05)(256, 6 * 256) * 256 ** (-0.5))

    def _L1_attn_setup():
        import jax, jax.numpy as jnp
        import numpy as np
        import math
        from jax import lax
        B, L, D = (8, 1024, 256)
        FILTER_ORDER = 64
        EMB_DIM = 3
        SHIFT = 0.05
        KSIZE = 3

        def _implicit_filter(f_w1, f_b1, freq1, f_w2, f_b2, freq2, f_w3, f_b3, freq3, f_wout):
            t = jnp.linspace(0.0, 1.0, L)
            t_resc = jnp.linspace(0.0, L - 1.0, L)
            w = 2.0 * jnp.pi * t_resc / L
            bands = (EMB_DIM - 1) // 2
            f = jnp.linspace(0.0001, bands - 1.0, bands)
            fw = f[None, :] * w[:, None]
            z = jnp.concatenate([t[:, None], jnp.cos(fw), -jnp.sin(fw)], axis=-1)
            h = jnp.sin(freq1 * (z @ f_w1 + f_b1))
            h = jnp.sin(freq2 * (h @ f_w2 + f_b2))
            h = jnp.sin(freq3 * (h @ f_w3 + f_b3))
            h = h @ f_wout
            max_decay = math.log(0.01) / 0.3
            min_decay = math.log(0.01) / 1.5
            deltas = jnp.linspace(min_decay, max_decay, D)
            decay = jnp.exp(-t[:, None] * jnp.abs(deltas)[None, :])
            return h * (decay + SHIFT)
        key = jax.random.key(seed)
        ks = jax.random.split(key, 12)
        s = 0.02
        return {'u': jax.random.normal(ks[0], (B, L, D), jnp.float32), 'w_in': jax.random.normal(ks[1], (D, 3 * D), jnp.float32) * s, 'b_in': jnp.zeros((3 * D,), jnp.float32), 'sf_w': jax.random.normal(ks[2], (3 * D, KSIZE), jnp.float32) * 0.3, 'sf_b': jnp.zeros((3 * D,), jnp.float32), 'f_w1': jax.random.normal(ks[3], (EMB_DIM, FILTER_ORDER), jnp.float32) * 0.5, 'f_b1': jnp.zeros((FILTER_ORDER,), jnp.float32), 'freq1': jnp.ones((FILTER_ORDER,), jnp.float32), 'f_w2': jax.random.normal(ks[4], (FILTER_ORDER, FILTER_ORDER), jnp.float32) * 0.12, 'f_b2': jnp.zeros((FILTER_ORDER,), jnp.float32), 'freq2': jnp.ones((FILTER_ORDER,), jnp.float32), 'f_w3': jax.random.normal(ks[5], (FILTER_ORDER, FILTER_ORDER), jnp.float32) * 0.12, 'f_b3': jnp.zeros((FILTER_ORDER,), jnp.float32), 'freq3': jnp.ones((FILTER_ORDER,), jnp.float32), 'f_wout': jax.random.normal(ks[6], (FILTER_ORDER, D), jnp.float32) * s, 'filt_bias': jax.random.normal(ks[7], (D,), jnp.float32), 'w_out': jax.random.normal(ks[8], (D, D), jnp.float32) * s, 'b_out': jnp.zeros((D,), jnp.float32)}
    _L1_attn_in = _L1_attn_setup()

    def _L1_ffn_setup():
        import jax, jax.numpy as jnp
        import numpy as np
        DIM = 256
        DEPTH = 2
        HEADS = 8
        DIM_HEAD = 64
        WINDOW = 128
        INNER = HEADS * DIM_HEAD
        HID = int(DIM * 4 * 2 / 3)
        B, N = (2, 2048)
        QK_SCALE = 8.0

        def shift_token(t):
            t1, t2 = jnp.split(t, 2, axis=-1)
            t2 = jnp.pad(t2, ((0, 0), (1, 0), (0, 0)))[:, :-1]
            return jnp.concatenate([t1, t2], axis=-1)

        def l2norm(t):
            return t / jnp.clip(jnp.linalg.norm(t, axis=-1, keepdims=True), 1e-12)

        def rotate_half(x):
            x1, x2 = jnp.split(x, 2, axis=-1)
            return jnp.concatenate([-x2, x1], axis=-1)

        def rotary_xpos(q, k):
            n = q.shape[-2]
            half_idx = jnp.arange(0, DIM_HEAD, 2, dtype=jnp.float32)
            inv_freq = 1.0 / 10000.0 ** (half_idx / DIM_HEAD)
            t = jnp.arange(n, dtype=jnp.float32)
            freqs = t[:, None] * inv_freq[None, :]
            freqs = jnp.concatenate([freqs, freqs], axis=-1)
            base = (half_idx + 0.4 * DIM_HEAD) / (1.4 * DIM_HEAD)
            power = (t - n // 2) / float(WINDOW // 2)
            scale = base[None, :] ** power[:, None]
            scale = jnp.concatenate([scale, scale], axis=-1)
            cos, sin = (jnp.cos(freqs), jnp.sin(freqs))
            q = q * cos * scale + rotate_half(q) * sin * scale
            k = k * cos / scale + rotate_half(k) * sin / scale
            return (q, k)

        def local_attention(q, k, v):
            b, h, n, d = q.shape
            w = n // WINDOW
            bq = q.reshape(b, h, w, WINDOW, d) * QK_SCALE
            bk = k.reshape(b, h, w, WINDOW, d)
            bv = v.reshape(b, h, w, WINDOW, d)

            def look_around(t):
                p = jnp.pad(t, ((0, 0), (0, 0), (1, 0), (0, 0), (0, 0)))
                return jnp.concatenate([p[:, :, :w], p[:, :, 1:]], axis=3)
            bk, bv = (look_around(bk), look_around(bv))
            bt = jnp.arange(n).reshape(w, WINDOW)
            btp = jnp.pad(bt, ((1, 0), (0, 0)), constant_values=-1)
            btk = jnp.concatenate([btp[:w], btp[1:]], axis=1)
            sim = jnp.einsum('bhwid,bhwjd->bhwij', bq, bk)
            i = bt[:, :, None]
            j = btk[:, None, :]
            mask = (i < j) | (i > j + WINDOW) | (j == -1)
            sim = jnp.where(mask, -jnp.finfo(sim.dtype).max, sim)
            attn = jax.nn.softmax(sim, axis=-1)
            out = jnp.einsum('bhwij,bhwjd->bhwid', attn, bv)
            return out.reshape(b, h, n, d)

        def _layer(x, wqkv, qs, ksc, wo, lg, lb, w1, b1, w2, b2):
            b, n, _ = x.shape
            h = shift_token(x)
            qkv = h @ wqkv
            q, k, v = jnp.split(qkv, 3, axis=-1)
            to_heads = lambda t: t.reshape(b, n, HEADS, DIM_HEAD).transpose(0, 2, 1, 3)
            q, k, v = (to_heads(q), to_heads(k), to_heads(v))
            q = l2norm(q) * qs
            k = l2norm(k) * ksc
            q, k = rotary_xpos(q, k)
            o = local_attention(q, k, v)
            o = o.transpose(0, 2, 1, 3).reshape(b, n, INNER)
            x = x + o @ wo
            h = shift_token(x)
            mu = h.mean(-1, keepdims=True)
            var = h.var(-1, keepdims=True)
            h = (h - mu) / jnp.sqrt(var + 1e-05) * lg + lb
            h = h @ w1 + b1
            a, g = jnp.split(h, 2, axis=-1)
            h = a * jax.nn.gelu(g, approximate=False)
            x = x + h @ w2 + b2
            return x
        key = jax.random.key(seed)
        ks = jax.random.split(key, 6)
        return {'x': jax.random.normal(ks[0], (B, N, DIM), jnp.float32), 'wqkv': jax.random.normal(ks[1], (DEPTH, DIM, 3 * INNER), jnp.float32) * 0.02, 'q_scale': jnp.ones((DEPTH, DIM_HEAD), jnp.float32), 'k_scale': jnp.ones((DEPTH, DIM_HEAD), jnp.float32), 'wo': jax.random.normal(ks[2], (DEPTH, INNER, DIM), jnp.float32) * 0.02, 'ln_g': jnp.ones((DEPTH, DIM), jnp.float32), 'ln_b': jnp.zeros((DEPTH, DIM), jnp.float32), 'w1': jax.random.normal(ks[3], (DEPTH, DIM, 2 * HID), jnp.float32) * 0.02, 'b1': jnp.zeros((DEPTH, 2 * HID), jnp.float32), 'w2': jax.random.normal(ks[4], (DEPTH, HID, DIM), jnp.float32) * 0.02, 'b2': jnp.zeros((DEPTH, DIM), jnp.float32)}
    _L1_ffn_in = _L1_ffn_setup()
    _L1_c = _w((lambda *s: np.random.randn(*s).astype(np.float32) * 0.05)(2, 256))
    _L1_wmod = _w((lambda *s: np.random.randn(*s).astype(np.float32) * 0.05)(256, 6 * 256) * 256 ** (-0.5))
    _d = {'L0_attn_x': _L0_attn_in['x'], 'L0_attn_Wq': _L0_attn_in['Wq'], 'L0_attn_bq': _L0_attn_in['bq'], 'L0_attn_Wk': _L0_attn_in['Wk'], 'L0_attn_bk': _L0_attn_in['bk'], 'L0_attn_Wv': _L0_attn_in['Wv'], 'L0_attn_bv': _L0_attn_in['bv'], 'L0_attn_Wo': _L0_attn_in['Wo'], 'L0_attn_bo': _L0_attn_in['bo'], 'L0_attn_W_cross': _L0_attn_in['W_cross'], 'L0_attn_shift_weights': _L0_attn_in['shift_weights'], 'L0_attn_gate': _L0_attn_in['gate'], 'L0_ffn_w1_w': _L0_ffn_in['w1_w'], 'L0_ffn_w1_s': _L0_ffn_in['w1_s'], 'L0_ffn_w2_w': _L0_ffn_in['w2_w'], 'L0_ffn_w2_s': _L0_ffn_in['w2_s'], 'L0_ffn_h1_w': _L0_ffn_in['h1_w'], 'L0_ffn_h1_s': _L0_ffn_in['h1_s'], 'L0_ffn_h2_w': _L0_ffn_in['h2_w'], 'L0_ffn_h2_s': _L0_ffn_in['h2_s'], 'L0_ffn_w3_w': _L0_ffn_in['w3_w'], 'L0_ffn_w3_s': _L0_ffn_in['w3_s'], 'L0_c': _L0_c, 'L0_wmod': _L0_wmod, 'L1_attn_w_in': _L1_attn_in['w_in'], 'L1_attn_b_in': _L1_attn_in['b_in'], 'L1_attn_sf_w': _L1_attn_in['sf_w'], 'L1_attn_sf_b': _L1_attn_in['sf_b'], 'L1_attn_f_w1': _L1_attn_in['f_w1'], 'L1_attn_f_b1': _L1_attn_in['f_b1'], 'L1_attn_freq1': _L1_attn_in['freq1'], 'L1_attn_f_w2': _L1_attn_in['f_w2'], 'L1_attn_f_b2': _L1_attn_in['f_b2'], 'L1_attn_freq2': _L1_attn_in['freq2'], 'L1_attn_f_w3': _L1_attn_in['f_w3'], 'L1_attn_f_b3': _L1_attn_in['f_b3'], 'L1_attn_freq3': _L1_attn_in['freq3'], 'L1_attn_f_wout': _L1_attn_in['f_wout'], 'L1_attn_filt_bias': _L1_attn_in['filt_bias'], 'L1_attn_w_out': _L1_attn_in['w_out'], 'L1_attn_b_out': _L1_attn_in['b_out'], 'L1_ffn_wqkv': _L1_ffn_in['wqkv'], 'L1_ffn_q_scale': _L1_ffn_in['q_scale'], 'L1_ffn_k_scale': _L1_ffn_in['k_scale'], 'L1_ffn_wo': _L1_ffn_in['wo'], 'L1_ffn_ln_g': _L1_ffn_in['ln_g'], 'L1_ffn_ln_b': _L1_ffn_in['ln_b'], 'L1_ffn_w1': _L1_ffn_in['w1'], 'L1_ffn_b1': _L1_ffn_in['b1'], 'L1_ffn_w2': _L1_ffn_in['w2'], 'L1_ffn_b2': _L1_ffn_in['b2'], 'L1_c': _L1_c, 'L1_wmod': _L1_wmod}
    _x0 = _d['L0_attn_x']
    _d['L0_attn_x'] = jax.random.normal(jax.random.fold_in(jax.random.key(seed), 1), (2, 2048, 256), dtype=_x0.dtype)
    del _x0
    return _d

def reference(L0_attn_x, L0_attn_Wq, L0_attn_bq, L0_attn_Wk, L0_attn_bk, L0_attn_Wv, L0_attn_bv, L0_attn_Wo, L0_attn_bo, L0_attn_W_cross, L0_attn_shift_weights, L0_attn_gate, L0_ffn_w1_w, L0_ffn_w1_s, L0_ffn_w2_w, L0_ffn_w2_s, L0_ffn_h1_w, L0_ffn_h1_s, L0_ffn_h2_w, L0_ffn_h2_s, L0_ffn_w3_w, L0_ffn_w3_s, L0_c, L0_wmod, L1_attn_w_in, L1_attn_b_in, L1_attn_sf_w, L1_attn_sf_b, L1_attn_f_w1, L1_attn_f_b1, L1_attn_freq1, L1_attn_f_w2, L1_attn_f_b2, L1_attn_freq2, L1_attn_f_w3, L1_attn_f_b3, L1_attn_freq3, L1_attn_f_wout, L1_attn_filt_bias, L1_attn_w_out, L1_attn_b_out, L1_ffn_wqkv, L1_ffn_q_scale, L1_ffn_k_scale, L1_ffn_wo, L1_ffn_ln_g, L1_ffn_ln_b, L1_ffn_w1, L1_ffn_b1, L1_ffn_w2, L1_ffn_b2, L1_c, L1_wmod):

    def _L0_attn_ref(x, Wq, bq, Wk, bk, Wv, bv, Wo, bo, W_cross, shift_weights, gate):
        import jax, jax.numpy as jnp
        import numpy as np
        D_MODEL = 256
        N_HEADS = 16
        HEAD_DIM = D_MODEL // N_HEADS
        MAX_SHIFT = HEAD_DIM // 2
        BATCH, SEQ = (2, 512)

        def _forward(x, Wq, bq, Wk, bk, Wv, bv, Wo, bo, W_cross, shift_weights, gate):
            b, s, _ = x.shape
            H, hd = (W_cross.shape[0], W_cross.shape[1])
            ms = shift_weights.shape[1]
            Q = (x @ Wq.T + bq).reshape(b, s, H, hd)
            K = (x @ Wk.T + bk).reshape(b, s, H, hd)
            V = (x @ Wv.T + bv).reshape(b, s, H, hd)
            Qt = jnp.einsum('bqhf,hfg->bqhg', Q, W_cross)
            scores_cross = jnp.einsum('bqhd,bkhd->bhqk', Qt, K)
            f = jnp.arange(hd)[:, None]
            g = jnp.arange(hd)[None, :]
            tau = g - f
            valid = (tau >= 0) & (tau < ms)
            M = jnp.where(valid[None], shift_weights[:, jnp.clip(tau, 0, ms - 1)], 0.0)
            K_mixed = jnp.einsum('hfg,bkhg->bkhf', M, K)
            scores_conv = jnp.einsum('bqhf,bkhf->bhqk', Q, K_mixed)
            gt = jax.nn.sigmoid(gate).reshape(1, H, 1, 1)
            scale = hd ** (-0.5)
            scores = (gt * scores_cross + (1.0 - gt) * scores_conv) * scale
            causal = jnp.tril(jnp.ones((s, s), dtype=bool))
            scores = jnp.where(causal[None, None], scores, -jnp.inf)
            attn = jax.nn.softmax(scores, axis=-1)
            out = jnp.einsum('bhqk,bkhd->bqhd', attn, V).reshape(b, s, H * hd)
            return out @ Wo.T + bo
        return _forward(x, Wq, bq, Wk, bk, Wv, bv, Wo, bo, W_cross, shift_weights, gate)

    def _L0_ffn_ref(x, w1_w, w1_s, w2_w, w2_s, h1_w, h1_s, h2_w, h2_s, w3_w, w3_s):
        import jax, jax.numpy as jnp
        import numpy as np
        D_IN, D_HID = (256, 1024)

        def _ternary(key, shape):
            return jax.random.randint(key, shape, -1, 2).astype(jnp.float32)

        def _tlin(x, w, s):
            return jnp.einsum('bsi,oi->bso', x, w) * s
        h = jax.nn.silu(_tlin(x, w1_w, w1_s)) * _tlin(x, w2_w, w2_s)
        h = jax.nn.gelu(_tlin(h, h1_w, h1_s), approximate=False)
        h = jax.nn.gelu(_tlin(h, h2_w, h2_s), approximate=False)
        return _tlin(h, w3_w, w3_s)

    def _L1_attn_ref(u, w_in, b_in, sf_w, sf_b, f_w1, f_b1, freq1, f_w2, f_b2, freq2, f_w3, f_b3, freq3, f_wout, filt_bias, w_out, b_out):
        import jax, jax.numpy as jnp
        import numpy as np
        import math
        from jax import lax
        B, L, D = (8, 1024, 256)
        FILTER_ORDER = 64
        EMB_DIM = 3
        SHIFT = 0.05
        KSIZE = 3

        def _implicit_filter(f_w1, f_b1, freq1, f_w2, f_b2, freq2, f_w3, f_b3, freq3, f_wout):
            t = jnp.linspace(0.0, 1.0, L)
            t_resc = jnp.linspace(0.0, L - 1.0, L)
            w = 2.0 * jnp.pi * t_resc / L
            bands = (EMB_DIM - 1) // 2
            f = jnp.linspace(0.0001, bands - 1.0, bands)
            fw = f[None, :] * w[:, None]
            z = jnp.concatenate([t[:, None], jnp.cos(fw), -jnp.sin(fw)], axis=-1)
            h = jnp.sin(freq1 * (z @ f_w1 + f_b1))
            h = jnp.sin(freq2 * (h @ f_w2 + f_b2))
            h = jnp.sin(freq3 * (h @ f_w3 + f_b3))
            h = h @ f_wout
            max_decay = math.log(0.01) / 0.3
            min_decay = math.log(0.01) / 1.5
            deltas = jnp.linspace(min_decay, max_decay, D)
            decay = jnp.exp(-t[:, None] * jnp.abs(deltas)[None, :])
            return h * (decay + SHIFT)
        b, l, d = u.shape
        up = (u @ w_in + b_in).transpose(0, 2, 1)
        uc = lax.conv_general_dilated(up, sf_w[:, None, :], (1,), [(KSIZE - 1, KSIZE - 1)], feature_group_count=3 * d, dimension_numbers=('NCH', 'OIH', 'NCH'))[..., :l] + sf_b[None, :, None]
        x0, x1, v = jnp.split(uc, 3, axis=1)
        k = _implicit_filter(f_w1, f_b1, freq1, f_w2, f_b2, freq2, f_w3, f_b3, freq3, f_wout).T
        v = v * x1
        n = 2 * l
        y = jnp.fft.irfft(jnp.fft.rfft(v, n=n) * jnp.fft.rfft(k, n=n), n=n)[..., :l]
        v = y + v * filt_bias[None, :, None]
        out = (v * x0).transpose(0, 2, 1)
        return out @ w_out + b_out

    def _L1_ffn_ref(x, wqkv, q_scale, k_scale, wo, ln_g, ln_b, w1, b1, w2, b2):
        import jax, jax.numpy as jnp
        import numpy as np
        DIM = 256
        DEPTH = 2
        HEADS = 8
        DIM_HEAD = 64
        WINDOW = 128
        INNER = HEADS * DIM_HEAD
        HID = int(DIM * 4 * 2 / 3)
        B, N = (2, 2048)
        QK_SCALE = 8.0

        def shift_token(t):
            t1, t2 = jnp.split(t, 2, axis=-1)
            t2 = jnp.pad(t2, ((0, 0), (1, 0), (0, 0)))[:, :-1]
            return jnp.concatenate([t1, t2], axis=-1)

        def l2norm(t):
            return t / jnp.clip(jnp.linalg.norm(t, axis=-1, keepdims=True), 1e-12)

        def rotate_half(x):
            x1, x2 = jnp.split(x, 2, axis=-1)
            return jnp.concatenate([-x2, x1], axis=-1)

        def rotary_xpos(q, k):
            n = q.shape[-2]
            half_idx = jnp.arange(0, DIM_HEAD, 2, dtype=jnp.float32)
            inv_freq = 1.0 / 10000.0 ** (half_idx / DIM_HEAD)
            t = jnp.arange(n, dtype=jnp.float32)
            freqs = t[:, None] * inv_freq[None, :]
            freqs = jnp.concatenate([freqs, freqs], axis=-1)
            base = (half_idx + 0.4 * DIM_HEAD) / (1.4 * DIM_HEAD)
            power = (t - n // 2) / float(WINDOW // 2)
            scale = base[None, :] ** power[:, None]
            scale = jnp.concatenate([scale, scale], axis=-1)
            cos, sin = (jnp.cos(freqs), jnp.sin(freqs))
            q = q * cos * scale + rotate_half(q) * sin * scale
            k = k * cos / scale + rotate_half(k) * sin / scale
            return (q, k)

        def local_attention(q, k, v):
            b, h, n, d = q.shape
            w = n // WINDOW
            bq = q.reshape(b, h, w, WINDOW, d) * QK_SCALE
            bk = k.reshape(b, h, w, WINDOW, d)
            bv = v.reshape(b, h, w, WINDOW, d)

            def look_around(t):
                p = jnp.pad(t, ((0, 0), (0, 0), (1, 0), (0, 0), (0, 0)))
                return jnp.concatenate([p[:, :, :w], p[:, :, 1:]], axis=3)
            bk, bv = (look_around(bk), look_around(bv))
            bt = jnp.arange(n).reshape(w, WINDOW)
            btp = jnp.pad(bt, ((1, 0), (0, 0)), constant_values=-1)
            btk = jnp.concatenate([btp[:w], btp[1:]], axis=1)
            sim = jnp.einsum('bhwid,bhwjd->bhwij', bq, bk)
            i = bt[:, :, None]
            j = btk[:, None, :]
            mask = (i < j) | (i > j + WINDOW) | (j == -1)
            sim = jnp.where(mask, -jnp.finfo(sim.dtype).max, sim)
            attn = jax.nn.softmax(sim, axis=-1)
            out = jnp.einsum('bhwij,bhwjd->bhwid', attn, bv)
            return out.reshape(b, h, n, d)

        def _layer(x, wqkv, qs, ksc, wo, lg, lb, w1, b1, w2, b2):
            b, n, _ = x.shape
            h = shift_token(x)
            qkv = h @ wqkv
            q, k, v = jnp.split(qkv, 3, axis=-1)
            to_heads = lambda t: t.reshape(b, n, HEADS, DIM_HEAD).transpose(0, 2, 1, 3)
            q, k, v = (to_heads(q), to_heads(k), to_heads(v))
            q = l2norm(q) * qs
            k = l2norm(k) * ksc
            q, k = rotary_xpos(q, k)
            o = local_attention(q, k, v)
            o = o.transpose(0, 2, 1, 3).reshape(b, n, INNER)
            x = x + o @ wo
            h = shift_token(x)
            mu = h.mean(-1, keepdims=True)
            var = h.var(-1, keepdims=True)
            h = (h - mu) / jnp.sqrt(var + 1e-05) * lg + lb
            h = h @ w1 + b1
            a, g = jnp.split(h, 2, axis=-1)
            h = a * jax.nn.gelu(g, approximate=False)
            x = x + h @ w2 + b2
            return x
        for l in range(DEPTH):
            x = _layer(x, wqkv[l], q_scale[l], k_scale[l], wo[l], ln_g[l], ln_b[l], w1[l], b1[l], w2[l], b2[l])
        return x
    x = L0_attn_x
    mod = (_silu(L0_c) @ L0_wmod).reshape(L0_c.shape[0], 6, 1, -1)
    sa, ca, ga, sb, cb, gb = (mod[:, 0], mod[:, 1], mod[:, 2], mod[:, 3], mod[:, 4], mod[:, 5])
    ga = (2 * (ga >= 0) - 1) * jnp.maximum(jnp.abs(ga), 0.25)
    gb = (2 * (gb >= 0) - 1) * jnp.maximum(jnp.abs(gb), 0.25)
    h = _layernorm(x, axis=-1) * (1 + ca) + sa
    x = x + ga * _L0_attn_ref(h, L0_attn_Wq, L0_attn_bq, L0_attn_Wk, L0_attn_bk, L0_attn_Wv, L0_attn_bv, L0_attn_Wo, L0_attn_bo, L0_attn_W_cross, L0_attn_shift_weights, L0_attn_gate)
    h = _layernorm(x, axis=-1) * (1 + cb) + sb
    x = x + gb * _L0_ffn_ref(h, L0_ffn_w1_w, L0_ffn_w1_s, L0_ffn_w2_w, L0_ffn_w2_s, L0_ffn_h1_w, L0_ffn_h1_s, L0_ffn_h2_w, L0_ffn_h2_s, L0_ffn_w3_w, L0_ffn_w3_s)
    mod = (_silu(L1_c) @ L1_wmod).reshape(L1_c.shape[0], 6, 1, -1)
    sa, ca, ga, sb, cb, gb = (mod[:, 0], mod[:, 1], mod[:, 2], mod[:, 3], mod[:, 4], mod[:, 5])
    ga = (2 * (ga >= 0) - 1) * jnp.maximum(jnp.abs(ga), 0.25)
    gb = (2 * (gb >= 0) - 1) * jnp.maximum(jnp.abs(gb), 0.25)
    h = _layernorm(x, axis=-1) * (1 + ca) + sa
    x = x + ga * _L1_attn_ref(h, L1_attn_w_in, L1_attn_b_in, L1_attn_sf_w, L1_attn_sf_b, L1_attn_f_w1, L1_attn_f_b1, L1_attn_freq1, L1_attn_f_w2, L1_attn_f_b2, L1_attn_freq2, L1_attn_f_w3, L1_attn_f_b3, L1_attn_freq3, L1_attn_f_wout, L1_attn_filt_bias, L1_attn_w_out, L1_attn_b_out)
    h = _layernorm(x, axis=-1) * (1 + cb) + sb
    x = x + gb * _L1_ffn_ref(h, L1_ffn_wqkv, L1_ffn_q_scale, L1_ffn_k_scale, L1_ffn_wo, L1_ffn_ln_g, L1_ffn_ln_b, L1_ffn_w1, L1_ffn_b1, L1_ffn_w2, L1_ffn_b2)
    return x

_drawn_inputs = setup_inputs


def setup_inputs(seed=0):
    import zlib

    import numpy as np

    out = dict(_drawn_inputs(seed))
    spreads = {'L0_attn_bq': (0.0, 0.1),
     'L0_attn_bk': (0.0, 0.1),
     'L0_attn_bv': (0.0, 0.1),
     'L0_attn_bo': (0.0, 0.1),
     'L0_attn_gate': (0.0, 0.1),
     'L1_attn_b_in': (0.0, 0.1),
     'L1_attn_sf_b': (0.0, 0.1),
     'L1_attn_f_b1': (0.0, 0.1),
     'L1_attn_freq1': (1.0, 0.2),
     'L1_attn_f_b2': (0.0, 0.1),
     'L1_attn_freq2': (1.0, 0.2),
     'L1_attn_f_b3': (0.0, 0.1),
     'L1_attn_freq3': (1.0, 0.2),
     'L1_attn_b_out': (0.0, 0.1),
     'L1_ffn_q_scale': (1.0, 0.2),
     'L1_ffn_k_scale': (1.0, 0.2),
     'L1_ffn_ln_g': (1.0, 0.2),
     'L1_ffn_ln_b': (0.0, 0.1),
     'L1_ffn_b1': (0.0, 0.1),
     'L1_ffn_b2': (0.0, 0.1)}
    factors = {}
    for name, (base, spread) in spreads.items():
        noise = np.random.default_rng([zlib.crc32(name.encode()), seed]).standard_normal(out[name].shape)
        drawn = base * np.exp(spread * noise) if base else spread * noise
        out[name] = jnp.asarray(drawn.astype(out[name].dtype))
    for name, factor in factors.items():
        out[name] = (out[name] * factor).astype(out[name].dtype)
    return out
```

```python
from contextlib import ExitStack

import numpy as np

import concourse.bass as bass
from concourse import mybir
from concourse.alu_op_type import AluOpType as ALU

F32 = mybir.dt.float32
BF16 = mybir.dt.bfloat16
ACT = mybir.ActivationFunctionType
AX_X = mybir.AxisListType.X

P = 128
D = 256
DC = D // P
NB = 2
S = 2048
T = 512
TPB = S // T
EPS = 1e-5
BIG = 1e30

BELOW, ABOVE = 0, 1

SA, CA, GA, SB_, CB, GB = range(6)


def tok(b, i):
    return bass.ds(i * T + b * S, T)


class Core:

    def __init__(self, nc, stack, io):
        self.nc, self.io, self.stack = nc, io, stack
        self.XP = stack.enter_context(nc.sbuf_tensor("X", [P, DC * NB * (1 + S)], F32))
        self.X = self.XP[:, 0:DC * NB * S].rearrange("p (c t) -> p c t", c=DC)
        self.ones = stack.enter_context(nc.sbuf_tensor("ones", [P, P], F32))
        self.ident = stack.enter_context(nc.sbuf_tensor("ident", [P, P], F32))
        self.identb = stack.enter_context(nc.sbuf_tensor("identb", [P, P], BF16))
        self.lower = stack.enter_context(nc.sbuf_tensor("lower", [P, P], BF16))
        self.mask = stack.enter_context(nc.sbuf_tensor("mask", [P, 2, P], BF16))
        self.eps = stack.enter_context(nc.sbuf_tensor("eps", [P, 1], F32))
        self.mod = stack.enter_context(nc.sbuf_tensor("mod", [P, 2, 6, DC, NB], F32))
        self.PS = stack.enter_context(nc.psum_tensor("PS", [P, 8, 512], F32))
        self.tick = self.sem("tick")
        self.qk_parts = nc.dram_tensor("qk_parts", [2, NB, 3, D, S], BF16, kind="Internal").ap()
        self.o_dram = nc.dram_tensor("o_dram", [NB, NH0, HD0, S], F32, kind="Internal").ap()
        self.sum_dram = nc.dram_tensor("sum_dram", [NB, NH0, S], F32, kind="Internal").ap()
        self.kpad = nc.dram_tensor("kpad", [D, KW], F32, kind="Internal").ap()
        self.x_dram = nc.dram_tensor("x_dram", [D, NB * S], F32, kind="Internal").ap()
        self.y_dram = nc.dram_tensor("y_dram", [D * NB * NI, OW], F32, kind="Internal").ap()
        self.recip_dram = nc.dram_tensor("recip_dram", [NB, NH0, S], F32, kind="Internal").ap()

    def sem(self, name):
        return self.nc.alloc_semaphore(name=name)


def setup(core):
    nc, io, mod = core.nc, core.io, core.mod
    loaded, x_in = core.sem("su_loaded"), core.sem("su_x_in")
    filled, picked = core.sem("su_filled"), core.sem("su_picked")
    c_act, mod_ps, mod_sb, gate_parts = (core.sem("su_" + n) for n in ("c_act", "mod_ps", "mod_sb", "gate_parts"))
    done = core.sem("su_done")
    with ExitStack() as st:
        sb = lambda n, s, d=F32: st.enter_context(nc.sbuf_tensor(n, s, d))
        cT = sb("cT", [P, DC, 2, NB])
        cs = sb("cs", [P, DC, 2, NB])
        wm = sb("wm", [P, 2, DC, 6 * D])
        sgn = sb("sgn", [P, 2, 2, DC, NB])
        mag = sb("mag", [P, 2, 2, DC, NB])
        ps = core.PS[:, 0]
        with nc.Block() as block:

            @block.sync
            def _(sp):
                sp.dma_start(cT[:], io["cT"].rearrange("(k p) l b -> p k l b", p=P)).then_inc(loaded, 16)
                for layer in range(2):
                    sp.dma_start(wm[:, layer], io["wmod"][layer].rearrange("(k p) n -> p k n", p=P)).then_inc(loaded, 16)
                sp.dma_start(core.X[:], io["xT"].rearrange("(k p) t -> p k t", p=P)).then_inc(x_in, 16)
                sp.wait_ge(x_in, 16)

            @block.gpsimd
            def _(pool):
                nc.gpsimd.memset(core.eps[:], EPS)
                nc.gpsimd.memset(core.ones[:], 1.0 / D)
                nc.gpsimd.memset(core.ident[:], 0.0)
                nc.gpsimd.memset(core.identb[:], 0.0)
                nc.gpsimd.memset(core.lower[:], 0.0)
                nc.gpsimd.memset(core.mask[:], 0.0).then_inc(filled, 1)
                pool.wait_ge(filled, 1)
                eye = [[-1, P]]
                nc.gpsimd.affine_select(out=core.ident[:], in_=core.ident[:], compare_op=ALU.not_equal, fill=1.0,
                                        base=0, pattern=eye, channel_multiplier=1)
                nc.gpsimd.affine_select(out=core.identb[:], in_=core.identb[:], compare_op=ALU.not_equal, fill=1.0,
                                        base=0, pattern=eye, channel_multiplier=1)
                nc.gpsimd.affine_select(out=core.lower[:], in_=core.lower[:], compare_op=ALU.not_equal, fill=-BIG,
                                        base=0, pattern=eye, channel_multiplier=1)
                nc.gpsimd.affine_select(out=core.mask[:, BELOW], in_=core.mask[:, BELOW], compare_op=ALU.is_ge, fill=1.0,
                                        base=0, pattern=[[1, P]], channel_multiplier=-1)
                nc.gpsimd.affine_select(out=core.mask[:, ABOVE], in_=core.mask[:, ABOVE], compare_op=ALU.is_ge, fill=1.0,
                                        base=0, pattern=[[-1, P]], channel_multiplier=1).then_inc(picked, 1)
                pool.wait_ge(picked, 1)

            @block.scalar
            def _(act):
                act.wait_ge(loaded, 16 * 3)
                nc.scalar.activation(cs[:], cT[:], ACT.Silu).then_inc(c_act, 1)

            @block.tensor
            def _(pe):
                pe.wait_ge(c_act, 1)
                for layer in range(2):
                    for o in range(6 * DC):
                        col = (layer * 6 * DC + o) * NB
                        for k in range(DC):
                            mm = nc.tensor.matmul(ps[:, col:col + NB], wm[:, layer, k, o * P:(o + 1) * P],
                                                  cs[:, k, layer, :], start=(k == 0), stop=(k == DC - 1))
                mm.then_inc(mod_ps, 1)

            @block.vector
            def _(dve):
                dve.wait_ge(mod_ps, 1)
                nc.vector.tensor_copy(mod[:].rearrange("p l w k b -> p (l w k b)"),
                                      ps[:, 0:2 * 6 * DC * NB]).then_inc(mod_sb, 1)
                dve.wait_ge(mod_sb, 1)
                for j, w in enumerate((GA, GB)):
                    nc.vector.tensor_scalar(sgn[:, j], mod[:, :, w], 0.0, 2.0, ALU.is_ge, ALU.mult).then_inc(gate_parts, 1)
                    for layer in range(2):
                        nc.vector.scalar_tensor_tensor(mag[:, j, layer], mod[:, layer, w], -1.0, mod[:, layer, w],
                                                       ALU.mult, ALU.max).then_inc(gate_parts, 1)
                dve.wait_ge(gate_parts, 6)
                nc.vector.tensor_scalar(mag[:], mag[:], 0.25, None, ALU.max).then_inc(gate_parts, 1)
                dve.wait_ge(gate_parts, 7)
                for j, w in enumerate((GA, GB)):
                    for layer in range(2):
                        nc.vector.scalar_tensor_tensor(mod[:, layer, w], sgn[:, j, layer], -1.0, mag[:, j, layer],
                                                       ALU.add, ALU.mult).then_inc(done, 1)
                for w in (CA, CB):
                    nc.vector.tensor_scalar(mod[:, :, w], mod[:, :, w], 1.0, None, ALU.add).then_inc(done, 1)
                dve.wait_ge(done, 6)


def layernorm(core, tag, src, dst, scale, bias):
    nc, PS = core.nc, core.PS
    mean, centred, squared, var, logged, rstd, normed, done = (
        core.sem(f"{tag}_{n}") for n in ("mean", "centred", "squared", "var", "logged", "rstd", "normed", "done"))
    with ExitStack() as st:
        sb = lambda n, sh: st.enter_context(nc.sbuf_tensor(f"{tag}_{n}", sh, F32))
        xc = [sb(f"xc{b}", [P, DC, T]) for b in range(NB)]
        sq = [sb(f"sq{b}", [P, DC, T]) for b in range(NB)]
        ln = [sb(f"ln{b}", [P, T]) for b in range(NB)]
        rs = [sb(f"rs{b}", [P, T]) for b in range(NB)]
        with nc.Block() as block:

            @block.tensor
            def _(pe):
                def means(i, b):
                    for c in range(DC):
                        mm = nc.tensor.matmul(PS[:, b], core.ones[:], src(c, b, i), start=(c == 0), stop=(c == DC - 1))
                    mm.then_inc(mean, 1)

                def variances(i, b):
                    pe.wait_ge(squared, NB * i + b + 1)
                    for c in range(DC):
                        mm = nc.tensor.matmul(PS[:, 2 + b], core.ones[:], sq[b][:, c], start=(c == 0), stop=(c == DC - 1))
                    mm.then_inc(var, 1)

                for b in range(NB):
                    means(0, b)
                with pe.Fori(0, TPB - 1) as i:
                    for b in range(NB):
                        pe.wait_ge(centred, NB * i + b + 1)
                        means(i + 1, b)
                        variances(i, b)
                for b in range(NB):
                    variances(TPB - 1, b)

            @block.vector
            def _(dve):
                with dve.Fori(0, TPB) as i:
                    for b in range(NB):
                        dve.wait_ge(mean, NB * i + b + 1)
                        if b == 0:
                            dve.wait_ge(done, NB * i + 1)
                        for c in range(DC):
                            op = nc.vector.tensor_tensor(xc[b][:, c], src(c, b, i), PS[:, b], ALU.subtract)
                        op.then_inc(centred, 1)
                    for b in range(NB):
                        dve.wait_ge(rstd, NB * i + b + 1)
                        for c in range(DC):
                            op = nc.vector.tensor_tensor(xc[b][:, c], xc[b][:, c], rs[b][:], ALU.mult)
                        op.then_inc(normed, 1)
                        dve.wait_ge(normed, NB * i + b + 1)
                        for c in range(DC):
                            op = nc.vector.tensor_scalar(dst(c, b, i), xc[b][:, c], scale(c, b), bias(c, b),
                                                         ALU.mult, ALU.add)
                        op.then_inc(done, 1)

            @block.scalar
            def _(act):
                nc.scalar.preload_act_table_set("natural_log_exp_and_others")
                act.sem_inc(done, 1)
                with act.Fori(0, TPB) as i:
                    for b in range(NB):
                        act.wait_ge(centred, NB * i + b + 1)
                        nc.scalar.activation(sq[b][:], xc[b][:], ACT.Square).then_inc(squared, 1)
                    for b in range(NB):
                        act.wait_ge(var, NB * i + b + 1)
                        nc.scalar.activation(ln[b][:], PS[:, 2 + b], ACT.Ln, bias=core.eps[:]).then_inc(logged, 1)
                        act.wait_ge(logged, NB * i + b + 1)
                        nc.scalar.activation(rs[b][:], ln[b][:], ACT.Exp, scale=-0.5).then_inc(rstd, 1)



NH0 = 16
HD0 = D // NH0
HPC = P // HD0
MS0 = HD0 // 2
NBLK = S // P
TB = T // P
Q_PARTS = (0, 0, 0, 1, 2, 1)
K_PARTS = (0, 1, 2, 0, 0, 1)
STK = len(Q_PARTS) * HD0
AUG = STK + 3


def attn0_project(core, H, VV):
    nc, io, PS = core.nc, core.io, core.PS
    names = ("w_in sig mixed hs_ready q_ps k_ps qt_ps v_ps q_sb k_sb hi_q hi_k rest_q rest_k mid_q mid_k lo_q lo_k "
             "v_sb zeroed table")
    w_in, sig, mixed, hs_ready, q_ps, k_ps, qt_ps, v_ps, q_sb, k_sb, hi_q, hi_k, rest_q, rest_k, mid_q, mid_k, lo_q, \
        lo_k, v_sb, zeroed, table = (core.sem("a0p_" + n) for n in names.split())
    parts_out = [core.sem(f"a0p_parts_out{b}") for b in range(NB)]
    tick = core.sem("a0p_tick")
    with ExitStack() as st:
        sb = lambda n, sh, d=F32: st.enter_context(nc.sbuf_tensor("a0p_" + n, sh, d))
        wq, wk, wv = (sb(n, [P, DC, D]) for n in ("wq", "wk", "wv"))
        bq, bk, gate, g = (sb(n, [P, DC]) for n in ("bq", "bk", "gate", "g"))
        wc, wm = sb("wc", [P, DC, P]), sb("wm", [P, DC, P])
        A = sb("A", [P, DC, P])
        Hs = [sb(f"Hs{b}", [P, DC, T]) for b in range(NB)]
        qsb = [sb(f"qsb{b}", [P, DC, T]) for b in range(NB)]
        ksb = [sb(f"ksb{b}", [P, DC, T]) for b in range(NB)]
        rest = [sb(f"rest{b}", [P, 2, DC, T]) for b in range(NB)]
        parts = [sb(f"parts{b}", [P, 2, 3, DC, T], BF16) for b in range(NB)]
        n_w = 8
        with nc.Block() as block:

            @block.sync
            def _(sp):
                for t, name in ((wq, "wqT"), (wk, "wkT"), (wv, "wvT")):
                    sp.dma_start(t[:], io[name].rearrange("(k p) o -> p k o", p=P)).then_inc(w_in, 16)
                for t, name in ((wc, "wc_bd"), (wm, "shift_bd")):
                    sp.dma_start(t[:], io[name].rearrange("k p o -> p k o")).then_inc(w_in, 16)
                for t, name in ((bq, "bq"), (bk, "bk"), (gate, "gate_rep")):
                    sp.dma_start(t[:], io[name]).then_inc(w_in, 16)
                with sp.Fori(0, TPB) as i:
                    for b in range(NB):
                        for w, ready in ((0, lo_q), (1, lo_k)):
                            sp.wait_ge(ready, NB * i + b + 1)
                            for part in range(3):
                                dst = core.qk_parts[w, b, part].rearrange("(c p) s -> p c s", p=P)[:, :, bass.ds(i * T, T)]
                                sp.dma_start(dst, parts[b][:, w, part]).then_inc(parts_out[b], 16)
                for b in range(NB):
                    sp.wait_ge(parts_out[b], 96 * (TPB + 1))

            @block.gpsimd
            def _(pool):
                nc.gpsimd.memset(VV[:], 1.0).then_inc(zeroed, 1)
                with pool.Fori(0, TPB) as i:
                    for b in range(NB):
                        pool.wait_ge(v_sb, NB * i + b + 1)
                        pool.sem_inc(tick, 1)
                        nc.gpsimd.tensor_copy(Hs[b][:], H[:, :, tok(b, i)]).then_inc(hs_ready, 1)
                        for w, r, m in ((0, rest_q, mid_q), (1, rest_k, mid_k)):
                            pool.wait_ge(r, NB * i + b + 1)
                            pool.sem_inc(tick, 1)
                            nc.gpsimd.tensor_copy(parts[b][:, w, 1], rest[b][:, w]).then_inc(m, 1)

            @block.scalar
            def _(act):
                for b in range(NB):
                    act.sem_inc(parts_out[b], 96)
                act.wait_ge(w_in, 16 * n_w)
                nc.scalar.activation(g[:], gate[:], ACT.Sigmoid).then_inc(sig, 1)
                with act.Fori(0, TPB) as i:
                    for b in range(NB):
                        act.wait_ge(q_ps, NB * i + b + 1)
                        for c in range(DC):
                            op = nc.scalar.activation(qsb[b][:, c], PS[:, c], ACT.Identity, bias=bq[:, c:c + 1])
                        op.then_inc(q_sb, 1)
                        act.wait_ge(k_ps, NB * i + b + 1)
                        for c in range(DC):
                            op = nc.scalar.activation(ksb[b][:, c], PS[:, 2 + c], ACT.Identity, bias=bk[:, c:c + 1])
                        op.then_inc(k_sb, 1)
                        act.wait_ge(parts_out[b], 96 * (i + 1))
                        act.wait_ge(k_sb, NB * i + b + 1)
                        nc.scalar.copy(parts[b][:, 1, 0], ksb[b][:]).then_inc(hi_k, 1)
                        act.wait_ge(qt_ps, NB * i + b + 1)
                        nc.scalar.copy(parts[b][:, 0, 0], PS[:, 4:6]).then_inc(hi_q, 1)

            @block.vector
            def _(dve):
                dve.sem_inc(v_sb, NB)
                dve.wait_ge(sig, 1)
                nc.vector.tensor_tensor(wc[:], wc[:], wm[:], ALU.subtract).then_inc(mixed, 1)
                dve.wait_ge(mixed, 1)
                for c in range(DC):
                    nc.vector.scalar_tensor_tensor(A[:, c], wc[:, c], g[:, c:c + 1], wm[:, c], ALU.mult, ALU.add).then_inc(mixed, 1)
                dve.wait_ge(mixed, 1 + DC)
                nc.vector.tensor_scalar(A[:], A[:], float(HD0) ** -0.5, None, ALU.mult).then_inc(mixed, 1)
                dve.wait_ge(zeroed, 1)
                with dve.Fori(0, TPB) as i:
                    for b in range(NB):
                        dve.wait_ge(hi_k, NB * i + b + 1)
                        nc.vector.tensor_tensor(rest[b][:, 1], ksb[b][:], parts[b][:, 1, 0], ALU.subtract).then_inc(rest_k, 1)
                        dve.wait_ge(v_ps, NB * i + b + 1)
                        for j in range(2):
                            dst = VV[:, b, bass.ds(i * TB + 2 * j, 2), :, 0:HD0]
                            op = nc.vector.tensor_copy(dst, PS[:, 6 + j].rearrange("p (k h f) -> p k h f", k=2, h=NH0))
                        op.then_inc(v_sb, 1)
                        dve.wait_ge(hi_q, NB * i + b + 1)
                        nc.vector.tensor_tensor(rest[b][:, 0], PS[:, 4:6], parts[b][:, 0, 0], ALU.subtract).then_inc(rest_q, 1)
                        dve.wait_ge(mid_k, NB * i + b + 1)
                        nc.vector.tensor_tensor(parts[b][:, 1, 2], rest[b][:, 1], parts[b][:, 1, 1], ALU.subtract).then_inc(lo_k, 1)
                        dve.wait_ge(mid_q, NB * i + b + 1)
                        nc.vector.tensor_tensor(parts[b][:, 0, 2], rest[b][:, 0], parts[b][:, 0, 1], ALU.subtract).then_inc(lo_q, 1)

            @block.tensor
            def _(pe):
                pe.wait_ge(w_in, 16 * n_w)
                pe.wait_ge(mixed, 2 + DC)
                with pe.Fori(0, TPB) as i:
                    for b in range(NB):
                        for c in range(DC):
                            for k in range(DC):
                                mm = nc.tensor.matmul(PS[:, c], wq[:, k, c * P:(c + 1) * P], H[:, k, tok(b, i)],
                                                      start=(k == 0), stop=(k == DC - 1))
                        mm.then_inc(q_ps, 1)
                        pe.wait_ge(k_sb, NB * i + b)
                        for c in range(DC):
                            for k in range(DC):
                                mm = nc.tensor.matmul(PS[:, 2 + c], wk[:, k, c * P:(c + 1) * P], H[:, k, tok(b, i)],
                                                      start=(k == 0), stop=(k == DC - 1))
                        mm.then_inc(k_ps, 1)
                        pe.wait_ge(hs_ready, NB * i + b + 1)
                        pe.wait_ge(v_sb, NB * i + b + NB)
                        for j in range(TB):
                            for k in range(DC):
                                mm = nc.tensor.matmul(PS[:, 6 + j // 2, (j % 2) * D:(j % 2 + 1) * D],
                                                      Hs[b][:, k, j * P:(j + 1) * P], wv[:, k],
                                                      start=(k == 0), stop=(k == DC - 1))
                        mm.then_inc(v_ps, 1)
                        pe.wait_ge(q_sb, NB * i + b + 1)
                        pe.wait_ge(rest_q, NB * i + b)
                        for c in range(DC):
                            mm = nc.tensor.matmul(PS[:, 4 + c], A[:, c], qsb[b][:, c], start=True, stop=True)
                        mm.then_inc(qt_ps, 1)


def attn0_scores(core, VV):
    nc, PS = core.nc, core.PS
    ST = NH0
    names = "ones_set vu mx_set p1_ps p1_read mx neg part m_ps m_sb m_in s_ps exp_done pv_done o_sb"
    ones_set, vu, mx_set, p1_ps, p1_read, mx_s, neg_s, part_s, m_ps, m_sb, m_in, s_ps, exp_done, pv_done, o_sb = (
        core.sem("a0s_" + n) for n in names.split())
    stack_in = [core.sem(f"a0s_stack_in{p}") for p in range(2)]
    o_out = core.sem("a0s_o_out")
    tick = core.sem("a0s_tick")
    N_IN = 16 * NB * 9
    N_P1 = NB * (sum((q // 4 + 1) for q in range(NBLK)) + 1)
    N_S2 = NB * (NBLK + NBLK // 2)
    N_PV = NB * NBLK
    N_OUT = 16 * NB * 8
    with ExitStack() as st:
        sb = lambda n, sh, d=F32: st.enter_context(nc.sbuf_tensor("a0s_" + n, sh, d))
        QS = [[sb(f"QS{p}{b}", [AUG, S], BF16) for b in range(NB)] for p in range(2)]
        KS = [[sb(f"KS{p}{b}", [AUG, S], BF16) for b in range(NB)] for p in range(2)]
        VU = [[sb(f"VU{p}{b}", [P, NBLK, HD0 + 1]) for b in range(NB)] for p in range(2)]
        PT = [[sb(f"PT{b}{k}", [P, S]) for k in range(2)] for b in range(NB)]
        mx = [sb(f"mx{b}", [P, NBLK, 4]) for b in range(NB)]
        rowmax = [sb(f"rowmax{b}", [P, NBLK]) for b in range(NB)]
        rest = [sb(f"rest{b}", [P, NBLK]) for b in range(NB)]
        mparts = [sb(f"mparts{b}", [P, P // NBLK, NBLK], BF16) for b in range(NB)]
        mrow = [sb(f"mrow{b}", [3 * NBLK, P], BF16) for b in range(NB)]
        O = [sb(f"O{b}", [P, T]) for b in range(NB)]

        def stages(eng, stage):
            with eng.Fori(0, ST // 2 - 1) as it:
                for par in range(2):
                    stage(2 * it + par, par, it, True)
            for par in range(2):
                stage(ST - 2 + par, par, ST // 2 - 1, par == 0)

        def pass1_blocks():
            for b in range(NB):
                for q in range(NBLK):
                    for j in range(q // 4 + 1):
                        yield b, q, j
                    if b == 1 and q == 3:
                        yield 0, None, None
            yield 1, None, None

        P1 = list(pass1_blocks())
        assert len(P1) == N_P1

        def p2_groups(kt):
            return [g for g in range(2) if 1024 * (g + 1) > kt * P]

        def group(b, qc):
            return qc if b == 0 else 3 - qc

        G2 = {}
        for kt in range(NBLK):
            for b in range(NB):
                for g in p2_groups(kt):
                    G2[kt, b, g] = len(G2)
        assert len(G2) == N_S2

        with nc.Block() as block:

            @block.sync
            def _(sp):
                def load(n, par, h):
                    for b in range(NB):
                        rows = bass.ds(h * HD0, HD0)
                        q, k = core.qk_parts[0, b], core.qk_parts[1, b]
                        qs, ks = QS[par][b], KS[par][b]
                        for j in range(3):
                            sp.dma_start(qs[j * HD0:(j + 1) * HD0, :], q[0, rows, :]).then_inc(stack_in[par], 16)
                        for j, part in ((3, 1), (4, 2), (5, 1)):
                            sp.dma_start(qs[j * HD0:(j + 1) * HD0, :], q[part, rows, :]).then_inc(stack_in[par], 16)
                        sp.dma_start(ks[0:3 * HD0, :], k[:, rows, :]).then_inc(stack_in[par], 16)
                        sp.dma_start(ks[3 * HD0:4 * HD0, :], k[0, rows, :]).then_inc(stack_in[par], 16)
                        sp.dma_start(ks[4 * HD0:6 * HD0, :], k[0:2, rows, :]).then_inc(stack_in[par], 16)

                def maxima(n, par):
                    for b in range(NB):
                        sp.wait_ge(m_sb, NB * n + b + 1)
                        for j in range(3):
                            dst = QS[par][b][STK + j:STK + j + 1, :].rearrange("o (q c) -> o q c", c=P)
                            src = mrow[b][j * NBLK:(j + 1) * NBLK, :]
                            sp.dma_start(dst, src).then_inc(m_in, 16)

                load(0, 0, 0)
                maxima(0, 0)

                def stage(n, par, it, more):
                    if more:
                        sp.wait_ge(pv_done, N_PV * n + 4)
                        load(n + 1, 1 - par, n + 1)
                        maxima(n + 1, 1 - par)
                    for b in range(NB):
                        sp.wait_ge(o_sb, NB * n + b + 1)
                        for qc in range(4):
                            r = 32 * group(b, qc)
                            sp.dma_start(core.o_dram[b, bass.ds(n, 1), :, qc * T:(qc + 1) * T].rearrange("o f t -> (o f) t"),
                                         O[b][r:r + HD0, :]).then_inc(o_out, 16)
                            sp.dma_start(core.sum_dram[b, bass.ds(n, 1), qc * T:(qc + 1) * T],
                                         O[b][r + HD0:r + HD0 + 1, :]).then_inc(o_out, 16)

                stages(sp, stage)
                sp.wait_ge(o_out, N_OUT * ST)

            @block.gpsimd
            def _(pool):
                for b in range(NB):
                    nc.gpsimd.tensor_copy(VU[0][b][:], VV[:, b, :, 0, :]).then_inc(vu, 1)

                def stage(n, par, it, more):
                    if more:
                        pool.wait_ge(pv_done, N_PV * n + 4)
                        pool.sem_inc(tick, 1)
                        for b in range(NB):
                            nc.gpsimd.tensor_copy(VU[1 - par][b][:], VV[:, b, :, bass.ds(n + 1, 1), :].rearrange("p k o f -> p k (o f)")).then_inc(vu, 1)

                stages(pool, stage)

            @block.vector
            def _(dve):
                for b in range(NB):
                    nc.vector.memset(mx[b][:], -3e38).then_inc(mx_set, 1)
                    nc.vector.memset(mparts[b][:], 0.0).then_inc(ones_set, 1)
                    for p in range(2):
                        nc.vector.memset(KS[p][b][96:AUG, :], 1.0).then_inc(ones_set, 1)
                dve.wait_ge(mx_set, NB)
                dve.wait_ge(ones_set, 3 * NB)
                dve.sem_inc(p1_read, 2)

                def row_maxima(b, n):
                    nc.vector.tensor_reduce(rowmax[b][:], mx[b][:], AX_X, ALU.max).then_inc(mx_s, 1)
                    dve.wait_ge(mx_s, NB * n + b + 1)
                    nc.vector.tensor_scalar(mparts[b][:, 0], rowmax[b][:], -1.0, None, ALU.mult).then_inc(part_s, 1)
                    dve.wait_ge(part_s, 3 * (NB * n + b) + 1)
                    nc.vector.scalar_tensor_tensor(rest[b][:], rowmax[b][:], -1.0, mparts[b][:, 0], ALU.mult, ALU.subtract).then_inc(neg_s, 1)
                    dve.wait_ge(neg_s, NB * n + b + 1)
                    nc.vector.tensor_copy(mparts[b][:, 1], rest[b][:]).then_inc(part_s, 1)
                    dve.wait_ge(part_s, 3 * (NB * n + b) + 2)
                    nc.vector.tensor_tensor(mparts[b][:, 2], rest[b][:], mparts[b][:, 1], ALU.subtract).then_inc(part_s, 1)

                def pass1(n):
                    for x, (b, q, j) in enumerate(P1):
                        dve.wait_ge(p1_ps, N_P1 * n + x + 1)
                        ps = PS[:, 6 + x % 2]
                        if q is None:
                            nc.vector.tensor_copy(mrow[b][:], ps.bitcast(BF16)[0:3 * NBLK, 0:P]).then_inc(m_sb, 1)
                            dve.wait_ge(m_sb, NB * n + b + 1)
                            dve.sem_inc(p1_read, 1)
                            continue
                        w = min(T, (q + 1) * P - j * T)
                        nc.vector.tensor_reduce(mx[b][:, q, j:j + 1], ps[:, 0:w], AX_X, ALU.max).then_inc(p1_read, 1)
                        if q == NBLK - 1 and j == 3:
                            dve.wait_ge(p1_read, N_P1 * n + x + 1 + 2)
                            row_maxima(b, n)

                pass1(0)

                def stage(n, par, it, more):
                    if more:
                        pass1(n + 1)
                    for b in range(NB):
                        dve.wait_ge(pv_done, N_PV * (n + 1) - NB + b + 1 + 4)
                        if b == 0:
                            dve.wait_ge(o_out, N_OUT * n)
                        nc.vector.tensor_copy(O[b][:], PS[:, b]).then_inc(o_sb, 1)

                stages(dve, stage)

            @block.scalar
            def _(act):
                nc.scalar.preload_act_table_set("exp_and_others")
                act.sem_inc(exp_done, 2)

                def stage(n, par, it, more):
                    for kt in range(NBLK):
                        for b in range(NB):
                            act.wait_ge(pv_done, N_PV * n + 2 * kt + b + 1)
                            for g in p2_groups(kt):
                                x = G2[kt, b, g]
                                act.wait_ge(s_ps, N_S2 * n + x + 1)
                                lo = max(kt * P - 1024 * g, 0)
                                src = PS[:, 2 + 2 * (x % 2):4 + 2 * (x % 2)].rearrange("p a t -> p (a t)")
                                nc.scalar.activation(PT[b][kt % 2][:, 1024 * g + lo:1024 * (g + 1)], src[:, lo:1024],
                                                     ACT.Exp).then_inc(exp_done, 1)

                stages(act, stage)

            @block.tensor
            def _(pe):
                pe.sem_inc(pv_done, 4)

                def pass1(n, par, x):
                    b, q, j = P1[x]
                    pe.wait_ge(p1_read, N_P1 * n + x + 1)
                    ps = PS[:, 6 + x % 2]
                    if q is None:
                        pe.wait_ge(part_s, 3 * (NB * n + b + 1))
                        nc.tensor.transpose(ps.bitcast(BF16)[:, 0:P], mparts[b][:].rearrange("p a q -> p (a q)"),
                                            core.identb[:]).then_inc(p1_ps, 1)
                        return
                    w = min(T, (q + 1) * P - j * T)
                    diag = j == q // 4
                    if diag:
                        nc.tensor.matmul(ps[:, w - P:w], core.lower[:], core.mask[:, ABOVE], start=True, stop=True)
                    nc.tensor.matmul(ps[:, 0:w], QS[par][b][0:STK, q * P:(q + 1) * P], KS[par][b][0:STK, j * T:j * T + w],
                                     start=not diag, stop=True, skip_group_check=diag).then_inc(p1_ps, 1)

                def pass2(n, par, kt):
                    for b in range(NB):
                        for g in p2_groups(kt):
                            x = G2[kt, b, g]
                            pe.wait_ge(exp_done, N_S2 * n + x + 1)
                            for qc in (2 * g, 2 * g + 1):
                                lo = max(kt * P, qc * T)
                                if lo >= (qc + 1) * T:
                                    continue
                                ps = PS[:, 2 + 2 * (x % 2) + qc % 2]
                                diag = kt // 4 == qc
                                if diag:
                                    nc.tensor.matmul(ps[:, lo - qc * T:lo - qc * T + P], core.lower[:], core.mask[:, BELOW],
                                                     start=True, stop=True)
                                mm = nc.tensor.matmul(ps[:, lo - qc * T:T], KS[par][b][:, kt * P:(kt + 1) * P],
                                                      QS[par][b][:, lo:(qc + 1) * T], start=not diag, stop=True,
                                                      skip_group_check=diag)
                            mm.then_inc(s_ps, 1)

                def pv(n, par, kt):
                    for b in range(NB):
                        pe.wait_ge(exp_done, N_S2 * n + G2[kt, b, 1] + 1 + 2)
                        if kt == 0:
                            pe.wait_ge(o_sb, NB * n)
                        for qc in range(kt // 4, 4):
                            lo = max(kt * P, qc * T)
                            r = 32 * group(b, qc)
                            mm = nc.tensor.matmul(PS[r:r + HD0 + 1, b, lo - qc * T:T], VU[par][b][:, kt],
                                                  PT[b][kt % 2][:, lo:(qc + 1) * T], start=(kt == 0), stop=(kt >= 4 * qc),
                                                  skip_group_check=(kt > 4 * qc))
                        mm.then_inc(pv_done, 1)

                pe.wait_ge(stack_in[0], N_IN)
                pe.wait_ge(ones_set, 3 * NB)
                for x in range(N_P1):
                    pass1(0, 0, x)

                def stage(n, par, it, more):
                    pe.wait_ge(m_in, 16 * 3 * NB * (n + 1))
                    pe.wait_ge(vu, NB * (n + 1))
                    pass2(n, par, 0)
                    done = 0
                    for kt in range(NBLK):
                        if kt + 1 < NBLK:
                            pass2(n, par, kt + 1)
                        if more:
                            if kt == 1:
                                pe.wait_ge(stack_in[1 - par], N_IN * (it + 1 + par))
                            upto = min(N_P1, max(0, kt) * 7) if kt < 12 else N_P1
                            for x in range(done, upto):
                                pass1(n + 1, 1 - par, x)
                            done = upto
                        pv(n, par, kt)

                stages(pe, stage)


def attn0_out(core):
    nc, io, PS, X = core.nc, core.io, core.PS, core.X
    w_in, sums_in, recip, recip_out, gbo_s, o_ready, o_ps, o_sb, x_done = (
        core.sem("a0o_" + n) for n in "w_in sums_in recip recip_out gbo normed o_ps o_sb x_done".split())
    tile_in = [core.sem(f"a0o_tile_in{b}") for b in range(NB)]
    with ExitStack() as st:
        sb = lambda n, sh, d=F32: st.enter_context(nc.sbuf_tensor("a0o_" + n, sh, d))
        wo, bv, bo, gbo = sb("wo", [P, DC, D]), sb("bv", [P, DC]), sb("bo", [P, DC]), sb("gbo", [P, DC, NB])
        sums = sb("sums", [P, NB * NH0 * S // P])
        o = [sb(f"o{b}", [P, DC, T]) for b in range(NB)]
        r = [sb(f"r{b}", [P, DC, T]) for b in range(NB)]
        y = [sb(f"y{b}", [P, DC, T]) for b in range(NB)]
        with nc.Block() as block:

            @block.sync
            def _(sp):
                sp.dma_start(sums[:], core.sum_dram.rearrange("b h (a t) -> (b h a) t", a=4)).then_inc(sums_in, 16)
                sp.dma_start(wo[:], io["woT"].rearrange("(k p) o -> p k o", p=P)).then_inc(w_in, 16)
                sp.dma_start(bv[:], io["bv"]).then_inc(w_in, 16)
                sp.dma_start(bo[:], io["bo"]).then_inc(w_in, 16)
                sp.wait_ge(recip, 1)
                sp.dma_start(core.recip_dram.rearrange("b h (a t) -> (b h a) t", a=4), sums[:]).then_inc(recip_out, 16)
                sp.wait_ge(recip_out, 16)
                with sp.Fori(0, TPB) as i:
                    for b in range(NB):
                        sp.wait_ge(o_ps, NB * i + b + 1)
                        for c in range(DC):
                            sp.dma_start(o[b][:, c], core.o_dram[b, c * HPC:(c + 1) * HPC].rearrange("h f s -> (h f) s")[:, bass.ds(i * T, T)]
                                         ).then_inc(tile_in[b], 16)
                            src = core.recip_dram[b, c * HPC:(c + 1) * HPC, bass.ds(i * T, T)].unsqueeze(1).broadcast_to([HPC, HD0, T])
                            sp.dma_start(r[b][:, c], src).then_inc(tile_in[b], 16)

            @block.vector
            def _(dve):
                dve.wait_ge(sums_in, 16)
                nc.vector.reciprocal(sums[:], sums[:]).then_inc(recip, 1)
                dve.wait_ge(w_in, 48)
                for b in range(NB):
                    nc.vector.tensor_tensor(gbo[:, :, b], core.mod[:, 0, GA, :, b], bo[:], ALU.mult).then_inc(gbo_s, 1)
                with dve.Fori(0, TPB) as i:
                    for b in range(NB):
                        dve.wait_ge(tile_in[b], 64 * (i + 1))
                        nc.vector.tensor_tensor(o[b][:], o[b][:], r[b][:], ALU.mult).then_inc(o_ready, 1)
                        dve.wait_ge(o_ready, 2 * (NB * i + b) + 1)
                        for c in range(DC):
                            op = nc.vector.tensor_scalar(o[b][:, c], o[b][:, c], bv[:, c:c + 1], None, ALU.add)
                        op.then_inc(o_ready, 1)
                    for b in range(NB):
                        dve.wait_ge(o_sb, NB * i + b + 1)
                        nc.vector.tensor_tensor(X[:, :, tok(b, i)], X[:, :, tok(b, i)], y[b][:], ALU.add).then_inc(x_done, 1)

            @block.tensor
            def _(pe):
                pe.sem_inc(o_ps, NB)
                pe.wait_ge(w_in, 48)
                with pe.Fori(0, TPB) as i:
                    for b in range(NB):
                        pe.wait_ge(o_ready, 2 * (NB * i + b + 1))
                        pe.wait_ge(o_sb, NB * i)
                        for c in range(DC):
                            for k in range(DC):
                                mm = nc.tensor.matmul(PS[:, 2 * b + c], wo[:, k, c * P:(c + 1) * P], o[b][:, k],
                                                      start=(k == 0), stop=(k == DC - 1))
                        mm.then_inc(o_ps, 1)

            @block.scalar
            def _(act):
                act.wait_ge(gbo_s, NB)
                with act.Fori(0, TPB) as i:
                    for b in range(NB):
                        act.wait_ge(o_ps, NB * i + b + 1 + NB)
                        act.wait_ge(x_done, NB * i)
                        for c in range(DC):
                            op = nc.scalar.activation(y[b][:, c], PS[:, 2 * b + c], ACT.Identity,
                                                      bias=gbo[:, c, b:b + 1], scale=core.mod[:, 0, GA, c, b:b + 1])
                        op.then_inc(o_sb, 1)



FH = 1024
FC = FH // P


def ffn0(core, H):
    nc, io, PS, X = core.nc, core.io, core.PS, core.X
    in_w12, in_s, scales, pair_ps, tanh_s, half_s, gate_s, h1_ps, h1_s, h2_ps, h2_s, w3_ps, x_done = (
        core.sem("f0_" + n) for n in
        "in_w12 in_s scales pair_ps tanh half gate h1_ps h1 h2_ps h2 w3_ps x_done".split())
    in_h1, in_h2, in_w3 = (core.sem("f0_in_" + n) for n in ("h1", "h2", "w3"))
    with ExitStack() as st:
        sb = lambda n, sh, d=F32: st.enter_context(nc.sbuf_tensor("f0_" + n, sh, d))
        w1, w2 = sb("w1", [P, DC, FH]), sb("w2", [P, DC, FH])
        h1, h2 = sb("h1", [P, FC, FH]), sb("h2", [P, FC, FH])
        w3 = sb("w3", [P, FC, D])
        s1, s2, sh1, sh2 = (sb(n, [P, FC]) for n in ("s1", "s2", "sh1", "sh2"))
        s3 = sb("s3", [P, DC])
        s1h, s12 = sb("s1h", [P, FC]), sb("s12", [P, FC])
        g3 = sb("g3", [P, DC, NB])
        hA, hB = sb("hA", [P, FC, T]), sb("hB", [P, FC, T])
        th = [sb(f"th{k}", [P, T]) for k in range(2)]
        hf = [sb(f"hf{k}", [P, T]) for k in range(2)]
        with nc.Block() as block:

            @block.sync
            def _(sp):
                for t, name in ((w1, "w1T"), (w2, "w2T")):
                    sp.dma_start(t[:], io[name].rearrange("(k p) o -> p k o", p=P)).then_inc(in_w12, 16)
                for t, name in ((s1, "w1s"), (s2, "w2s"), (sh1, "h1s"), (sh2, "h2s"), (s3, "w3s")):
                    sp.dma_start(t[:], io[name]).then_inc(in_s, 16)
                for t, name, ready in ((h1, "h1T", in_h1), (h2, "h2T", in_h2), (w3, "w3T", in_w3)):
                    sp.dma_start(t[:], io[name].rearrange("(k p) o -> p k o", p=P)).then_inc(ready, 16)

            @block.tensor
            def _(pe):
                def dense(bank, w, x, o, n_k, done):
                    for k in range(n_k):
                        mm = nc.tensor.matmul(PS[:, bank], w[:, k, o * P:(o + 1) * P], x[:, k], start=(k == 0), stop=(k == n_k - 1))
                    mm.then_inc(done, 1)

                pe.wait_ge(in_w12, 32)
                with pe.Fori(0, TPB) as i:
                    for b in range(NB):
                        u = NB * i + b
                        h = H[:, :, tok(b, i)]
                        for o in range(FC):
                            if o >= 2:
                                pe.wait_ge(gate_s, FC * u + o - 1)
                            dense(2 * (o % 2), w1, h, o, DC, pair_ps)
                            dense(2 * (o % 2) + 1, w2, h, o, DC, pair_ps)
                        pe.wait_ge(gate_s, FC * (u + 1))
                        pe.wait_ge(in_h1, 16)
                        pe.wait_ge(x_done, u)
                        for o in range(FC):
                            if o >= 2:
                                pe.wait_ge(h1_s, FC * u + o - 1)
                            dense(4 + o % 2, h1, hA, o, FC, h1_ps)
                        pe.wait_ge(h1_s, FC * (u + 1))
                        pe.wait_ge(in_h2, 16)
                        for o in range(FC):
                            if o >= 2:
                                pe.wait_ge(h2_s, FC * u + o - 1)
                            dense(6 + o % 2, h2, hB, o, FC, h2_ps)
                        pe.wait_ge(h2_s, FC * (u + 1))
                        pe.wait_ge(in_w3, 16)
                        for o in range(DC):
                            dense(4 + o, w3, hA, o, FC, w3_ps)

            @block.scalar
            def _(act):
                nc.scalar.preload_act_table_set("gelu_and_others")
                act.wait_ge(scales, 1)
                with act.Fori(0, TPB) as i:
                    for b in range(NB):
                        u = NB * i + b
                        for o in range(FC):
                            act.wait_ge(pair_ps, 2 * (FC * u + o) + 1)
                            nc.scalar.activation(th[o % 2][:], PS[:, 2 * (o % 2)], ACT.Tanh, scale=s1h[:, o:o + 1]).then_inc(tanh_s, 1)
                        for o in range(FC):
                            act.wait_ge(h1_ps, FC * u + o + 1)
                            nc.scalar.activation(hB[:, o], PS[:, 4 + o % 2], ACT.Gelu, scale=sh1[:, o:o + 1]).then_inc(h1_s, 1)
                        for o in range(FC):
                            act.wait_ge(h2_ps, FC * u + o + 1)
                            nc.scalar.activation(hA[:, o], PS[:, 6 + o % 2], ACT.Gelu, scale=sh2[:, o:o + 1]).then_inc(h2_s, 1)

            @block.vector
            def _(dve):
                dve.wait_ge(in_s, 16 * 5)
                for b in range(NB):
                    nc.vector.tensor_tensor(g3[:, :, b], core.mod[:, 0, GB, :, b], s3[:], ALU.mult)
                nc.vector.scalar_tensor_tensor(s12[:], s1[:], 0.5, s2[:], ALU.mult, ALU.mult)
                nc.vector.tensor_scalar(s1h[:], s1[:], 0.5, None, ALU.mult).then_inc(scales, 1)
                with dve.Fori(0, TPB) as i:
                    for b in range(NB):
                        u = NB * i + b
                        for o in range(FC):
                            dve.wait_ge(tanh_s, FC * u + o + 1)
                            g1, g2 = PS[:, 2 * (o % 2)], PS[:, 2 * (o % 2) + 1]
                            nc.vector.scalar_tensor_tensor(hf[o % 2][:], th[o % 2][:], 1.0, g1, ALU.add, ALU.mult).then_inc(half_s, 1)
                            dve.wait_ge(half_s, FC * u + o + 1)
                            dve.wait_ge(pair_ps, 2 * (FC * u + o + 1))
                            nc.vector.scalar_tensor_tensor(hA[:, o], hf[o % 2][:], s12[:, o:o + 1], g2, ALU.mult, ALU.mult).then_inc(gate_s, 1)
                        dve.wait_ge(w3_ps, DC * (u + 1))
                        for c in range(DC):
                            op = nc.vector.scalar_tensor_tensor(X[:, c, tok(b, i)], PS[:, 4 + c], g3[:, c, b:b + 1],
                                                                X[:, c, tok(b, i)], ALU.mult, ALU.add)
                        op.then_inc(x_done, 1)



NT = 1024
FO = 64
UC = 3 * D // P
BS = 64
NJ = S // BS
OW = 256
NI = S // OW
BPO = OW // BS
PAIRS = 4
LAG0 = -(BPO - 1)
LAG1 = NT // BS
LAGS = range(LAG0, LAG1 + 1)
JPAD = LAG1
HW = (len(LAGS) - 1) * BS + OW
KOFF = -LAG0 * BS + BS
KW = BS + HW
TWO_PI = 2.0 * np.pi
PI2_HI = float(np.float32(6.28125))
PI2_LO = float(TWO_PI - 6.28125)
ROUND = 1.5 * 2.0 ** 23
PI_IN = float(np.nextafter(np.float32(np.pi), np.float32(0)))


def filter_taps(core):
    nc, io, PS = core.nc, core.io, core.PS
    w_in, zeroed, ps_done, arg_s, sin_s, tap_ps, taps_s, out_s = (
        core.sem("ft_" + n) for n in "w_in zeroed ps arg sin tap_ps taps out".split())
    with ExitStack() as st:
        sb = lambda n, sh, d=F32: st.enter_context(nc.sbuf_tensor("ft_" + n, sh, d))
        z = sb("z", [3, NT])
        w = [sb("w1", [3, FO]), sb("w2", [FO, FO]), sb("w3", [FO, FO])]
        bf = sb("bf", [FO, 3, 2])
        wout = sb("wout", [FO, D])
        decay = sb("decay", [P, DC, NT])
        arg, turns, h = sb("arg", [FO, NT]), sb("turns", [FO, NT]), sb("h", [FO, NT])
        taps = sb("taps", [P, DC, KW])
        NH = NT // 512
        with nc.Block() as block:

            @block.sync
            def _(sp):
                loads = [(z[:], io["f_z"]), (bf[:], io["f_bf"]), (wout[:], io["f_wout"]),
                         (decay[:], io["f_decay"].rearrange("(c p) t -> p c t", p=P))]
                loads += [(w[k][:], io[f"f_w{k + 1}"]) for k in range(3)]
                for dst, src in loads:
                    sp.dma_start(dst, src).then_inc(w_in, 16)
                sp.wait_ge(taps_s, DC * NH)
                sp.wait_ge(zeroed, 1)
                sp.dma_start(core.kpad.rearrange("(c p) w -> p c w", p=P), taps[:]).then_inc(out_s, 16)
                sp.wait_ge(out_s, 16)

            @block.gpsimd
            def _(pool):
                nc.gpsimd.memset(taps[:], 0.0).then_inc(zeroed, 1)

            @block.tensor
            def _(pe):
                pe.wait_ge(w_in, 16 * 7)
                for layer in range(3):
                    x = z if layer == 0 else h
                    if layer:
                        pe.wait_ge(sin_s, layer)
                    for n in range(NH):
                        mm = nc.tensor.matmul(PS[0:FO, n], w[layer][:], x[:, n * 512:(n + 1) * 512], start=True, stop=True)
                    mm.then_inc(ps_done, 1)
                pe.wait_ge(sin_s, 3)
                for c in range(DC):
                    for n in range(NH):
                        mm = nc.tensor.matmul(PS[:, 2 + NH * c + n], wout[:, c * P:(c + 1) * P], h[:, n * 512:(n + 1) * 512],
                                              start=True, stop=True)
                mm.then_inc(tap_ps, 1)

            @block.vector
            def _(dve):
                dve.wait_ge(w_in, 16 * 7)
                n = 0

                def then(op):
                    nonlocal n
                    n += 1
                    op.then_inc(arg_s, 1)
                    dve.wait_ge(arg_s, n)

                for layer in range(3):
                    dve.wait_ge(ps_done, layer + 1)
                    ps = PS[0:FO, 0:NH].rearrange("p a t -> p (a t)")
                    then(nc.vector.tensor_scalar(arg[:], ps, bf[:, layer, 0:1], bf[:, layer, 1:2], ALU.add, ALU.mult))
                    then(nc.vector.tensor_scalar(turns[:], arg[:], 1.0 / TWO_PI, ROUND, ALU.mult, ALU.add))
                    then(nc.vector.tensor_scalar(turns[:], turns[:], ROUND, None, ALU.subtract))
                    then(nc.vector.scalar_tensor_tensor(arg[:], turns[:], -PI2_HI, arg[:], ALU.mult, ALU.add))
                    then(nc.vector.scalar_tensor_tensor(arg[:], turns[:], -PI2_LO, arg[:], ALU.mult, ALU.add))
                    then(nc.vector.tensor_scalar(arg[:], arg[:], PI_IN, -PI_IN, ALU.min, ALU.max))
                dve.wait_ge(tap_ps, 1)
                dve.wait_ge(zeroed, 1)
                for c in range(DC):
                    for k in range(NH):
                        at = slice(KOFF + k * 512, KOFF + (k + 1) * 512)
                        nc.vector.tensor_tensor(taps[:, c, at], PS[:, 2 + NH * c + k], decay[:, c, k * 512:(k + 1) * 512],
                                                ALU.mult).then_inc(taps_s, 1)

            @block.scalar
            def _(act):
                for layer in range(3):
                    act.wait_ge(arg_s, 6 * (layer + 1))
                    nc.scalar.activation(h[:], arg[:], ACT.Sin).then_inc(sin_s, 1)


def backwards(ap, start, n):
    return bass.AP(ap.tensor, ap.offset + start + n - 1, [list(ap.ap[0]), [-1, n]])


def conv_inputs(core, H, V, X0, RR):
    nc, io, PS = core.nc, core.io, core.PS
    w_in, zeroed, pj_ps, pj_sb, tap_s, uc_s, v_s, tr_ps, rr_s, hist, v_free, turned = (
        core.sem("ci_" + n) for n in "w_in zeroed pj_ps pj_sb tap uc v tr_ps rr hist v_free turned".split())
    with ExitStack() as st:
        sb = lambda n, sh, d=F32: st.enter_context(nc.sbuf_tensor("ci_" + n, sh, d))
        wi = sb("wi", [P, DC, 3 * D])
        bi, fb, fw = sb("bi", [P, UC]), sb("fb", [P, UC]), sb("fw", [P, UC, 3])
        U = [sb(f"U{b}", [P, UC, 2 + T]) for b in range(NB)]
        C = sb("C", [P, T])
        X1 = sb("X1", [P, DC, T])
        Vt = [sb(f"Vt{b}", [P, DC, T]) for b in range(NB)]
        NTR = DC * T // BS // 4

        with nc.Block() as block:

            @block.sync
            def _(sp):
                sp.dma_start(wi[:], io["h_win"].rearrange("(k p) o -> p k o", p=P)).then_inc(w_in, 16)
                for t, name in ((bi, "h_bin"), (fb, "h_sfb"), (fw, "h_sfw")):
                    sp.dma_start(t[:], io[name]).then_inc(w_in, 16)

            @block.tensor
            def _(pe):
                def project(i, b, u):
                    for o in range(UC):
                        pe.wait_ge(pj_sb, UC * u)
                        for k in range(DC):
                            mm = nc.tensor.matmul(PS[:, o], wi[:, k, o * P:(o + 1) * P], H[:, k, tok(b, i)],
                                                  start=(k == 0), stop=(k == DC - 1))
                        mm.then_inc(pj_ps, 1)

                def turn(b, u):
                    pe.wait_ge(v_s, DC * (u + 1))
                    for n in range(NTR):
                        pe.wait_ge(rr_s, NTR * u + n + 1)
                        pe.sem_inc(core.tick, 1)
                        for j in range(4):
                            c, blk = divmod(4 * n + j, T // BS)
                            mm = nc.tensor.transpose(PS[0:BS, 6 + n % 2, j * P:(j + 1) * P],
                                                     Vt[b][:, c, T - (blk + 1) * BS:T - blk * BS], core.ident[:])
                        mm.then_inc(tr_ps, 1)
                    pe.wait_ge(tr_ps, NTR * (u + 1))
                    pe.sem_inc(turned, NTR)

                pe.sem_inc(rr_s, 2)
                pe.sem_inc(turned, NTR * NB)
                pe.wait_ge(w_in, 64)
                project(0, 0, 0)
                with pe.Fori(0, TPB - 1) as i:
                    project(i, 1, NB * i + 1)
                    turn(0, NB * i)
                    project(i + 1, 0, NB * i + 2)
                    turn(1, NB * i + 1)
                last = TPB - 1
                project(last, 1, NB * last + 1)
                turn(0, NB * last)
                turn(1, NB * last + 1)

            @block.scalar
            def _(act):
                act.wait_ge(w_in, 64)
                act.wait_ge(zeroed, 1)

                def take(i, b, u):
                    act.wait_ge(hist, u + 1)
                    for o in range(UC):
                        act.wait_ge(pj_ps, UC * u + o + 1)
                        nc.scalar.activation(U[b][:, o, 2:2 + T], PS[:, o], ACT.Identity, bias=bi[:, o:o + 1]).then_inc(pj_sb, 1)

                def spread(i, b, u):
                    for n in range(NTR):
                        act.wait_ge(tr_ps, NTR * u + n + 1)
                        c, blk = divmod(4 * n, T // BS)
                        for half in range(2):
                            src = PS[0:BS, 6 + n % 2].rearrange("p (r d two) -> p d r two", r=BPO, two=2)[:, :, :, half]
                            dst = RR[half * BS:(half + 1) * BS, c * 64:(c + 1) * 64, :, bass.ds(i * (T // OW) + blk // BPO, 1), b]
                            dst = dst.rearrange("p d r o -> p d (r o)")
                            op = nc.scalar.copy(dst, src)
                        op.then_inc(rr_s, 1)

                take(0, 0, 0)
                with act.Fori(0, TPB - 1) as i:
                    take(i, 1, NB * i + 1)
                    spread(i, 0, NB * i)
                    take(i + 1, 0, NB * i + 2)
                    spread(i, 1, NB * i + 1)
                last = TPB - 1
                take(last, 1, NB * last + 1)
                spread(last, 0, NB * last)
                spread(last, 1, NB * last + 1)

            @block.vector
            def _(dve):
                dve.wait_ge(w_in, 64)
                for b in range(NB):
                    op = nc.vector.memset(U[b][:, :, 0:2], 0.0)
                op.then_inc(zeroed, 1)
                dve.wait_ge(zeroed, 1)
                dve.sem_inc(hist, NB)
                with dve.Fori(0, TPB) as i:
                    for b in range(NB):
                        u = NB * i + b
                        for n, o in enumerate((2, 3, 4, 5, 0, 1)):
                            dve.wait_ge(pj_sb, UC * u + o + 1)
                            c = o % DC
                            a = C[:]
                            at = 2 * (UC * u + n)
                            dve.wait_ge(uc_s, UC * u + n)
                            if n >= 3:
                                dve.wait_ge(v_s, DC * u + min(n - 2, DC))
                            nc.vector.tensor_scalar(a, U[b][:, o, 2:2 + T], fw[:, o, 2:3], fb[:, o:o + 1], ALU.mult, ALU.add).then_inc(tap_s, 1)
                            dve.wait_ge(tap_s, at + 1)
                            nc.vector.scalar_tensor_tensor(a, U[b][:, o, 1:1 + T], fw[:, o, 1:2], a, ALU.mult, ALU.add).then_inc(tap_s, 1)
                            dve.wait_ge(tap_s, at + 2)
                            dst = X0[:, c, tok(b, i)] if o < DC else X1[:, c] if o < 2 * DC else a
                            nc.vector.scalar_tensor_tensor(dst, U[b][:, o, 0:T], fw[:, o, 0:1], a, ALU.mult, ALU.add).then_inc(uc_s, 1)
                            if o >= 2 * DC:
                                dve.wait_ge(uc_s, UC * u + n + 1)
                                if c == 0:
                                    dve.wait_ge(v_free, u + 1)
                                    dve.wait_ge(turned, NTR * (u + 1))
                                nc.vector.tensor_tensor(backwards(Vt[b][:, c], 0, T), a, X1[:, c], ALU.mult).then_inc(v_s, 1)
                        dve.wait_ge(uc_s, UC * (u + 1))
                        nc.vector.tensor_copy(U[b][:, :, 0:2], U[b][:, :, T:T + 2]).then_inc(hist, 1)

            @block.gpsimd
            def _(pool):
                pool.sem_inc(v_free, NB)
                with pool.Fori(0, TPB) as i:
                    for b in range(NB):
                        pool.wait_ge(v_s, DC * (NB * i + b + 1))
                        pool.sem_inc(core.tick, 1)
                        for c in range(DC):
                            op = nc.gpsimd.tensor_copy(V[:, c, tok(b, i)], backwards(Vt[b][:, c], 0, T))
                        op.then_inc(v_free, 1)


def long_conv(core, RR):
    nc, PS = core.nc, core.PS
    zeroed, spread_s, y_ps, y_sb, y_done = (core.sem("lc_" + n) for n in "zeroed spread y_ps y_sb all".split())
    strip_in = [core.sem(f"lc_strip_in{k}") for k in range(2)]
    y_out = [core.sem(f"lc_y_out{k}") for k in range(2)]
    G = D // (2 * PAIRS)
    with ExitStack() as st:
        sb = lambda n, sh, d=F32: st.enter_context(nc.sbuf_tensor("lc_" + n, sh, d))
        strip = [sb(f"strip{k}", [P, PAIRS, HW]) for k in range(2)]
        blocks = [sb(f"blocks{k}", [P, PAIRS, BPO, (JPAD + NJ) // BPO, 2, NB]) for k in range(2)]
        Y = [sb(f"Y{k}", [P, OW]) for k in range(2)]
        with nc.Block() as block:

            @block.sync
            def _(sp):
                with sp.Fori(0, G // 2) as i:
                    for k in range(2):
                        g = 2 * i + k
                        sp.wait_ge(y_ps, g + 1)
                        for j in range(PAIRS):
                            src = bass.AP(core.kpad.tensor, (g * PAIRS + j) * 2 * KW + 1, [[KW, 2], [1, BS], [1, HW]])
                            sp.dma_start(strip[k][:, j], src).then_inc(strip_in[k], 16)

            @block.vector
            def _(dve):
                for k in range(2):
                    op = nc.vector.memset(blocks[k][:], 0.0)
                op.then_inc(zeroed, 1)
                dve.wait_ge(zeroed, 1)
                with dve.Fori(0, G // 2) as i:
                    for k in range(2):
                        g = 2 * i + k
                        dve.wait_ge(y_ps, g + 1)
                        for half in range(2):
                            rows = slice(half * BS, (half + 1) * BS)
                            for b in range(NB):
                                op = nc.vector.tensor_copy(blocks[k][rows, :, :, JPAD // BPO:, half, b],
                                                           RR[rows, bass.ds(g * PAIRS, PAIRS), :, :, b])
                        op.then_inc(spread_s, 1)

            @block.tensor
            def _(pe):
                pe.sem_inc(y_ps, 2)
                with pe.Fori(0, G // 2) as i:
                    for k in range(2):
                        g = 2 * i + k
                        pe.wait_ge(spread_s, g + 1)
                        pe.wait_ge(strip_in[k], 16 * PAIRS * (i + 1))
                        pe.wait_ge(y_sb, g)
                        for lag in LAGS:
                            for j in range(PAIRS):
                                q, r = divmod(JPAD - lag, BPO)
                                lhsT = blocks[k][:, j, r, q:q + NI].rearrange("p q c b -> p (q c b)")
                                mm = nc.tensor.matmul(PS[32 * j:32 * j + 32, k, 0:OW], lhsT,
                                                      strip[k][:, j, (lag - LAG0) * BS:(lag - LAG0) * BS + OW],
                                                      start=(lag == LAG0), stop=(lag == LAG1))
                        mm.then_inc(y_ps, 1)

            @block.scalar
            def _(act):
                for k in range(2):
                    act.sem_inc(y_out[k], 16)
                with act.Fori(0, G // 2) as i:
                    for k in range(2):
                        g = 2 * i + k
                        act.wait_ge(y_ps, g + 1 + 2)
                        act.wait_ge(y_out[k], 16 * (i + 1))
                        nc.scalar.copy(Y[k][:], PS[:, k, 0:OW]).then_inc(y_sb, 1)
                        act.wait_ge(y_sb, g + 1)
                        act.dma_start(core.y_dram[bass.ds(g * P, P)], Y[k][:]).then_inc(y_out[k], 16)
                for k in range(2):
                    act.wait_ge(y_out[k], 16 * (G // 2 + 1))


def conv_out(core, V, X0):
    nc, io, PS, X = core.nc, core.io, core.PS, core.X
    w_in, gbo_s, z_s, o_ps, o_sb, x_done = (core.sem("co_" + n) for n in "w_in gbo z o_ps o_sb x_done".split())
    y_in = [core.sem(f"co_y_in{b}") for b in range(NB)]
    y_view = core.y_dram.rearrange("(pr i ch b) t -> pr ch i b t", b=NB, i=NI, ch=2)
    with ExitStack() as st:
        sb = lambda n, sh, d=F32: st.enter_context(nc.sbuf_tensor("co_" + n, sh, d))
        wo, bo, gbo, fb = sb("wo", [P, DC, D]), sb("bo", [P, DC]), sb("gbo", [P, DC, NB]), sb("fb", [P, DC])
        z = [sb(f"z{b}", [P, DC, T]) for b in range(NB)]
        y = [sb(f"y{b}", [P, DC, T]) for b in range(NB)]
        with nc.Block() as block:

            @block.sync
            def _(sp):
                sp.dma_start(wo[:], io["h_wout"].rearrange("(k p) o -> p k o", p=P)).then_inc(w_in, 16)
                sp.dma_start(bo[:], io["h_bout"]).then_inc(w_in, 16)
                sp.dma_start(fb[:], io["h_fb"]).then_inc(w_in, 16)
                with sp.Fori(0, TPB) as i:
                    for b in range(NB):
                        sp.wait_ge(o_ps, NB * i + b + 1)
                        for c in range(DC):
                            for k in range(T // OW):
                                src = y_view[c * P // 2:(c + 1) * P // 2, :, bass.ds(i * (T // OW) + k, 1), b]
                                sp.dma_start(z[b][:, c, k * OW:(k + 1) * OW], src.rearrange("pr ch o t -> pr ch (o t)")).then_inc(y_in[b], 16)

            @block.vector
            def _(dve):
                dve.wait_ge(w_in, 48)
                for b in range(NB):
                    nc.vector.tensor_tensor(gbo[:, :, b], core.mod[:, 1, GA, :, b], bo[:], ALU.mult).then_inc(gbo_s, 1)
                with dve.Fori(0, TPB) as i:
                    for b in range(NB):
                        dve.wait_ge(y_in[b], 16 * DC * T // OW * (i + 1))
                        for c in range(DC):
                            op = nc.vector.scalar_tensor_tensor(z[b][:, c], V[:, c, tok(b, i)], fb[:, c:c + 1], z[b][:, c],
                                                                ALU.mult, ALU.add)
                        op.then_inc(z_s, 1)
                        dve.wait_ge(z_s, 2 * (NB * i + b) + 1)
                        nc.vector.tensor_tensor(z[b][:], z[b][:], X0[:, :, tok(b, i)], ALU.mult).then_inc(z_s, 1)
                    for b in range(NB):
                        dve.wait_ge(o_sb, NB * i + b + 1)
                        nc.vector.tensor_tensor(X[:, :, tok(b, i)], X[:, :, tok(b, i)], y[b][:], ALU.add).then_inc(x_done, 1)

            @block.tensor
            def _(pe):
                pe.sem_inc(o_ps, NB)
                pe.wait_ge(w_in, 48)
                with pe.Fori(0, TPB) as i:
                    for b in range(NB):
                        pe.wait_ge(z_s, 2 * (NB * i + b + 1))
                        pe.wait_ge(o_sb, NB * i)
                        for c in range(DC):
                            for k in range(DC):
                                mm = nc.tensor.matmul(PS[:, 2 * b + c], wo[:, k, c * P:(c + 1) * P], z[b][:, k],
                                                      start=(k == 0), stop=(k == DC - 1))
                        mm.then_inc(o_ps, 1)

            @block.scalar
            def _(act):
                act.wait_ge(gbo_s, NB)
                with act.Fori(0, TPB) as i:
                    for b in range(NB):
                        act.wait_ge(o_ps, NB * i + b + 1 + NB)
                        act.wait_ge(x_done, NB * i)
                        for c in range(DC):
                            op = nc.scalar.activation(y[b][:, c], PS[:, 2 * b + c], ACT.Identity,
                                                      bias=gbo[:, c, b:b + 1], scale=core.mod[:, 1, GA, c, b:b + 1])
                        op.then_inc(o_sb, 1)



NH1 = 8
HD1 = 64
INNER = NH1 * HD1
IC = INNER // P
WPT = T // P
NPAIR = WPT * IC
HID = 682
HCS = [min(P, HID - o) for o in range(0, HID, P)]
HC = len(HCS)
NORM2_MIN = 1e-24
LN_SCALE = 2.0 ** 20


def shifted(Y, c, b, i):
    return Y[:, c, b, bass.ds(i * T + (0 if c else 1), T)]


def plain(Y, c, b, i):
    return Y[:, c, b, bass.ds(i * T + 1, T)]


UNITS = NPAIR // 2
LAG = 2


def attn1(core, layer, Y, Yn):
    nc, io, PS = core.nc, core.io, core.PS
    tag = f"a1{layer}_"
    w_in, rot_w, hs, pj_ps, raw_s, sqr_s, rot_ps, kss_ps, qss_ps, t1_s, t2_s, kmax, klog, krn, ksum, roped = (
        core.sem(tag + n) for n in
        "w_in rot_w hs pj_ps raw sqr rot_ps kss_ps qss_ps t1 t2 kmax klog krn ksum roped".split())
    qmax, qlog, rq_s, v_ps, v_sb, hist, s_ps, mx_s, nb_s, exp_s, rsum_s, norm_s, tr_ps, pt_s, pv_ps, o_sb, wo_ps, \
        y_done, tab_in = (core.sem(tag + n) for n in
                          "qmax qlog rq v_ps v_sb hist s_ps mx nb exp rsum norm tr_ps pt pv_ps o_sb wo_ps y_done tab_in".split())
    n_w = DC + 5
    QK = 2 * IC
    with ExitStack() as st:
        sb = lambda n, sh, d=F32: st.enter_context(nc.sbuf_tensor(tag + n, sh, d))
        wqkv = sb("wqkv", [P, DC, 3 * INNER])
        wo = sb("wo", [P, IC, D])
        sc = sb("sc", [P, 2])
        rot, rots = sb("rot", [P, P]), sb("rots", [P, 2, P])
        pairsum = sb("pairsum", [P, P])
        headsum = sb("headsum", [P, 2])
        tab = sb("tab", [P, 4, T])
        Hs = sb("Hs", [P, DC, T])
        raw = [sb(f"raw{k}", [P, T]) for k in range(2)]
        sqr = [sb(f"sqr{k}", [P, T]) for k in range(2)]
        t1, t2, kn, rn = sb("t1", [P, T]), sb("t2", [P, T]), sb("kn", [P, T]), sb("rn", [P, T])
        QT = sb("QT", [P, IC, T])
        KT = [sb(f"KT{b}", [P, IC, P + T]) for b in range(NB)]
        V = [sb(f"V{b}", [P, 1 + WPT, INNER]) for b in range(NB)]
        rq = sb("rq", [P, WPT, NH1])
        mx, nb, sums, rsum = (sb(n, [P, WPT, NH1]) for n in ("mx", "nb", "sums", "rsum"))
        Pb = [sb(f"P{k}", [P, 2, 2, 2 * P]) for k in range(3)]
        PTb = [sb(f"PT{k}", [P, 2, 2, P]) for k in range(2)]
        OT = sb("OT", [P, IC, T])

        def tiles(eng, tile):
            for b in range(NB):
                tile(0, b, b, True)
            with eng.Fori(1, TPB) as i:
                for b in range(NB):
                    tile(i, b, NB * i + b, False)

        def keys(x, first):
            return slice(P, 2 * P) if first and x < IC else slice(0, 2 * P)

        def scores(v, ks):
            return PS[:, 2 * (v % 2):2 * (v % 2) + 2].rearrange("p h (j t) -> p h j t", j=2)[:, :, :, ks]

        def heads(buf, v):
            w, g = divmod(v, 2)
            return buf[:, w, 4 * g:4 * g + 4].rearrange("p (j h) -> p h j", h=2)

        with nc.Block() as block:

            @block.sync
            def _(sp):
                for k in range(DC):
                    sp.dma_start(wqkv[:, k], io["wqkv"][layer, k * P:(k + 1) * P]).then_inc(w_in, 16)
                sp.dma_start(wo[:], io["wo"][layer].rearrange("(k p) o -> p k o", p=P)).then_inc(w_in, 16)
                sp.dma_start(sc[:], io["qk_scale"][layer]).then_inc(w_in, 16)
                for t, name in ((rot, "rot"), (pairsum, "pairsum"), (headsum, "headsum")):
                    sp.dma_start(t[:], io[name]).then_inc(w_in, 16)
                tables = io["tables"].rearrange("a p t -> p a t")
                sp.dma_start(tab[:], tables[:, :, 0:T]).then_inc(tab_in, 16)
                with sp.Fori(1, TPB) as i:
                    sp.wait_ge(roped, QK * NB * i)
                    sp.dma_start(tab[:], tables[:, :, bass.ds(i * T, T)]).then_inc(tab_in, 16)

            @block.gpsimd
            def _(pool):
                def tile(i, b, u, first):
                    pool.wait_ge(v_ps, WPT * u)
                    pool.sem_inc(core.tick, 1)
                    for c in range(DC):
                        op = nc.gpsimd.tensor_copy(Hs[:, c], shifted(Y, c, b, i))
                    op.then_inc(hs, 1)
                    for x in range(NPAIR):
                        w, c = divmod(x, IC)
                        ks = keys(x, first)
                        v = x // 2
                        if x % 2 == 0:
                            pool.wait_ge(rsum_s, UNITS * u + v + 1)
                            pool.sem_inc(core.tick, 1)
                        for h in range(2):
                            op = nc.gpsimd.tensor_scalar(Pb[v % 3][:, x % 2, h, ks], Pb[v % 3][:, x % 2, h, ks],
                                                         rsum[:, w, 2 * c + h:2 * c + h + 1], None, ALU.mult)
                        op.then_inc(norm_s, 1)

                tiles(pool, tile)

            @block.tensor
            def _(pe):
                pe.wait_ge(w_in, 16 * n_w)
                pe.wait_ge(rot_w, 2)

                def project(i, b, u):
                    pe.wait_ge(y_done, u)
                    for x in range(QK + 1):
                        if x < QK:
                            if x >= 2:
                                pe.wait_ge(sqr_s, QK * u + x - 1)
                            for k in range(DC):
                                mm = nc.tensor.matmul(PS[:, x % 2], wqkv[:, k, x * P:(x + 1) * P], shifted(Y, k, b, i),
                                                      start=(k == 0), stop=(k == DC - 1))
                            mm.then_inc(pj_ps, 1)
                        if x >= 1:
                            y = x - 1
                            pe.wait_ge(sqr_s, QK * u + y + 1)
                            if y >= 2:
                                pe.wait_ge(t2_s, QK * u + y - 1)
                            nc.tensor.matmul(PS[:, 2 + y % 2], rots[:, y // IC], raw[y % 2][:], start=True, stop=True
                                             ).then_inc(rot_ps, 1)
                            if y >= IC:
                                if y >= IC + 2:
                                    pe.wait_ge(kmax, IC * u + y - IC - 1)
                                nc.tensor.matmul(PS[:, 4 + y % 2], pairsum[:], sqr[y % 2][:], start=True, stop=True
                                                 ).then_inc(kss_ps, 1)
                            else:
                                for w in range(WPT):
                                    col = w * NH1 + 2 * y
                                    mm = nc.tensor.matmul(PS[:, 7, col:col + 2], sqr[y % 2][:, w * P:(w + 1) * P], headsum[:],
                                                          start=True, stop=True)
                                mm.then_inc(qss_ps, 1)
                    pe.wait_ge(hs, u + 1)
                    for w in range(WPT):
                        if w >= 2:
                            pe.wait_ge(v_sb, WPT * u + w - 1)
                        for k in range(DC):
                            mm = nc.tensor.matmul(PS[:, w % 2], Hs[:, k, w * P:(w + 1) * P], wqkv[:, k, 2 * INNER:],
                                                  start=(k == 0), stop=(k == DC - 1))
                        mm.then_inc(v_ps, 1)

                def attend(b, u, first):
                    masks = core.mask[:].rearrange("p a t -> p (a t)")
                    pe.wait_ge(roped, QK * (u + 1))
                    pe.wait_ge(v_sb, WPT * (u + 1))
                    def turn(y):
                        pe.wait_ge(norm_s, NPAIR * u + y + 1)
                        if y >= 2:
                            pe.wait_ge(pt_s, NPAIR * u + y - 1)
                        for h in range(2):
                            for kb in range(keys(y, first).start // P, 2):
                                mm = nc.tensor.transpose(PS[:, 4 + y % 2, (2 * h + kb) * P:(2 * h + kb + 1) * P],
                                                         Pb[y // 2 % 3][:, y % 2, h, kb * P:(kb + 1) * P], core.ident[:])
                        mm.then_inc(tr_ps, 1)

                    def outputs(z):
                        w, c = divmod(z, IC)
                        pe.wait_ge(pt_s, NPAIR * u + z + 1)
                        if c == 0 and w >= 2:
                            pe.wait_ge(o_sb, WPT * u + w - 1)
                        kbs = range(keys(z, first).start // P, 2)
                        for h in range(2):
                            for kb in kbs:
                                mm = nc.tensor.matmul(PS[HD1 * h:HD1 * (h + 1), 6 + w % 2, c * P:(c + 1) * P],
                                                      V[b][:, w + kb, (2 * c + h) * HD1:(2 * c + h + 1) * HD1],
                                                      PTb[z % 2][:, h, kb], start=(kb == kbs[0]), stop=(kb == 1))
                        mm.then_inc(pv_ps, 1)

                    for v in range(UNITS + LAG):
                        if v < UNITS:
                            if v >= 2:
                                pe.wait_ge(exp_s, UNITS * u + v - 1)
                            w, g = divmod(v, 2)
                            ks = keys(2 * v, first)
                            out = scores(v, ks)
                            for h in range(2):
                                rows = slice(HD1 * h, HD1 * (h + 1))
                                for j in range(2):
                                    c = 2 * g + j
                                    nc.tensor.matmul(out[:, h, j], core.lower[:], masks[:, ks], start=True, stop=True)
                                    mm = nc.tensor.matmul(out[:, h, j], QT[rows, c, w * P:(w + 1) * P],
                                                          KT[b][rows, c, w * P + ks.start:w * P + ks.stop],
                                                          start=False, stop=True, skip_group_check=True)
                            mm.then_inc(s_ps, 1)
                        for y in (2 * (v - LAG), 2 * (v - LAG) + 1):
                            if y >= 0:
                                turn(y)
                            if y >= 1:
                                outputs(y - 1)
                    outputs(NPAIR - 1)
                    pe.wait_ge(o_sb, WPT * (u + 1))
                    for c in range(DC):
                        for k in range(IC):
                            mm = nc.tensor.matmul(PS[:, 4 + c], wo[:, k, c * P:(c + 1) * P], OT[:, k], start=(k == 0), stop=(k == IC - 1))
                    mm.then_inc(wo_ps, 1)

                def tile(i, b, u, first):
                    project(i, b, u)
                    attend(b, u, first)

                tiles(pe, tile)

            @block.scalar
            def _(act):
                nc.scalar.preload_act_table_set("natural_log_exp_and_others")

                def tile(i, b, u, first):
                    for x in range(QK + 1):
                        if x < QK:
                            act.wait_ge(pj_ps, QK * u + x + 1)
                            if x >= 2:
                                act.wait_ge(rot_ps, QK * u + x - 1)
                                act.wait_ge(t1_s, QK * u + x - 1)
                                if x - 2 < IC:
                                    act.wait_ge(qss_ps, IC * u + x - 1)
                                else:
                                    act.wait_ge(kss_ps, IC * u + x - 1 - IC)
                            nc.scalar.copy(raw[x % 2][:], PS[:, x % 2]).then_inc(raw_s, 1)
                            nc.scalar.activation(sqr[x % 2][:], PS[:, x % 2], ACT.Square).then_inc(sqr_s, 1)
                        y = x - 1
                        if y >= IC:
                            n = IC * u + y - IC
                            act.wait_ge(kmax, n + 1)
                            nc.scalar.activation(rn[:], rn[:], ACT.Ln, scale=LN_SCALE).then_inc(klog, 1)
                            act.wait_ge(klog, n + 1)
                            nc.scalar.activation(rn[:], rn[:], ACT.Exp, scale=-0.5).then_inc(krn, 1)
                    act.wait_ge(qmax, u + 1)
                    nc.scalar.activation(rq[:], rq[:], ACT.Ln, scale=LN_SCALE).then_inc(qlog, 1)
                    act.wait_ge(qlog, u + 1)
                    nc.scalar.activation(rq[:], rq[:], ACT.Exp, scale=-0.5).then_inc(rq_s, 1)
                    for w in range(WPT):
                        act.wait_ge(v_ps, WPT * u + w + 1)
                        if w == 0:
                            act.wait_ge(hist, u + 1)
                        nc.scalar.copy(V[b][:, 1 + w], PS[:, w % 2]).then_inc(v_sb, 1)

                    def outputs(w):
                        act.wait_ge(pv_ps, NPAIR * u + IC * (w + 1))
                        nc.scalar.copy(OT[:, :, w * P:(w + 1) * P], PS[:, 6 + w % 2].rearrange("p (c t) -> p c t", c=IC)
                                       ).then_inc(o_sb, 1)

                    for v in range(UNITS):
                        w, g = divmod(v, 2)
                        act.wait_ge(nb_s, UNITS * u + v + 1)
                        if v >= 3:
                            act.wait_ge(tr_ps, NPAIR * u + 2 * (v - 2))
                        ks = keys(2 * v, first)
                        for h in range(2):
                            for j in range(2):
                                a = 4 * g + 2 * j + h
                                op = nc.scalar.activation(Pb[v % 3][:, j, h, ks], scores(v, ks)[:, h, j], ACT.Exp,
                                                          bias=nb[:, w, a:a + 1], scale=rq[:, w, a:a + 1],
                                                          accum_out=sums[:, w, a:a + 1])
                        op.then_inc(exp_s, 1)
                        if (v - LAG) % 2 == 1 and v > LAG + 1:
                            outputs((v - LAG) // 2 - 1)
                    for w in range((UNITS - LAG) // 2 - 1, WPT):
                        outputs(w)

                tiles(act, tile)

            @block.vector
            def _(dve):
                dve.wait_ge(w_in, 16 * n_w)
                for a in range(2):
                    nc.vector.tensor_scalar(rots[:, a], rot[:], sc[:, a:a + 1], None, ALU.mult).then_inc(rot_w, 1)

                def keep(b, u, first):
                    if first:
                        dve.sem_inc(hist, 1)
                    else:
                        nc.vector.tensor_copy(KT[b][:, :, 0:P], KT[b][:, :, T:T + P])
                        nc.vector.tensor_copy(V[b][:, 0], V[b][:, WPT]).then_inc(hist, 1)

                def rope(i, b, u):
                    if b == 0:
                        dve.wait_ge(tab_in, 16 * (i + 1))
                    for y in range(QK):
                        a, c = divmod(y, IC)
                        n, m = QK * u + y, IC * u + c
                        dve.wait_ge(raw_s, n + 1)
                        dve.wait_ge(roped, n)
                        nc.vector.scalar_tensor_tensor(t1[:], raw[y % 2][:], sc[:, a:a + 1], tab[:, 2 * a], ALU.mult, ALU.mult
                                                       ).then_inc(t1_s, 1)
                        dve.wait_ge(rot_ps, n + 1)
                        nc.vector.tensor_tensor(t2[:], PS[:, 2 + y % 2], tab[:, 2 * a + 1], ALU.mult).then_inc(t2_s, 1)
                        if a == 1:
                            dve.wait_ge(kss_ps, m + 1)
                            nc.vector.tensor_scalar(rn[:], PS[:, 4 + y % 2], NORM2_MIN, None, ALU.max).then_inc(kmax, 1)
                        dve.wait_ge(t2_s, n + 1)
                        if a == 0:
                            nc.vector.tensor_tensor(QT[:, c], t1[:], t2[:], ALU.add).then_inc(roped, 1)
                        else:
                            nc.vector.tensor_tensor(kn[:], t1[:], t2[:], ALU.add).then_inc(ksum, 1)
                            dve.wait_ge(krn, m + 1)
                            dve.wait_ge(ksum, m + 1)
                            if c == 0:
                                dve.wait_ge(hist, u + 1)
                            nc.vector.tensor_tensor(KT[b][:, c, P:], kn[:], rn[:], ALU.mult).then_inc(roped, 1)
                        if y == IC:
                            dve.wait_ge(qss_ps, IC * (u + 1))
                            nc.vector.tensor_scalar(rq[:].rearrange("p w h -> p (w h)"), PS[:, 7, 0:WPT * NH1], NORM2_MIN, None,
                                                    ALU.max).then_inc(qmax, 1)

                def attend(i, b, u, first):
                    dve.wait_ge(rq_s, u + 1)
                    for v in range(UNITS + LAG):
                        if v < UNITS:
                            n = UNITS * u + v
                            dve.wait_ge(s_ps, n + 1)
                            nc.vector.tensor_reduce(heads(mx, v), scores(v, keys(2 * v, first)), AX_X, ALU.max).then_inc(mx_s, 1)
                            dve.wait_ge(mx_s, n + 1)
                            nc.vector.scalar_tensor_tensor(heads(nb, v), heads(mx, v), -1.0, heads(rq, v), ALU.mult, ALU.mult
                                                           ).then_inc(nb_s, 1)
                        if 1 <= v <= UNITS:
                            dve.wait_ge(exp_s, UNITS * u + v)
                            nc.vector.reciprocal(heads(rsum, v - 1), heads(sums, v - 1)).then_inc(rsum_s, 1)
                        for z in (2 * (v - LAG), 2 * (v - LAG) + 1):
                            if z >= 0:
                                kb = keys(z, first).start // P
                                dve.wait_ge(tr_ps, NPAIR * u + z + 1)
                                if z >= 2:
                                    dve.wait_ge(pv_ps, NPAIR * u + z - 1)
                                src = PS[:, 4 + z % 2].rearrange("p (h k t) -> p h k t", h=2, k=2)
                                nc.vector.tensor_copy(PTb[z % 2][:, :, kb:], src[:, :, kb:]).then_inc(pt_s, 1)
                    dve.wait_ge(wo_ps, u + 1)
                    for c in range(DC):
                        op = nc.vector.tensor_tensor(plain(Yn, c, b, i), plain(Y, c, b, i), PS[:, 4 + c], ALU.add)
                    op.then_inc(y_done, 1)

                def tile(i, b, u, first):
                    keep(b, u, first)
                    rope(i, b, u)
                    attend(i, b, u, first)

                tiles(dve, tile)


def ffn1(core, layer, Y, H):
    nc, io, PS = core.nc, core.io, core.PS
    tag = f"f1{layer}_"
    w_in, ag_ps, gelu_s, hid_s, w2_ps, y_done = (core.sem(tag + n) for n in "w_in ag_ps gelu hid w2_ps y_done".split())
    lag = 2
    with ExitStack() as st:
        sb = lambda n, sh: st.enter_context(nc.sbuf_tensor(tag + n, sh, F32))
        w1, w2 = sb("w1", [P, DC, 2 * HID]), sb("w2", [P, HC, D])
        b1, b2 = sb("b1", [P, 2, HC]), sb("b2", [P, DC])
        gl = [sb(f"gl{k}", [P, T]) for k in range(2)]
        hid = [sb(f"hid{k}", [P, T]) for k in range(4)]
        with nc.Block() as block:

            @block.sync
            def _(sp):
                for k in range(DC):
                    sp.dma_start(w1[:, k], io["l_w1"][layer, k * P:(k + 1) * P]).then_inc(w_in, 16)
                sp.dma_start(w2[:], io["l_w2"][layer]).then_inc(w_in, 16)
                sp.dma_start(b1[:], io["l_b1"][layer]).then_inc(w_in, 16)
                sp.dma_start(b2[:], io["l_b2"][layer]).then_inc(w_in, 16)

            @block.tensor
            def _(pe):
                pe.wait_ge(w_in, 16 * (DC + 3))
                with pe.Fori(0, TPB) as i:
                    for b in range(NB):
                        u = NB * i + b
                        for x in range(HC + lag):
                            if x < HC:
                                if x >= 2:
                                    pe.wait_ge(hid_s, HC * u + x - 1)
                                    pe.sem_inc(core.tick, 1)
                                for half in range(2):
                                    o = half * HID + x * P
                                    for k in range(DC):
                                        mm = nc.tensor.matmul(PS[0:HCS[x], 2 * (x % 2) + half], w1[:, k, o:o + HCS[x]],
                                                              H[:, k, tok(b, i)], start=(k == 0), stop=(k == DC - 1))
                                    mm.then_inc(ag_ps, 1)
                            z = x - lag
                            if z >= 0:
                                pe.wait_ge(hid_s, HC * u + z + 1)
                                if z == 0 and b == 0:
                                    pe.wait_ge(y_done, NB * i)
                                for c in range(DC):
                                    mm = nc.tensor.matmul(PS[:, 4 + 2 * b + c], w2[0:HCS[z], z, c * P:(c + 1) * P],
                                                          hid[z % 4][0:HCS[z]], start=(z == 0), stop=(z == HC - 1))
                                mm.then_inc(w2_ps, 1)

            @block.scalar
            def _(act):
                nc.scalar.preload_act_table_set("gelu_and_others")
                act.wait_ge(w_in, 16 * (DC + 3))
                with act.Fori(0, TPB) as i:
                    for b in range(NB):
                        u = NB * i + b
                        for x in range(HC):
                            g = HC * u + x
                            act.wait_ge(ag_ps, 2 * (g + 1))
                            nc.scalar.activation(gl[x % 2][0:HCS[x]], PS[0:HCS[x], 2 * (x % 2) + 1], ACT.Gelu,
                                                 bias=b1[0:HCS[x], 1, x:x + 1]).then_inc(gelu_s, 1)

            @block.vector
            def _(dve):
                dve.wait_ge(w_in, 16 * (DC + 3))
                with dve.Fori(0, TPB) as i:
                    for b in range(NB):
                        u = NB * i + b
                        for x in range(HC):
                            g = HC * u + x
                            dve.wait_ge(gelu_s, g + 1)
                            if x >= 4:
                                dve.wait_ge(w2_ps, g - 3)
                            nc.vector.scalar_tensor_tensor(hid[x % 4][0:HCS[x]], PS[0:HCS[x], 2 * (x % 2)], b1[0:HCS[x], 0, x:x + 1],
                                                           gl[x % 2][0:HCS[x]], ALU.add, ALU.mult).then_inc(hid_s, 1)
                        dve.wait_ge(w2_ps, HC * (u + 1))
                        for c in range(DC):
                            y = plain(Y, c, b, i)
                            op = nc.vector.scalar_tensor_tensor(y, PS[:, 4 + 2 * b + c], b2[:, c:c + 1], y, ALU.add, ALU.add)
                        op.then_inc(y_done, 1)


def local_layers(core):
    nc, io, mod = core.nc, core.io, core.mod
    saved, zeroed, zeroed_z, ln_in, x_in, out_s, written = (
        core.sem("ll_" + n) for n in "saved zeroed zeroed_z ln_in x_in out written".split())
    padded = lambda n: nc.sbuf_tensor(n, [P, DC, NB, 1 + S], F32)
    with ExitStack() as st:
        Y = st.enter_context(padded("Y"))
        lgb = st.enter_context(nc.sbuf_tensor("lgb", [P, 2, 2, DC], F32))
        with nc.Block() as block:
            @block.sync
            def _(sp):
                sp.dma_start(lgb[:], io["l_ln"]).then_inc(ln_in, 16)
                sp.dma_start(core.x_dram.rearrange("(k p) t -> p k t", p=P), core.X[:]).then_inc(saved, 16)
                sp.wait_ge(saved, 16)
                sp.wait_ge(ln_in, 16)

            @block.gpsimd
            def _(pool):
                nc.gpsimd.memset(Y[:, :, :, 0:1], 0.0).then_inc(zeroed, 1)
                pool.wait_ge(zeroed, 1)
        layernorm(core, "ln3", lambda c, b, i: core.X[:, c, tok(b, i)], lambda c, b, i: plain(Y, c, b, i),
                  lambda c, b: mod[:, 1, CB, c, b:b + 1], lambda c, b: mod[:, 1, SB_, c, b:b + 1])
        Z = core.XP[:].rearrange("p (c b t) -> p c b t", c=DC, b=NB)
        with nc.Block() as block:
            @block.gpsimd
            def _(pool):
                nc.gpsimd.memset(Z[:, :, :, 0:1], 0.0).then_inc(zeroed_z, 1)
                pool.wait_ge(zeroed_z, 1)
        for layer, (src, dst) in enumerate(((Y, Z), (Z, Y))):
            with nc.cleanup_on_exit():
                attn1(core, layer, src, dst)
                with nc.sbuf_tensor(f"H{3 + layer}", [P, DC, NB * S], F32) as H:
                    layernorm(core, f"ln{4 + layer}", lambda c, b, i: shifted(dst, c, b, i), lambda c, b, i: H[:, c, tok(b, i)],
                              lambda c, b: lgb[:, layer, 0, c:c + 1], lambda c, b: lgb[:, layer, 1, c:c + 1])
                    ffn1(core, layer, dst, H)
        xi = [st.enter_context(nc.sbuf_tensor(f"ll_x{b}", [P, DC, T], F32)) for b in range(NB)]
        with nc.Block() as block:
            @block.sync
            def _(sp):
                x_view = core.x_dram.rearrange("(k p) t -> p k t", p=P)
                out_view = io["out"].rearrange("(k p) t -> p k t", p=P)
                with sp.Fori(0, TPB) as i:
                    for b in range(NB):
                        sp.wait_ge(written, 16 * NB * i)
                        sp.dma_start(xi[b][:], x_view[:, :, tok(b, i)]).then_inc(x_in, 16)
                        sp.wait_ge(x_in, 16 * (NB * i + b + 1))
                    for b in range(NB):
                        sp.wait_ge(out_s, NB * i + b + 1)
                        sp.dma_start(out_view[:, :, tok(b, i)], xi[b][:]).then_inc(written, 16)
                sp.wait_ge(written, 16 * NB * TPB)

            @block.vector
            def _(dve):
                with dve.Fori(0, TPB) as i:
                    for b in range(NB):
                        dve.wait_ge(x_in, 16 * (NB * i + b + 1))
                        for c in range(DC):
                            op = nc.vector.scalar_tensor_tensor(xi[b][:, c], plain(Y, c, b, i), mod[:, 1, GB, c, b:b + 1], xi[b][:, c],
                                                                ALU.mult, ALU.add)
                        op.then_inc(out_s, 1)


def program(nc, io):
    with ExitStack() as stack:
        core = Core(nc, stack, io)
        X, mod = core.X, core.mod
        setup(core)
        x_tile = lambda c, b, i: X[:, c, tok(b, i)]
        h_tile = lambda H: lambda c, b, i: H[:, c, tok(b, i)]
        modulated = lambda layer, w_scale, w_shift: (lambda c, b: mod[:, layer, w_scale, c, b:b + 1],
                                                     lambda c, b: mod[:, layer, w_shift, c, b:b + 1])
        with nc.cleanup_on_exit():
            with nc.sbuf_tensor("H", [P, DC, NB * S], F32) as H:
                layernorm(core, "ln0", x_tile, h_tile(H), *modulated(0, CA, SA))
                with nc.sbuf_tensor("VV", [P, NB, NBLK, NH0, HD0 + 1], F32) as VV:
                    attn0_project(core, H, VV)
                    attn0_scores(core, VV)
            attn0_out(core)
        with nc.cleanup_on_exit():
            with nc.sbuf_tensor("H1", [P, DC, NB * S], F32) as H:
                layernorm(core, "ln1", x_tile, h_tile(H), *modulated(0, CB, SB_))
                ffn0(core, H)
            filter_taps(core)
            with ExitStack() as st:
                V, X0 = (st.enter_context(nc.sbuf_tensor(n, [P, DC, NB * S], F32)) for n in ("V", "X0"))
                RR = st.enter_context(nc.sbuf_tensor("RR", [P, D // 2, BPO, NJ // BPO, NB], F32))
                with nc.sbuf_tensor("H2", [P, DC, NB * S], F32) as H:
                    layernorm(core, "ln2", x_tile, h_tile(H), *modulated(1, CA, SA))
                    conv_inputs(core, H, V, X0, RR)
                long_conv(core, RR)
                conv_out(core, V, X0)
        local_layers(core)




def columns(v):
    v = np.asarray(v)
    v = v.reshape(v.shape[:-1] + (-1, P))
    return np.moveaxis(v, -1, 0)


def filter_positions():
    f32 = np.float32
    t = np.linspace(0, 1, NT).astype(f32)
    w = (2 * np.pi * np.linspace(0, NT - 1, NT) / NT).astype(f32)
    fw = f32(1e-4) * w
    deltas = np.abs(np.linspace(np.log(0.01) / 1.5, np.log(0.01) / 0.3, D)).astype(f32)
    return {"f_z": np.stack([t, np.cos(fw), -np.sin(fw)]).astype(f32),
            "f_decay": (np.exp(-deltas[:, None] * t[None]) + f32(0.05)).astype(f32)}


def rotary_tables():
    f32 = np.float32
    half = np.arange(0, HD1, 2, dtype=f32)
    t = np.arange(S, dtype=f32)
    angle = t[:, None] * (1 / f32(10000) ** (half / f32(HD1))).astype(f32)[None]
    base = ((half + f32(0.4 * HD1)) / f32(1.4 * HD1)).astype(f32)
    power = ((t - S // 2) / f32(P // 2)).astype(f32)
    scale = base[None] ** power[:, None]
    cos, sin = np.cos(angle), np.sin(angle)
    up = f32(LN_SCALE ** 0.5)
    tables = np.stack([cos * scale * (8 * up), sin * scale * (8 * up), cos / scale * up, sin / scale * up])
    return np.tile(tables.transpose(0, 2, 1), (1, 4, 1)).astype(f32)


def head_matrices():
    rot = np.zeros((P, P), np.float32)
    for h in range(0, P, HD1):
        for j in range(HD1 // 2):
            rot[h + j + HD1 // 2, h + j] = -1
            rot[h + j, h + j + HD1 // 2] = 1
    head = np.arange(P) // HD1
    return {"rot": rot, "pairsum": (head[:, None] == head[None]).astype(np.float32),
            "headsum": (head[:, None] == np.arange(2)[None]).astype(np.float32)}


def layout(d):
    d = {k: np.asarray(v) for k, v in d.items()}
    o = {"xT": d["L0_attn_x"].reshape(NB * S, D).T,
         "cT": np.stack([d["L0_c"], d["L1_c"]]).transpose(2, 0, 1),
         "wmod": np.stack([d["L0_wmod"], d["L1_wmod"]])}
    for n in ("Wq", "Wk", "Wv", "Wo"):
        o[n.lower() + "T"] = d["L0_attn_" + n].T
    for n in ("bq", "bk", "bv", "bo"):
        o[n] = columns(d["L0_attn_" + n])
    cross, shift = np.zeros((DC, P, P), np.float32), np.zeros((DC, P, P), np.float32)
    for h in range(NH0):
        c, r = h // HPC, h % HPC * HD0
        cross[c, r:r + HD0, r:r + HD0] = d["L0_attn_W_cross"][h]
        for f in range(HD0):
            n = min(MS0, HD0 - f)
            shift[c, r + f, r + f:r + f + n] = d["L0_attn_shift_weights"][h, :n]
    o["wc_bd"], o["shift_bd"] = cross, shift
    o["gate_rep"] = columns(np.repeat(d["L0_attn_gate"], HD0))
    for n in ("w1", "w2", "h1", "h2", "w3"):
        o[n + "T"] = d[f"L0_ffn_{n}_w"].T
        o[n + "s"] = columns(d[f"L0_ffn_{n}_s"])
    A = lambda n: d["L1_attn_" + n]
    o.update(filter_positions())
    for k in (1, 2, 3):
        o[f"f_w{k}"] = A(f"f_w{k}")
    o["f_bf"] = np.stack([np.stack([A(f"f_b{k}"), A(f"freq{k}")], -1) for k in (1, 2, 3)], 1)
    o["f_wout"], o["h_win"], o["h_wout"] = A("f_wout"), A("w_in"), A("w_out")
    o["h_bin"], o["h_sfb"], o["h_bout"], o["h_fb"] = (columns(A(n)) for n in ("b_in", "sf_b", "b_out", "filt_bias"))
    o["h_sfw"] = A("sf_w").reshape(UC, P, -1).transpose(1, 0, 2)
    F = lambda n: d["L1_ffn_" + n]
    depth = F("wqkv").shape[0]
    o["wqkv"], o["wo"], o["l_w1"] = F("wqkv"), F("wo"), F("w1")
    o["qk_scale"] = np.stack([np.tile(F(n), (1, P // HD1)) for n in ("q_scale", "k_scale")], -1)
    o["tables"] = rotary_tables()
    o.update(head_matrices())
    o["l_ln"] = columns(np.stack([F("ln_g"), F("ln_b")], 1))
    w2 = np.zeros((depth, HC * P, D), np.float32)
    w2[:, :HID] = F("w2")
    o["l_w2"] = w2.reshape(depth, HC, P, D).transpose(0, 2, 1, 3)
    b1 = np.zeros((depth, 2, HC * P), np.float32)
    b1[:, :, :HID] = F("b1").reshape(depth, 2, HID)
    o["l_b1"] = b1.reshape(depth, 2, HC, P).transpose(0, 3, 1, 2)
    o["l_b2"] = F("b2").reshape(depth, DC, P).transpose(0, 2, 1)
    return {k: np.ascontiguousarray(v) for k, v in o.items()}


def kernel(**inputs):
    import concourse.bacc as bacc
    from concourse.bass_utils import run_bass_kernel_spmd

    nc = bacc.Bacc("TRN2", target_bir_lowering=False, num_devices=1)
    arrays = {"in_" + k: v for k, v in layout(inputs).items()}
    io = {k[3:]: nc.dram_tensor(k, v.shape, mybir.dt.from_np(v.dtype), kind="ExternalInput").ap()
          for k, v in arrays.items()}
    io["out"] = nc.dram_tensor("out", (D, NB * S), F32, kind="ExternalOutput").ap()
    program(nc, io)
    r = run_bass_kernel_spmd(nc, [arrays], core_ids=[0])
    return np.ascontiguousarray(r.results[0]["out"].T).reshape(NB, S, D)
```

```python
from contextlib import ExitStack

import numpy as np

import concourse.bass as bass
from concourse import mybir
from concourse.alu_op_type import AluOpType as ALU

F32 = mybir.dt.float32
BF16 = mybir.dt.bfloat16
ACT = mybir.ActivationFunctionType
AX_X = mybir.AxisListType.X

P = 128
D = 256
DC = D // P
NB = 2
S = 2048
T = 512
TPB = S // T
EPS = 1e-5
BIG = 1e30

BELOW, ABOVE = 0, 1

SA, CA, GA, SB_, CB, GB = range(6)


def tok(b, i):
    return bass.ds(i * T + b * S, T)


class Core:

    def __init__(self, nc, stack, io):
        self.nc, self.io, self.stack = nc, io, stack
        self.XP = stack.enter_context(nc.sbuf_tensor("X", [P, DC * NB * (1 + S)], F32))
        self.X = self.XP[:, 0:DC * NB * S].rearrange("p (c t) -> p c t", c=DC)
        self.ones = stack.enter_context(nc.sbuf_tensor("ones", [P, P], F32))
        self.ident = stack.enter_context(nc.sbuf_tensor("ident", [P, P], F32))
        self.identb = stack.enter_context(nc.sbuf_tensor("identb", [P, P], BF16))
        self.lower = stack.enter_context(nc.sbuf_tensor("lower", [P, P], BF16))
        self.mask = stack.enter_context(nc.sbuf_tensor("mask", [P, 2, P], BF16))
        self.eps = stack.enter_context(nc.sbuf_tensor("eps", [P, 1], F32))
        self.mod = stack.enter_context(nc.sbuf_tensor("mod", [P, 2, 6, DC, NB], F32))
        self.PS = stack.enter_context(nc.psum_tensor("PS", [P, 8, 512], F32))
        self.tick = self.sem("tick")
        self.qk_parts = nc.dram_tensor("qk_parts", [2, NB, 3, D, S], BF16, kind="Internal").ap()
        self.o_dram = nc.dram_tensor("o_dram", [NB, NH0, HD0, S], F32, kind="Internal").ap()
        self.sum_dram = nc.dram_tensor("sum_dram", [NB, NH0, S], F32, kind="Internal").ap()
        self.kpad = nc.dram_tensor("kpad", [D, KW], F32, kind="Internal").ap()
        self.x_dram = nc.dram_tensor("x_dram", [D, NB * S], F32, kind="Internal").ap()
        self.y_dram = nc.dram_tensor("y_dram", [D * NB * NI, OW], F32, kind="Internal").ap()
        self.recip_dram = nc.dram_tensor("recip_dram", [NB, NH0, S], F32, kind="Internal").ap()

    def sem(self, name):
        return self.nc.alloc_semaphore(name=name)


def setup(core):
    nc, io, mod = core.nc, core.io, core.mod
    loaded, x_in = core.sem("su_loaded"), core.sem("su_x_in")
    filled, picked = core.sem("su_filled"), core.sem("su_picked")
    c_act, mod_ps, mod_sb, gate_parts = (core.sem("su_" + n) for n in ("c_act", "mod_ps", "mod_sb", "gate_parts"))
    done = core.sem("su_done")
    with ExitStack() as st:
        sb = lambda n, s, d=F32: st.enter_context(nc.sbuf_tensor(n, s, d))
        cT = sb("cT", [P, DC, 2, NB])
        cs = sb("cs", [P, DC, 2, NB])
        wm = sb("wm", [P, 2, DC, 6 * D])
        sgn = sb("sgn", [P, 2, 2, DC, NB])
        mag = sb("mag", [P, 2, 2, DC, NB])
        ps = core.PS[:, 0]
        with nc.Block() as block:

            @block.sync
            def _(sp):
                sp.dma_start(cT[:], io["cT"].rearrange("(k p) l b -> p k l b", p=P)).then_inc(loaded, 16)
                for layer in range(2):
                    sp.dma_start(wm[:, layer], io["wmod"][layer].rearrange("(k p) n -> p k n", p=P)).then_inc(loaded, 16)
                sp.dma_start(core.X[:], io["xT"].rearrange("(k p) t -> p k t", p=P)).then_inc(x_in, 16)
                sp.wait_ge(x_in, 16)

            @block.gpsimd
            def _(pool):
                nc.gpsimd.memset(core.eps[:], EPS)
                nc.gpsimd.memset(core.ones[:], 1.0 / D)
                nc.gpsimd.memset(core.ident[:], 0.0)
                nc.gpsimd.memset(core.identb[:], 0.0)
                nc.gpsimd.memset(core.lower[:], 0.0)
                nc.gpsimd.memset(core.mask[:], 0.0).then_inc(filled, 1)
                pool.wait_ge(filled, 1)
                eye = [[-1, P]]
                nc.gpsimd.affine_select(out=core.ident[:], in_=core.ident[:], compare_op=ALU.not_equal, fill=1.0,
                                        base=0, pattern=eye, channel_multiplier=1)
                nc.gpsimd.affine_select(out=core.identb[:], in_=core.identb[:], compare_op=ALU.not_equal, fill=1.0,
                                        base=0, pattern=eye, channel_multiplier=1)
                nc.gpsimd.affine_select(out=core.lower[:], in_=core.lower[:], compare_op=ALU.not_equal, fill=-BIG,
                                        base=0, pattern=eye, channel_multiplier=1)
                nc.gpsimd.affine_select(out=core.mask[:, BELOW], in_=core.mask[:, BELOW], compare_op=ALU.is_ge, fill=1.0,
                                        base=0, pattern=[[1, P]], channel_multiplier=-1)
                nc.gpsimd.affine_select(out=core.mask[:, ABOVE], in_=core.mask[:, ABOVE], compare_op=ALU.is_ge, fill=1.0,
                                        base=0, pattern=[[-1, P]], channel_multiplier=1).then_inc(picked, 1)
                pool.wait_ge(picked, 1)

            @block.scalar
            def _(act):
                act.wait_ge(loaded, 16 * 3)
                nc.scalar.activation(cs[:], cT[:], ACT.Silu).then_inc(c_act, 1)

            @block.tensor
            def _(pe):
                pe.wait_ge(c_act, 1)
                for layer in range(2):
                    for o in range(6 * DC):
                        col = (layer * 6 * DC + o) * NB
                        for k in range(DC):
                            mm = nc.tensor.matmul(ps[:, col:col + NB], wm[:, layer, k, o * P:(o + 1) * P],
                                                  cs[:, k, layer, :], start=(k == 0), stop=(k == DC - 1))
                mm.then_inc(mod_ps, 1)

            @block.vector
            def _(dve):
                dve.wait_ge(mod_ps, 1)
                nc.vector.tensor_copy(mod[:].rearrange("p l w k b -> p (l w k b)"),
                                      ps[:, 0:2 * 6 * DC * NB]).then_inc(mod_sb, 1)
                dve.wait_ge(mod_sb, 1)
                for j, w in enumerate((GA, GB)):
                    nc.vector.tensor_scalar(sgn[:, j], mod[:, :, w], 0.0, 2.0, ALU.is_ge, ALU.mult).then_inc(gate_parts, 1)
                    for layer in range(2):
                        nc.vector.scalar_tensor_tensor(mag[:, j, layer], mod[:, layer, w], -1.0, mod[:, layer, w],
                                                       ALU.mult, ALU.max).then_inc(gate_parts, 1)
                dve.wait_ge(gate_parts, 6)
                nc.vector.tensor_scalar(mag[:], mag[:], 0.25, None, ALU.max).then_inc(gate_parts, 1)
                dve.wait_ge(gate_parts, 7)
                for j, w in enumerate((GA, GB)):
                    for layer in range(2):
                        nc.vector.scalar_tensor_tensor(mod[:, layer, w], sgn[:, j, layer], -1.0, mag[:, j, layer],
                                                       ALU.add, ALU.mult).then_inc(done, 1)
                for w in (CA, CB):
                    nc.vector.tensor_scalar(mod[:, :, w], mod[:, :, w], 1.0, None, ALU.add).then_inc(done, 1)
                dve.wait_ge(done, 6)


def layernorm(core, tag, src, dst, scale, bias):
    nc, PS = core.nc, core.PS
    mean, centred, squared, var, logged, rstd, normed, done = (
        core.sem(f"{tag}_{n}") for n in ("mean", "centred", "squared", "var", "logged", "rstd", "normed", "done"))
    with ExitStack() as st:
        sb = lambda n, sh: st.enter_context(nc.sbuf_tensor(f"{tag}_{n}", sh, F32))
        xc = [sb(f"xc{b}", [P, DC, T]) for b in range(NB)]
        sq = [sb(f"sq{b}", [P, DC, T]) for b in range(NB)]
        ln = [sb(f"ln{b}", [P, T]) for b in range(NB)]
        rs = [sb(f"rs{b}", [P, T]) for b in range(NB)]
        with nc.Block() as block:

            def pipeline(eng, ahead, behind):
                ahead(0, 0)
                ahead(0, 1)
                behind(0, 0)
                with eng.Fori(1, TPB) as i:
                    ahead(i, 0)
                    behind(i - 1, 1)
                    ahead(i, 1)
                    behind(i, 0)
                behind(TPB - 1, 1)

            @block.tensor
            def _(pe):
                def means(i, b):
                    if not (isinstance(i, int) and i == 0):
                        pe.wait_ge(centred, NB * (i - 1) + b + 1)
                    for c in range(DC):
                        mm = nc.tensor.matmul(PS[:, b], core.ones[:], src(c, b, i), start=(c == 0), stop=(c == DC - 1))
                    mm.then_inc(mean, 1)

                def variances(i, b):
                    pe.wait_ge(squared, NB * i + b + 1)
                    for c in range(DC):
                        mm = nc.tensor.matmul(PS[:, 2 + b], core.ones[:], sq[b][:, c], start=(c == 0), stop=(c == DC - 1))
                    mm.then_inc(var, 1)

                pipeline(pe, means, variances)

            @block.vector
            def _(dve):
                def centre(i, b):
                    dve.wait_ge(mean, NB * i + b + 1)
                    if not (isinstance(i, int) and i == 0):
                        dve.wait_ge(done, NB * (i - 1) + b + 1)
                    for c in range(DC):
                        op = nc.vector.tensor_tensor(xc[b][:, c], src(c, b, i), PS[:, b], ALU.subtract)
                    op.then_inc(centred, 1)

                def scale_shift(i, b):
                    dve.wait_ge(rstd, NB * i + b + 1)
                    for c in range(DC):
                        op = nc.vector.tensor_tensor(xc[b][:, c], xc[b][:, c], rs[b][:], ALU.mult)
                    op.then_inc(normed, 1)
                    dve.wait_ge(normed, NB * i + b + 1)
                    for c in range(DC):
                        op = nc.vector.tensor_scalar(dst(c, b, i), xc[b][:, c], scale(c, b), bias(c, b), ALU.mult, ALU.add)
                    op.then_inc(done, 1)

                pipeline(dve, centre, scale_shift)

            @block.scalar
            def _(act):
                nc.scalar.preload_act_table_set("natural_log_exp_and_others")

                def square(i, b):
                    act.wait_ge(centred, NB * i + b + 1)
                    if not (isinstance(i, int) and i == 0):
                        act.wait_ge(var, NB * (i - 1) + b + 1)
                    nc.scalar.activation(sq[b][:], xc[b][:], ACT.Square).then_inc(squared, 1)

                def root(i, b):
                    act.wait_ge(var, NB * i + b + 1)
                    nc.scalar.activation(ln[b][:], PS[:, 2 + b], ACT.Ln, bias=core.eps[:]).then_inc(logged, 1)
                    act.wait_ge(logged, NB * i + b + 1)
                    nc.scalar.activation(rs[b][:], ln[b][:], ACT.Exp, scale=-0.5).then_inc(rstd, 1)

                pipeline(act, square, root)



NH0 = 16
HD0 = D // NH0
HPC = P // HD0
MS0 = HD0 // 2
NBLK = S // P
TB = T // P
Q_PARTS = (0, 0, 0, 1, 2, 1)
K_PARTS = (0, 1, 2, 0, 0, 1)
STK = len(Q_PARTS) * HD0
AUG = STK + 3
P1_FROM, P1_TO = 0.1, 0.9


def attn0_project(core, H, VV):
    nc, io, PS = core.nc, core.io, core.PS
    names = ("w_in sig mixed hs_ready q_ps k_ps qt_ps v_ps q_sb k_sb hi_q hi_k rest_q rest_k mid_q mid_k lo_q lo_k "
             "v_sb zeroed table")
    w_in, sig, mixed, hs_ready, q_ps, k_ps, qt_ps, v_ps, q_sb, k_sb, hi_q, hi_k, rest_q, rest_k, mid_q, mid_k, lo_q, \
        lo_k, v_sb, zeroed, table = (core.sem("a0p_" + n) for n in names.split())
    parts_out = [core.sem(f"a0p_parts_out{b}") for b in range(NB)]
    tick = core.sem("a0p_tick")
    with ExitStack() as st:
        sb = lambda n, sh, d=F32: st.enter_context(nc.sbuf_tensor("a0p_" + n, sh, d))
        wq, wk, wv = (sb(n, [P, DC, D]) for n in ("wq", "wk", "wv"))
        bq, bk, gate, g = (sb(n, [P, DC]) for n in ("bq", "bk", "gate", "g"))
        wc, wm = sb("wc", [P, DC, P]), sb("wm", [P, DC, P])
        A = sb("A", [P, DC, P])
        Hs = [sb(f"Hs{b}", [P, DC, T]) for b in range(NB)]
        qsb = [sb(f"qsb{b}", [P, DC, T]) for b in range(NB)]
        ksb = [sb(f"ksb{b}", [P, DC, T]) for b in range(NB)]
        rest = [sb(f"rest{b}", [P, 2, DC, T]) for b in range(NB)]
        parts = [sb(f"parts{b}", [P, 2, 3, DC, T], BF16) for b in range(NB)]
        n_w = 8
        with nc.Block() as block:

            @block.sync
            def _(sp):
                for t, name in ((wq, "wqT"), (wk, "wkT"), (wv, "wvT")):
                    sp.dma_start(t[:], io[name].rearrange("(k p) o -> p k o", p=P)).then_inc(w_in, 16)
                for t, name in ((wc, "wc_bd"), (wm, "shift_bd")):
                    sp.dma_start(t[:], io[name].rearrange("k p o -> p k o")).then_inc(w_in, 16)
                for t, name in ((bq, "bq"), (bk, "bk"), (gate, "gate_rep")):
                    sp.dma_start(t[:], io[name]).then_inc(w_in, 16)
                with sp.Fori(0, TPB) as i:
                    for b in range(NB):
                        for w, ready in ((0, lo_q), (1, lo_k)):
                            sp.wait_ge(ready, NB * i + b + 1)
                            for part in range(3):
                                dst = core.qk_parts[w, b, part].rearrange("(c p) s -> p c s", p=P)[:, :, bass.ds(i * T, T)]
                                sp.dma_start(dst, parts[b][:, w, part]).then_inc(parts_out[b], 16)
                for b in range(NB):
                    sp.wait_ge(parts_out[b], 96 * (TPB + 1))

            @block.gpsimd
            def _(pool):
                nc.gpsimd.memset(VV[:], 1.0).then_inc(zeroed, 1)
                def copy_h(i, b):
                    pool.wait_ge(v_sb, NB * i + b + 1)
                    pool.sem_inc(tick, 1)
                    nc.gpsimd.tensor_copy(Hs[b][:], H[:, :, tok(b, i)]).then_inc(hs_ready, 1)

                def middle(i, b):
                    for w, r, m in ((1, rest_k, mid_k), (0, rest_q, mid_q)):
                        pool.wait_ge(r, NB * i + b + 2)
                        pool.sem_inc(tick, 1)
                        nc.gpsimd.tensor_copy(parts[b][:, w, 1], rest[b][:, w]).then_inc(m, 1)

                pool.sem_inc(rest_k, 1)
                copy_h(0, 0)
                with pool.Fori(0, TPB - 1) as i:
                    copy_h(i, 1)
                    middle(i, 0)
                    copy_h(i + 1, 0)
                    middle(i, 1)
                copy_h(TPB - 1, 1)
                middle(TPB - 1, 0)
                middle(TPB - 1, 1)

            @block.scalar
            def _(act):
                for b in range(NB):
                    act.sem_inc(parts_out[b], 96)
                act.wait_ge(w_in, 16 * n_w)
                nc.scalar.activation(g[:], gate[:], ACT.Sigmoid).then_inc(sig, 1)
                with act.Fori(0, TPB) as i:
                    for b in range(NB):
                        act.wait_ge(q_ps, NB * i + b + 1)
                        for c in range(DC):
                            op = nc.scalar.activation(qsb[b][:, c], PS[:, c], ACT.Identity, bias=bq[:, c:c + 1])
                        op.then_inc(q_sb, 1)
                        act.wait_ge(k_ps, NB * i + b + 1)
                        for c in range(DC):
                            op = nc.scalar.activation(ksb[b][:, c], PS[:, 2 + c], ACT.Identity, bias=bk[:, c:c + 1])
                        op.then_inc(k_sb, 1)
                        act.wait_ge(parts_out[b], 96 * (i + 1))
                        act.wait_ge(k_sb, NB * i + b + 2)
                        nc.scalar.copy(parts[b][:, 1, 0], ksb[b][:]).then_inc(hi_k, 1)
                        act.wait_ge(qt_ps, NB * i + b + 1)
                        nc.scalar.copy(parts[b][:, 0, 0], PS[:, 4:6]).then_inc(hi_q, 1)

            @block.vector
            def _(dve):
                dve.sem_inc(v_sb, NB)
                dve.wait_ge(sig, 1)
                nc.vector.tensor_tensor(wc[:], wc[:], wm[:], ALU.subtract).then_inc(mixed, 1)
                dve.wait_ge(mixed, 1)
                for c in range(DC):
                    nc.vector.scalar_tensor_tensor(A[:, c], wc[:, c], g[:, c:c + 1], wm[:, c], ALU.mult, ALU.add).then_inc(mixed, 1)
                dve.wait_ge(mixed, 1 + DC)
                nc.vector.tensor_scalar(A[:], A[:], float(HD0) ** -0.5, None, ALU.mult).then_inc(mixed, 1)
                dve.wait_ge(zeroed, 1)
                with dve.Fori(0, TPB) as i:
                    for b in range(NB):
                        dve.wait_ge(hi_k, NB * i + b + 1)
                        nc.vector.tensor_tensor(rest[b][:, 1], ksb[b][:], parts[b][:, 1, 0], ALU.subtract).then_inc(rest_k, 1)
                        dve.wait_ge(v_ps, NB * i + b + 1)
                        for j in range(2):
                            dst = VV[:, b, bass.ds(i * TB + 2 * j, 2), :, 0:HD0]
                            op = nc.vector.tensor_copy(dst, PS[:, 6 + j].rearrange("p (k h f) -> p k h f", k=2, h=NH0))
                        op.then_inc(v_sb, 1)
                        dve.wait_ge(hi_q, NB * i + b + 1)
                        nc.vector.tensor_tensor(rest[b][:, 0], PS[:, 4:6], parts[b][:, 0, 0], ALU.subtract).then_inc(rest_q, 1)
                        dve.wait_ge(mid_k, NB * i + b + 1)
                        nc.vector.tensor_tensor(parts[b][:, 1, 2], rest[b][:, 1], parts[b][:, 1, 1], ALU.subtract).then_inc(lo_k, 1)
                        dve.wait_ge(mid_q, NB * i + b + 1)
                        nc.vector.tensor_tensor(parts[b][:, 0, 2], rest[b][:, 0], parts[b][:, 0, 1], ALU.subtract).then_inc(lo_q, 1)

            @block.tensor
            def _(pe):
                pe.wait_ge(w_in, 16 * n_w)
                pe.wait_ge(mixed, 2 + DC)
                pe.sem_inc(k_sb, 1)
                pe.sem_inc(rest_q, 1)
                with pe.Fori(0, TPB) as i:
                    for b in range(NB):
                        for c in range(DC):
                            for k in range(DC):
                                mm = nc.tensor.matmul(PS[:, c], wq[:, k, c * P:(c + 1) * P], H[:, k, tok(b, i)],
                                                      start=(k == 0), stop=(k == DC - 1))
                        mm.then_inc(q_ps, 1)
                        pe.wait_ge(k_sb, NB * i + b + 1)
                        for c in range(DC):
                            for k in range(DC):
                                mm = nc.tensor.matmul(PS[:, 2 + c], wk[:, k, c * P:(c + 1) * P], H[:, k, tok(b, i)],
                                                      start=(k == 0), stop=(k == DC - 1))
                        mm.then_inc(k_ps, 1)
                        pe.wait_ge(hs_ready, NB * i + b + 1)
                        pe.wait_ge(v_sb, NB * i + b + NB)
                        for j in range(TB):
                            for k in range(DC):
                                mm = nc.tensor.matmul(PS[:, 6 + j // 2, (j % 2) * D:(j % 2 + 1) * D],
                                                      Hs[b][:, k, j * P:(j + 1) * P], wv[:, k],
                                                      start=(k == 0), stop=(k == DC - 1))
                        mm.then_inc(v_ps, 1)
                        pe.wait_ge(q_sb, NB * i + b + 1)
                        pe.wait_ge(rest_q, NB * i + b + 1)
                        for c in range(DC):
                            mm = nc.tensor.matmul(PS[:, 4 + c], A[:, c], qsb[b][:, c], start=True, stop=True)
                        mm.then_inc(qt_ps, 1)


def attn0_scores(core, VV):
    nc, PS = core.nc, core.PS
    ST = NH0
    names = "ones_set vu mx_set p1_ps p1_read mx neg part m_ps m_sb m_in s_ps exp_done pv_done o_sb"
    ones_set, vu, mx_set, p1_ps, p1_read, mx_s, neg_s, part_s, m_ps, m_sb, m_in, s_ps, exp_done, pv_done, o_sb = (
        core.sem("a0s_" + n) for n in names.split())
    stack_in = [[core.sem(f"a0s_stack_in{p}{b}") for b in range(NB)] for p in range(2)]
    o_out = core.sem("a0s_o_out")
    tick = core.sem("a0s_tick")
    N_IN = 16 * 6
    N_P1 = NB * (sum((q // 4 + 1) for q in range(NBLK)) + 1)
    N_S2 = NB * (NBLK + NBLK // 2)
    N_PV = NB * NBLK
    N_OUT = 16 * NB * 8
    with ExitStack() as st:
        sb = lambda n, sh, d=F32: st.enter_context(nc.sbuf_tensor("a0s_" + n, sh, d))
        QS = [[sb(f"QS{p}{b}", [AUG, S], BF16) for b in range(NB)] for p in range(2)]
        KS = [[sb(f"KS{p}{b}", [AUG, S], BF16) for b in range(NB)] for p in range(2)]
        VU = [[sb(f"VU{p}{b}", [P, NBLK, HD0 + 1]) for b in range(NB)] for p in range(2)]
        PT = [[sb(f"PT{b}{k}", [P, S]) for k in range(2)] for b in range(NB)]
        mx = [sb(f"mx{b}", [P, NBLK, 4]) for b in range(NB)]
        rowmax = [sb(f"rowmax{b}", [P, NBLK]) for b in range(NB)]
        rest = [sb(f"rest{b}", [P, NBLK]) for b in range(NB)]
        mparts = [sb(f"mparts{b}", [P, P // NBLK, NBLK], BF16) for b in range(NB)]
        mrow = [sb(f"mrow{b}", [3 * NBLK, P], BF16) for b in range(NB)]
        O = [sb(f"O{b}", [P, T]) for b in range(NB)]

        last_pair = ST // 2 - 1

        def stages(eng, stage):
            with eng.Fori(0, last_pair) as it:
                for par in range(2):
                    stage(2 * it + par, par, it, True)
            for par in range(2):
                stage(ST - 2 + par, par, last_pair, par == 0)

        def pass1_blocks():
            for b in range(NB):
                for q in range(NBLK):
                    for j in range(q // 4 + 1):
                        yield b, q, j
                    if b == 1 and q == 3:
                        yield 0, None, None
            yield 1, None, None

        P1 = list(pass1_blocks())
        assert len(P1) == N_P1

        def p2_groups(kt):
            return [g for g in range(2) if 1024 * (g + 1) > kt * P]

        def group(b, qc):
            return qc if b == 0 else 3 - qc

        G2 = {}
        for kt in range(NBLK):
            for b in range(NB):
                for g in p2_groups(kt):
                    G2[kt, b, g] = len(G2)
        assert len(G2) == N_S2

        def order(more):
            main = [("s", (0, b, g)) for b in range(NB) for g in range(2)]
            for kt in range(NBLK):
                groups = [("s", (kt + 1, b, g)) for b in range(NB) for g in p2_groups(kt + 1)] if kt + 1 < NBLK else []
                main += groups[:len(groups) // 2] + [("o", kt)] + groups[len(groups) // 2:]

            def weight(what, key):
                if what == "o":
                    return 1.7 if key < 8 else 0.85
                kt, b, g = key
                return 0.2 + (1024 * (g + 1) - max(kt * P, 1024 * g)) / 1200

            total = sum(weight(*m) for m in main)
            done, x = 0.0, 0
            for m in main:
                while more and x < min(N_P1, N_P1 * (done / total - P1_FROM) / (P1_TO - P1_FROM)):
                    yield "p", x
                    x += 1
                yield m
                done += weight(*m)
            assert not more or x == N_P1

        def load(dma, par, b, h):
            rows = bass.ds(h * HD0, HD0)
            q, k = core.qk_parts[0, b], core.qk_parts[1, b]
            qs, ks, done = QS[par][b], KS[par][b], stack_in[par][b]
            dma(qs[0:3 * HD0, :], q[0:1, rows, :].broadcast_to([3, HD0, S])).then_inc(done, 16)
            dma(qs[3 * HD0:5 * HD0, :], q[1:3, rows, :]).then_inc(done, 16)
            dma(qs[5 * HD0:6 * HD0, :], q[1, rows, :]).then_inc(done, 16)
            dma(ks[0:3 * HD0, :], k[:, rows, :]).then_inc(done, 16)
            dma(ks[3 * HD0:4 * HD0, :], k[0, rows, :]).then_inc(done, 16)
            dma(ks[4 * HD0:6 * HD0, :], k[0:2, rows, :]).then_inc(done, 16)

        with nc.Block() as block:

            @block.sync
            def _(sp):
                def maxima(n, par):
                    for b in range(NB):
                        sp.wait_ge(m_sb, NB * n + b + 1)
                        for j in range(3):
                            dst = QS[par][b][STK + j:STK + j + 1, :].rearrange("o (q c) -> o q c", c=P)
                            src = mrow[b][j * NBLK:(j + 1) * NBLK, :]
                            sp.dma_start(dst, src).then_inc(m_in, 16)

                load(sp.dma_start, 0, 0, 0)
                load(sp.dma_start, 1, 0, 1)
                maxima(0, 0)

                def stage(n, par, it, more):
                    if more:
                        maxima(n + 1, 1 - par)
                    if it is not last_pair:
                        sp.wait_ge(pv_done, N_PV * (n + 1) + 4)
                        load(sp.dma_start, par, 0, n + 2)
                    for b in range(NB):
                        sp.wait_ge(o_sb, NB * n + b + 2)
                        for qc in range(4):
                            r = 32 * group(b, qc)
                            sp.dma_start(core.o_dram[b, bass.ds(n, 1), :, qc * T:(qc + 1) * T].rearrange("o f t -> (o f) t"),
                                         O[b][r:r + HD0, :]).then_inc(o_out, 16)
                            sp.dma_start(core.sum_dram[b, bass.ds(n, 1), qc * T:(qc + 1) * T],
                                         O[b][r + HD0:r + HD0 + 1, :]).then_inc(o_out, 16)

                stages(sp, stage)
                sp.wait_ge(o_out, N_OUT * ST + 1)

            @block.gpsimd
            def _(pool):
                load(pool.dma_start, 0, 1, 0)
                for b in range(NB):
                    nc.gpsimd.tensor_copy(VU[0][b][:], VV[:, b, :, 0, :]).then_inc(vu, 1)

                def stage(n, par, it, more):
                    if more:
                        pool.wait_ge(pv_done, N_PV * n + 4)
                        load(pool.dma_start, 1 - par, 1, n + 1)
                        for b in range(NB):
                            nc.gpsimd.tensor_copy(VU[1 - par][b][:], VV[:, b, :, bass.ds(n + 1, 1), :].rearrange("p k o f -> p k (o f)")).then_inc(vu, 1)

                stages(pool, stage)

            @block.vector
            def _(dve):
                for b in range(NB):
                    nc.vector.memset(mx[b][:], -3e38).then_inc(mx_set, 1)
                    nc.vector.memset(mparts[b][:], 0.0).then_inc(ones_set, 1)
                    for p in range(2):
                        nc.vector.memset(KS[p][b][96:AUG, :], 1.0).then_inc(ones_set, 1)
                dve.wait_ge(mx_set, NB)
                dve.wait_ge(ones_set, 3 * NB)
                dve.sem_inc(p1_read, 2)
                dve.sem_inc(o_out, 1)

                def row_maxima(b, n):
                    nc.vector.tensor_reduce(rowmax[b][:], mx[b][:], AX_X, ALU.max).then_inc(mx_s, 1)
                    dve.wait_ge(mx_s, NB * n + b + 1)
                    nc.vector.tensor_scalar(mparts[b][:, 0], rowmax[b][:], -1.0, None, ALU.mult).then_inc(part_s, 1)
                    dve.wait_ge(part_s, 3 * (NB * n + b) + 1)
                    nc.vector.scalar_tensor_tensor(rest[b][:], rowmax[b][:], -1.0, mparts[b][:, 0], ALU.mult, ALU.subtract).then_inc(neg_s, 1)
                    dve.wait_ge(neg_s, NB * n + b + 1)
                    nc.vector.tensor_copy(mparts[b][:, 1], rest[b][:]).then_inc(part_s, 1)
                    dve.wait_ge(part_s, 3 * (NB * n + b) + 2)
                    nc.vector.tensor_tensor(mparts[b][:, 2], rest[b][:], mparts[b][:, 1], ALU.subtract).then_inc(part_s, 1)

                def pass1(n):
                    for x, (b, q, j) in enumerate(P1):
                        dve.wait_ge(p1_ps, N_P1 * n + x + 1)
                        ps = PS[:, 6 + x % 2]
                        if q is None:
                            nc.vector.tensor_copy(mrow[b][:], ps.bitcast(BF16)[0:3 * NBLK, 0:P]).then_inc(m_sb, 1)
                            dve.wait_ge(m_sb, NB * n + b + 1)
                            dve.sem_inc(p1_read, 1)
                            continue
                        w = min(T, (q + 1) * P - j * T)
                        nc.vector.tensor_reduce(mx[b][:, q, j:j + 1], ps[:, 0:w], AX_X, ALU.max).then_inc(p1_read, 1)
                        if q == NBLK - 1 and j == 3:
                            dve.wait_ge(p1_read, N_P1 * n + x + 1 + 2)
                            row_maxima(b, n)

                pass1(0)

                def stage(n, par, it, more):
                    if more:
                        pass1(n + 1)
                    for b in range(NB):
                        dve.wait_ge(pv_done, N_PV * (n + 1) - NB + b + 1 + 4)
                        if b == 0:
                            dve.wait_ge(o_out, N_OUT * n + 1)
                        nc.vector.tensor_copy(O[b][:], PS[:, b]).then_inc(o_sb, 1)

                stages(dve, stage)

            @block.scalar
            def _(act):
                nc.scalar.preload_act_table_set("exp_and_others")
                act.sem_inc(exp_done, 2)

                def stage(n, par, it, more):
                    for kt in range(NBLK):
                        for b in range(NB):
                            act.wait_ge(pv_done, N_PV * n + 2 * kt + b + 1)
                            for g in p2_groups(kt):
                                x = G2[kt, b, g]
                                act.wait_ge(s_ps, N_S2 * n + x + 1)
                                lo = max(kt * P - 1024 * g, 0)
                                src = PS[:, 2 + 2 * (x % 2):4 + 2 * (x % 2)].rearrange("p a t -> p (a t)")
                                nc.scalar.activation(PT[b][kt % 2][:, 1024 * g + lo:1024 * (g + 1)], src[:, lo:1024],
                                                     ACT.Exp).then_inc(exp_done, 1)

                stages(act, stage)

            @block.tensor
            def _(pe):
                pe.sem_inc(pv_done, 4)
                pe.sem_inc(o_sb, 1)

                def pass1(n, par, x):
                    b, q, j = P1[x]
                    pe.wait_ge(p1_read, N_P1 * n + x + 1)
                    ps = PS[:, 6 + x % 2]
                    if q is None:
                        pe.wait_ge(part_s, 3 * (NB * n + b + 1))
                        nc.tensor.transpose(ps.bitcast(BF16)[:, 0:P], mparts[b][:].rearrange("p a q -> p (a q)"),
                                            core.identb[:]).then_inc(p1_ps, 1)
                        return
                    w = min(T, (q + 1) * P - j * T)
                    diag = j == q // 4
                    if diag:
                        nc.tensor.matmul(ps[:, w - P:w], core.lower[:], core.mask[:, ABOVE], start=True, stop=True)
                    nc.tensor.matmul(ps[:, 0:w], QS[par][b][0:STK, q * P:(q + 1) * P], KS[par][b][0:STK, j * T:j * T + w],
                                     start=not diag, stop=True, skip_group_check=diag).then_inc(p1_ps, 1)

                def pass2(n, par, kt, b, g):
                    x = G2[kt, b, g]
                    pe.wait_ge(exp_done, N_S2 * n + x + 1)
                    for qc in (2 * g, 2 * g + 1):
                        lo = max(kt * P, qc * T)
                        if lo >= (qc + 1) * T:
                            continue
                        ps = PS[:, 2 + 2 * (x % 2) + qc % 2]
                        diag = kt // 4 == qc
                        if diag:
                            nc.tensor.matmul(ps[:, lo - qc * T:lo - qc * T + P], core.lower[:], core.mask[:, BELOW],
                                             start=True, stop=True)
                        mm = nc.tensor.matmul(ps[:, lo - qc * T:T], KS[par][b][:, kt * P:(kt + 1) * P],
                                              QS[par][b][:, lo:(qc + 1) * T], start=not diag, stop=True,
                                              skip_group_check=diag)
                    mm.then_inc(s_ps, 1)

                def pv(n, par, kt):
                    for b in range(NB):
                        pe.wait_ge(exp_done, N_S2 * n + G2[kt, b, 1] + 1 + 2)
                        if kt == 0:
                            pe.wait_ge(o_sb, NB * n + 1)
                        for qc in range(kt // 4, 4):
                            lo = max(kt * P, qc * T)
                            r = 32 * group(b, qc)
                            mm = nc.tensor.matmul(PS[r:r + HD0 + 1, b, lo - qc * T:T], VU[par][b][:, kt],
                                                  PT[b][kt % 2][:, lo:(qc + 1) * T], start=(kt == 0), stop=(kt >= 4 * qc),
                                                  skip_group_check=(kt > 4 * qc))
                        mm.then_inc(pv_done, 1)

                for b in range(NB):
                    pe.wait_ge(stack_in[0][b], N_IN)
                pe.wait_ge(ones_set, 3 * NB)
                for x in range(N_P1):
                    pass1(0, 0, x)

                def stage(n, par, it, more):
                    pe.wait_ge(m_in, 16 * 3 * NB * (n + 1))
                    pe.wait_ge(vu, NB * (n + 1))
                    for what, key in order(more):
                        if what == "s":
                            pass2(n, par, *key)
                        elif what == "o":
                            pv(n, par, key)
                        else:
                            b = P1[key][0]
                            if key in (0, P1.index((1, 0, 0))):
                                pe.wait_ge(stack_in[1 - par][b], N_IN * (it + 1 + par))
                            pass1(n + 1, 1 - par, key)

                stages(pe, stage)


def attn0_out(core):
    nc, io, PS, X = core.nc, core.io, core.PS, core.X
    w_in, sums_in, recip, recip_out, gbo_s, o_ready, o_ps, o_sb, x_done = (
        core.sem("a0o_" + n) for n in "w_in sums_in recip recip_out gbo normed o_ps o_sb x_done".split())
    tile_in = [core.sem(f"a0o_tile_in{b}") for b in range(NB)]
    with ExitStack() as st:
        sb = lambda n, sh, d=F32: st.enter_context(nc.sbuf_tensor("a0o_" + n, sh, d))
        wo, bv, bo, gbo = sb("wo", [P, DC, D]), sb("bv", [P, DC]), sb("bo", [P, DC]), sb("gbo", [P, DC, NB])
        sums = sb("sums", [P, NB * NH0 * S // P])
        o = [sb(f"o{b}", [P, DC, T]) for b in range(NB)]
        r = [sb(f"r{b}", [P, DC, T]) for b in range(NB)]
        y = [sb(f"y{b}", [P, DC, T]) for b in range(NB)]
        with nc.Block() as block:

            @block.sync
            def _(sp):
                sp.dma_start(sums[:], core.sum_dram.rearrange("b h (a t) -> (b h a) t", a=4)).then_inc(sums_in, 16)
                sp.dma_start(wo[:], io["woT"].rearrange("(k p) o -> p k o", p=P)).then_inc(w_in, 16)
                sp.dma_start(bv[:], io["bv"]).then_inc(w_in, 16)
                sp.dma_start(bo[:], io["bo"]).then_inc(w_in, 16)
                sp.wait_ge(recip, 1)
                sp.dma_start(core.recip_dram.rearrange("b h (a t) -> (b h a) t", a=4), sums[:]).then_inc(recip_out, 16)
                sp.wait_ge(recip_out, 16)
                with sp.Fori(0, TPB) as i:
                    for b in range(NB):
                        sp.wait_ge(o_ps, NB * i + b + 1)
                        for c in range(DC):
                            sp.dma_start(o[b][:, c], core.o_dram[b, c * HPC:(c + 1) * HPC].rearrange("h f s -> (h f) s")[:, bass.ds(i * T, T)]
                                         ).then_inc(tile_in[b], 16)
                            src = core.recip_dram[b, c * HPC:(c + 1) * HPC, bass.ds(i * T, T)].unsqueeze(1).broadcast_to([HPC, HD0, T])
                            sp.dma_start(r[b][:, c], src).then_inc(tile_in[b], 16)

            @block.vector
            def _(dve):
                dve.wait_ge(sums_in, 16)
                nc.vector.reciprocal(sums[:], sums[:]).then_inc(recip, 1)
                dve.wait_ge(w_in, 48)
                for b in range(NB):
                    nc.vector.tensor_tensor(gbo[:, :, b], core.mod[:, 0, GA, :, b], bo[:], ALU.mult).then_inc(gbo_s, 1)
                with dve.Fori(0, TPB) as i:
                    for b in range(NB):
                        dve.wait_ge(tile_in[b], 64 * (i + 1))
                        nc.vector.tensor_tensor(o[b][:], o[b][:], r[b][:], ALU.mult).then_inc(o_ready, 1)
                        dve.wait_ge(o_ready, 2 * (NB * i + b) + 1)
                        for c in range(DC):
                            op = nc.vector.tensor_scalar(o[b][:, c], o[b][:, c], bv[:, c:c + 1], None, ALU.add)
                        op.then_inc(o_ready, 1)
                    for b in range(NB):
                        dve.wait_ge(o_sb, NB * i + b + 2)
                        nc.vector.tensor_tensor(X[:, :, tok(b, i)], X[:, :, tok(b, i)], y[b][:], ALU.add).then_inc(x_done, 1)

            @block.tensor
            def _(pe):
                pe.sem_inc(o_ps, NB)
                pe.wait_ge(w_in, 48)
                pe.sem_inc(o_sb, 1)
                with pe.Fori(0, TPB) as i:
                    for b in range(NB):
                        pe.wait_ge(o_ready, 2 * (NB * i + b + 1))
                        pe.wait_ge(o_sb, NB * i + 1)
                        for c in range(DC):
                            for k in range(DC):
                                mm = nc.tensor.matmul(PS[:, 2 * b + c], wo[:, k, c * P:(c + 1) * P], o[b][:, k],
                                                      start=(k == 0), stop=(k == DC - 1))
                        mm.then_inc(o_ps, 1)

            @block.scalar
            def _(act):
                act.wait_ge(gbo_s, NB)
                act.sem_inc(x_done, 1)
                with act.Fori(0, TPB) as i:
                    for b in range(NB):
                        act.wait_ge(o_ps, NB * i + b + 1 + NB)
                        act.wait_ge(x_done, NB * i + 1)
                        for c in range(DC):
                            op = nc.scalar.activation(y[b][:, c], PS[:, 2 * b + c], ACT.Identity,
                                                      bias=gbo[:, c, b:b + 1], scale=core.mod[:, 0, GA, c, b:b + 1])
                        op.then_inc(o_sb, 1)



FH = 1024
FC = FH // P


def ffn0(core, H):
    nc, io, PS, X = core.nc, core.io, core.PS, core.X
    in_w12, in_s, scales, pair_ps, tanh_s, half_s, gate_s, h1_ps, h1_s, h2_ps, h2_s, w3_ps, x_done = (
        core.sem("f0_" + n) for n in
        "in_w12 in_s scales pair_ps tanh half gate h1_ps h1 h2_ps h2 w3_ps x_done".split())
    in_h1, in_h2, in_w3 = (core.sem("f0_in_" + n) for n in ("h1", "h2", "w3"))
    with ExitStack() as st:
        sb = lambda n, sh, d=F32: st.enter_context(nc.sbuf_tensor("f0_" + n, sh, d))
        w1, w2 = sb("w1", [P, DC, FH]), sb("w2", [P, DC, FH])
        h1, h2 = sb("h1", [P, FC, FH]), sb("h2", [P, FC, FH])
        w3 = sb("w3", [P, FC, D])
        s1, s2, sh1, sh2 = (sb(n, [P, FC]) for n in ("s1", "s2", "sh1", "sh2"))
        s3 = sb("s3", [P, DC])
        s1h, s12 = sb("s1h", [P, FC]), sb("s12", [P, FC])
        g3 = sb("g3", [P, DC, NB])
        hA, hB = sb("hA", [P, FC, T]), sb("hB", [P, FC, T])
        th = [sb(f"th{k}", [P, T]) for k in range(2)]
        hf = [sb(f"hf{k}", [P, T]) for k in range(2)]
        with nc.Block() as block:

            @block.sync
            def _(sp):
                for t, name in ((w1, "w1T"), (w2, "w2T")):
                    sp.dma_start(t[:], io[name].rearrange("(k p) o -> p k o", p=P)).then_inc(in_w12, 16)
                for t, name in ((s1, "w1s"), (s2, "w2s"), (sh1, "h1s"), (sh2, "h2s"), (s3, "w3s")):
                    sp.dma_start(t[:], io[name]).then_inc(in_s, 16)
                for t, name, ready in ((h1, "h1T", in_h1), (h2, "h2T", in_h2), (w3, "w3T", in_w3)):
                    sp.dma_start(t[:], io[name].rearrange("(k p) o -> p k o", p=P)).then_inc(ready, 16)

            @block.tensor
            def _(pe):
                def dense(bank, w, x, o, n_k, done):
                    for k in range(n_k):
                        mm = nc.tensor.matmul(PS[:, bank], w[:, k, o * P:(o + 1) * P], x[:, k], start=(k == 0), stop=(k == n_k - 1))
                    mm.then_inc(done, 1)

                pe.wait_ge(in_w12, 32)
                pe.sem_inc(x_done, 1)
                with pe.Fori(0, TPB) as i:
                    for b in range(NB):
                        u = NB * i + b
                        h = H[:, :, tok(b, i)]
                        for o in range(FC):
                            if o >= 2:
                                pe.wait_ge(gate_s, FC * u + o - 1)
                            dense(2 * (o % 2), w1, h, o, DC, pair_ps)
                            dense(2 * (o % 2) + 1, w2, h, o, DC, pair_ps)
                        pe.wait_ge(gate_s, FC * (u + 1))
                        pe.wait_ge(in_h1, 16)
                        pe.wait_ge(x_done, u + 1)
                        for o in range(FC):
                            if o >= 2:
                                pe.wait_ge(h1_s, FC * u + o - 1)
                            dense(4 + o % 2, h1, hA, o, FC, h1_ps)
                        pe.wait_ge(h1_s, FC * (u + 1))
                        pe.wait_ge(in_h2, 16)
                        for o in range(FC):
                            if o >= 2:
                                pe.wait_ge(h2_s, FC * u + o - 1)
                            dense(6 + o % 2, h2, hB, o, FC, h2_ps)
                        pe.wait_ge(h2_s, FC * (u + 1))
                        pe.wait_ge(in_w3, 16)
                        for o in range(DC):
                            dense(4 + o, w3, hA, o, FC, w3_ps)

            @block.scalar
            def _(act):
                nc.scalar.preload_act_table_set("gelu_and_others")
                act.wait_ge(scales, 1)
                with act.Fori(0, TPB) as i:
                    for b in range(NB):
                        u = NB * i + b
                        for o in range(FC):
                            act.wait_ge(pair_ps, 2 * (FC * u + o) + 1)
                            nc.scalar.activation(th[o % 2][:], PS[:, 2 * (o % 2)], ACT.Tanh, scale=s1h[:, o:o + 1]).then_inc(tanh_s, 1)
                        for o in range(FC):
                            act.wait_ge(h1_ps, FC * u + o + 1)
                            nc.scalar.activation(hB[:, o], PS[:, 4 + o % 2], ACT.Gelu, scale=sh1[:, o:o + 1]).then_inc(h1_s, 1)
                        for o in range(FC):
                            act.wait_ge(h2_ps, FC * u + o + 1)
                            nc.scalar.activation(hA[:, o], PS[:, 6 + o % 2], ACT.Gelu, scale=sh2[:, o:o + 1]).then_inc(h2_s, 1)

            @block.vector
            def _(dve):
                dve.wait_ge(in_s, 16 * 5)
                for b in range(NB):
                    nc.vector.tensor_tensor(g3[:, :, b], core.mod[:, 0, GB, :, b], s3[:], ALU.mult)
                nc.vector.scalar_tensor_tensor(s12[:], s1[:], 0.5, s2[:], ALU.mult, ALU.mult)
                nc.vector.tensor_scalar(s1h[:], s1[:], 0.5, None, ALU.mult).then_inc(scales, 1)
                with dve.Fori(0, TPB) as i:
                    for b in range(NB):
                        u = NB * i + b
                        for o in range(FC):
                            dve.wait_ge(tanh_s, FC * u + o + 1)
                            g1, g2 = PS[:, 2 * (o % 2)], PS[:, 2 * (o % 2) + 1]
                            nc.vector.scalar_tensor_tensor(hf[o % 2][:], th[o % 2][:], 1.0, g1, ALU.add, ALU.mult).then_inc(half_s, 1)
                            dve.wait_ge(half_s, FC * u + o + 1)
                            dve.wait_ge(pair_ps, 2 * (FC * u + o + 1))
                            nc.vector.scalar_tensor_tensor(hA[:, o], hf[o % 2][:], s12[:, o:o + 1], g2, ALU.mult, ALU.mult).then_inc(gate_s, 1)
                        dve.wait_ge(w3_ps, DC * (u + 1))
                        for c in range(DC):
                            op = nc.vector.scalar_tensor_tensor(X[:, c, tok(b, i)], PS[:, 4 + c], g3[:, c, b:b + 1],
                                                                X[:, c, tok(b, i)], ALU.mult, ALU.add)
                        op.then_inc(x_done, 1)



NT = 1024
FO = 64
UC = 3 * D // P
BS = 64
NJ = S // BS
OW = 256
NI = S // OW
BPO = OW // BS
PAIRS = 4
LAG0 = -(BPO - 1)
LAG1 = NT // BS
LAGS = range(LAG0, LAG1 + 1)
JPAD = LAG1
HW = (len(LAGS) - 1) * BS + OW
KOFF = -LAG0 * BS + BS
KW = BS + HW
TWO_PI = 2.0 * np.pi
PI2_HI = float(np.float32(6.28125))
PI2_LO = float(TWO_PI - 6.28125)
ROUND = 1.5 * 2.0 ** 23
PI_IN = float(np.nextafter(np.float32(np.pi), np.float32(0)))


def filter_taps(core):
    nc, io, PS = core.nc, core.io, core.PS
    w_in, zeroed, ps_done, arg_s, sin_s, tap_ps, taps_s, out_s = (
        core.sem("ft_" + n) for n in "w_in zeroed ps arg sin tap_ps taps out".split())
    with ExitStack() as st:
        sb = lambda n, sh, d=F32: st.enter_context(nc.sbuf_tensor("ft_" + n, sh, d))
        z = sb("z", [3, NT])
        w = [sb("w1", [3, FO]), sb("w2", [FO, FO]), sb("w3", [FO, FO])]
        bf = sb("bf", [FO, 3, 2])
        wout = sb("wout", [FO, D])
        decay = sb("decay", [P, DC, NT])
        arg, turns, h = sb("arg", [FO, NT]), sb("turns", [FO, NT]), sb("h", [FO, NT])
        taps = sb("taps", [P, DC, KW])
        NH = NT // 512
        with nc.Block() as block:

            @block.sync
            def _(sp):
                loads = [(z[:], io["f_z"]), (bf[:], io["f_bf"]), (wout[:], io["f_wout"]),
                         (decay[:], io["f_decay"].rearrange("(c p) t -> p c t", p=P))]
                loads += [(w[k][:], io[f"f_w{k + 1}"]) for k in range(3)]
                for dst, src in loads:
                    sp.dma_start(dst, src).then_inc(w_in, 16)
                sp.wait_ge(taps_s, DC * NH)
                sp.wait_ge(zeroed, 1)
                sp.dma_start(core.kpad.rearrange("(c p) w -> p c w", p=P), taps[:]).then_inc(out_s, 16)
                sp.wait_ge(out_s, 16)

            @block.gpsimd
            def _(pool):
                nc.gpsimd.memset(taps[:], 0.0).then_inc(zeroed, 1)

            @block.tensor
            def _(pe):
                pe.wait_ge(w_in, 16 * 7)
                for layer in range(3):
                    x = z if layer == 0 else h
                    if layer:
                        pe.wait_ge(sin_s, layer)
                    for n in range(NH):
                        mm = nc.tensor.matmul(PS[0:FO, n], w[layer][:], x[:, n * 512:(n + 1) * 512], start=True, stop=True)
                    mm.then_inc(ps_done, 1)
                pe.wait_ge(sin_s, 3)
                for c in range(DC):
                    for n in range(NH):
                        mm = nc.tensor.matmul(PS[:, 2 + NH * c + n], wout[:, c * P:(c + 1) * P], h[:, n * 512:(n + 1) * 512],
                                              start=True, stop=True)
                mm.then_inc(tap_ps, 1)

            @block.vector
            def _(dve):
                dve.wait_ge(w_in, 16 * 7)
                n = 0

                def then(op):
                    nonlocal n
                    n += 1
                    op.then_inc(arg_s, 1)
                    dve.wait_ge(arg_s, n)

                for layer in range(3):
                    dve.wait_ge(ps_done, layer + 1)
                    ps = PS[0:FO, 0:NH].rearrange("p a t -> p (a t)")
                    then(nc.vector.tensor_scalar(arg[:], ps, bf[:, layer, 0:1], bf[:, layer, 1:2], ALU.add, ALU.mult))
                    then(nc.vector.tensor_scalar(turns[:], arg[:], 1.0 / TWO_PI, ROUND, ALU.mult, ALU.add))
                    then(nc.vector.tensor_scalar(turns[:], turns[:], ROUND, None, ALU.subtract))
                    then(nc.vector.scalar_tensor_tensor(arg[:], turns[:], -PI2_HI, arg[:], ALU.mult, ALU.add))
                    then(nc.vector.scalar_tensor_tensor(arg[:], turns[:], -PI2_LO, arg[:], ALU.mult, ALU.add))
                    then(nc.vector.tensor_scalar(arg[:], arg[:], PI_IN, -PI_IN, ALU.min, ALU.max))
                dve.wait_ge(tap_ps, 1)
                dve.wait_ge(zeroed, 1)
                for c in range(DC):
                    for k in range(NH):
                        at = slice(KOFF + k * 512, KOFF + (k + 1) * 512)
                        nc.vector.tensor_tensor(taps[:, c, at], PS[:, 2 + NH * c + k], decay[:, c, k * 512:(k + 1) * 512],
                                                ALU.mult).then_inc(taps_s, 1)

            @block.scalar
            def _(act):
                for layer in range(3):
                    act.wait_ge(arg_s, 6 * (layer + 1))
                    nc.scalar.activation(h[:], arg[:], ACT.Sin).then_inc(sin_s, 1)


def backwards(ap, start, n):
    return bass.AP(ap.tensor, ap.offset + start + n - 1, [list(ap.ap[0]), [-1, n]])


def conv_inputs(core, H, V, X0, RR):
    nc, io, PS = core.nc, core.io, core.PS
    w_in, zeroed, pj_ps, pj_sb, tap_s, uc_s, v_s, tr_ps, rr_s, hist, v_free, turned = (
        core.sem("ci_" + n) for n in "w_in zeroed pj_ps pj_sb tap uc v tr_ps rr hist v_free turned".split())
    with ExitStack() as st:
        sb = lambda n, sh, d=F32: st.enter_context(nc.sbuf_tensor("ci_" + n, sh, d))
        wi = sb("wi", [P, DC, 3 * D])
        bi, fb, fw = sb("bi", [P, UC]), sb("fb", [P, UC]), sb("fw", [P, UC, 3])
        U = [sb(f"U{b}", [P, UC, 2 + T]) for b in range(NB)]
        C = sb("C", [P, T])
        X1 = sb("X1", [P, DC, T])
        Vt = [sb(f"Vt{b}", [P, DC, T]) for b in range(NB)]
        NTR = DC * T // BS // 4

        with nc.Block() as block:

            @block.sync
            def _(sp):
                sp.dma_start(wi[:], io["h_win"].rearrange("(k p) o -> p k o", p=P)).then_inc(w_in, 16)
                for t, name in ((bi, "h_bin"), (fb, "h_sfb"), (fw, "h_sfw")):
                    sp.dma_start(t[:], io[name]).then_inc(w_in, 16)

            @block.tensor
            def _(pe):
                pe.sem_inc(pj_sb, 1)
                def project(i, b, u):
                    for o in range(UC):
                        pe.wait_ge(pj_sb, UC * u + 1)
                        for k in range(DC):
                            mm = nc.tensor.matmul(PS[:, o], wi[:, k, o * P:(o + 1) * P], H[:, k, tok(b, i)],
                                                  start=(k == 0), stop=(k == DC - 1))
                        mm.then_inc(pj_ps, 1)

                def turn(b, u):
                    pe.wait_ge(v_s, DC * (u + 1))
                    for n in range(NTR):
                        pe.wait_ge(rr_s, NTR * u + n + 1)
                        pe.sem_inc(core.tick, 1)
                        for j in range(4):
                            c, blk = divmod(4 * n + j, T // BS)
                            mm = nc.tensor.transpose(PS[0:BS, 6 + n % 2, j * P:(j + 1) * P],
                                                     Vt[b][:, c, T - (blk + 1) * BS:T - blk * BS], core.ident[:])
                        mm.then_inc(tr_ps, 1)
                    pe.wait_ge(tr_ps, NTR * (u + 1))
                    pe.sem_inc(turned, NTR)

                pe.sem_inc(rr_s, 2)
                pe.sem_inc(turned, NTR * NB)
                pe.wait_ge(w_in, 64)
                project(0, 0, 0)
                with pe.Fori(0, TPB - 1) as i:
                    project(i, 1, NB * i + 1)
                    turn(0, NB * i)
                    project(i + 1, 0, NB * i + 2)
                    turn(1, NB * i + 1)
                last = TPB - 1
                project(last, 1, NB * last + 1)
                turn(0, NB * last)
                turn(1, NB * last + 1)

            @block.scalar
            def _(act):
                act.wait_ge(w_in, 64)
                act.wait_ge(zeroed, 1)

                def take(i, b, u):
                    act.wait_ge(hist, u + 1)
                    for o in range(UC):
                        act.wait_ge(pj_ps, UC * u + o + 1)
                        nc.scalar.activation(U[b][:, o, 2:2 + T], PS[:, o], ACT.Identity, bias=bi[:, o:o + 1]).then_inc(pj_sb, 1)

                def spread(i, b, u):
                    for n in range(NTR):
                        act.wait_ge(tr_ps, NTR * u + n + 1)
                        c, blk = divmod(4 * n, T // BS)
                        for half in range(2):
                            src = PS[0:BS, 6 + n % 2].rearrange("p (r d two) -> p d r two", r=BPO, two=2)[:, :, :, half]
                            dst = RR[half * BS:(half + 1) * BS, c * 64:(c + 1) * 64, :, bass.ds(i * (T // OW) + blk // BPO, 1), b]
                            dst = dst.rearrange("p d r o -> p d (r o)")
                            op = nc.scalar.copy(dst, src)
                        op.then_inc(rr_s, 1)

                take(0, 0, 0)
                with act.Fori(0, TPB - 1) as i:
                    take(i, 1, NB * i + 1)
                    spread(i, 0, NB * i)
                    take(i + 1, 0, NB * i + 2)
                    spread(i, 1, NB * i + 1)
                last = TPB - 1
                take(last, 1, NB * last + 1)
                spread(last, 0, NB * last)
                spread(last, 1, NB * last + 1)

            @block.vector
            def _(dve):
                dve.wait_ge(w_in, 64)
                for b in range(NB):
                    op = nc.vector.memset(U[b][:, :, 0:2], 0.0)
                op.then_inc(zeroed, 1)
                dve.wait_ge(zeroed, 1)
                dve.sem_inc(hist, NB)
                with dve.Fori(0, TPB) as i:
                    for b in range(NB):
                        u = NB * i + b
                        for n, o in enumerate((2, 3, 4, 5, 0, 1)):
                            dve.wait_ge(pj_sb, UC * u + o + 2)
                            c = o % DC
                            a = C[:]
                            at = 2 * (UC * u + n)
                            dve.wait_ge(uc_s, UC * u + n)
                            if n >= 3:
                                dve.wait_ge(v_s, DC * u + min(n - 2, DC))
                            nc.vector.tensor_scalar(a, U[b][:, o, 2:2 + T], fw[:, o, 2:3], fb[:, o:o + 1], ALU.mult, ALU.add).then_inc(tap_s, 1)
                            dve.wait_ge(tap_s, at + 1)
                            nc.vector.scalar_tensor_tensor(a, U[b][:, o, 1:1 + T], fw[:, o, 1:2], a, ALU.mult, ALU.add).then_inc(tap_s, 1)
                            dve.wait_ge(tap_s, at + 2)
                            dst = X0[:, c, tok(b, i)] if o < DC else X1[:, c] if o < 2 * DC else a
                            nc.vector.scalar_tensor_tensor(dst, U[b][:, o, 0:T], fw[:, o, 0:1], a, ALU.mult, ALU.add).then_inc(uc_s, 1)
                            if o >= 2 * DC:
                                dve.wait_ge(uc_s, UC * u + n + 1)
                                if c == 0:
                                    dve.wait_ge(v_free, u + 1)
                                    dve.wait_ge(turned, NTR * (u + 1))
                                nc.vector.tensor_tensor(backwards(Vt[b][:, c], 0, T), a, X1[:, c], ALU.mult).then_inc(v_s, 1)
                        dve.wait_ge(uc_s, UC * (u + 1))
                        nc.vector.tensor_copy(U[b][:, :, 0:2], U[b][:, :, T:T + 2]).then_inc(hist, 1)

            @block.gpsimd
            def _(pool):
                pool.sem_inc(v_free, NB)
                with pool.Fori(0, TPB) as i:
                    for b in range(NB):
                        pool.wait_ge(v_s, DC * (NB * i + b + 1))
                        pool.sem_inc(core.tick, 1)
                        for c in range(DC):
                            op = nc.gpsimd.tensor_copy(V[:, c, tok(b, i)], backwards(Vt[b][:, c], 0, T))
                        op.then_inc(v_free, 1)


def long_conv(core, RR):
    nc, PS = core.nc, core.PS
    zeroed, spread_s, y_ps, y_sb, y_done = (core.sem("lc_" + n) for n in "zeroed spread y_ps y_sb all".split())
    strip_in = [core.sem(f"lc_strip_in{k}") for k in range(2)]
    y_out = [core.sem(f"lc_y_out{k}") for k in range(2)]
    G = D // (2 * PAIRS)
    with ExitStack() as st:
        sb = lambda n, sh, d=F32: st.enter_context(nc.sbuf_tensor("lc_" + n, sh, d))
        strip = [sb(f"strip{k}", [P, PAIRS, HW]) for k in range(2)]
        blocks = [sb(f"blocks{k}", [P, PAIRS, BPO, (JPAD + NJ) // BPO, 2, NB]) for k in range(2)]
        Y = [sb(f"Y{k}", [P, OW]) for k in range(2)]
        with nc.Block() as block:

            @block.sync
            def _(sp):
                with sp.Fori(0, G // 2) as i:
                    for k in range(2):
                        g = 2 * i + k
                        sp.wait_ge(y_ps, g + 1)
                        for j in range(PAIRS):
                            src = bass.AP(core.kpad.tensor, (g * PAIRS + j) * 2 * KW + 1, [[KW, 2], [1, BS], [1, HW]])
                            sp.dma_start(strip[k][:, j], src).then_inc(strip_in[k], 16)

            @block.vector
            def _(dve):
                for k in range(2):
                    op = nc.vector.memset(blocks[k][:], 0.0)
                op.then_inc(zeroed, 1)
                dve.wait_ge(zeroed, 1)
                with dve.Fori(0, G // 2) as i:
                    for k in range(2):
                        g = 2 * i + k
                        dve.wait_ge(y_ps, g + 1)
                        for half in range(2):
                            rows = slice(half * BS, (half + 1) * BS)
                            for b in range(NB):
                                op = nc.vector.tensor_copy(blocks[k][rows, :, :, JPAD // BPO:, half, b],
                                                           RR[rows, bass.ds(g * PAIRS, PAIRS), :, :, b])
                        op.then_inc(spread_s, 1)

            @block.tensor
            def _(pe):
                pe.sem_inc(y_ps, 2)
                pe.sem_inc(y_sb, 1)
                with pe.Fori(0, G // 2) as i:
                    for k in range(2):
                        g = 2 * i + k
                        pe.wait_ge(spread_s, g + 1)
                        pe.wait_ge(strip_in[k], 16 * PAIRS * (i + 1))
                        pe.wait_ge(y_sb, g + 1)
                        for lag in LAGS:
                            for j in range(PAIRS):
                                q, r = divmod(JPAD - lag, BPO)
                                lhsT = blocks[k][:, j, r, q:q + NI].rearrange("p q c b -> p (q c b)")
                                mm = nc.tensor.matmul(PS[32 * j:32 * j + 32, k, 0:OW], lhsT,
                                                      strip[k][:, j, (lag - LAG0) * BS:(lag - LAG0) * BS + OW],
                                                      start=(lag == LAG0), stop=(lag == LAG1))
                        mm.then_inc(y_ps, 1)

            @block.scalar
            def _(act):
                for k in range(2):
                    act.sem_inc(y_out[k], 16)
                with act.Fori(0, G // 2) as i:
                    for k in range(2):
                        g = 2 * i + k
                        act.wait_ge(y_ps, g + 1 + 2)
                        act.wait_ge(y_out[k], 16 * (i + 1))
                        nc.scalar.copy(Y[k][:], PS[:, k, 0:OW]).then_inc(y_sb, 1)
                        act.wait_ge(y_sb, g + 2)
                        act.dma_start(core.y_dram[bass.ds(g * P, P)], Y[k][:]).then_inc(y_out[k], 16)
                for k in range(2):
                    act.wait_ge(y_out[k], 16 * (G // 2 + 1))


def conv_out(core, V, X0):
    nc, io, PS, X = core.nc, core.io, core.PS, core.X
    w_in, gbo_s, z_s, o_ps, o_sb, x_done = (core.sem("co_" + n) for n in "w_in gbo z o_ps o_sb x_done".split())
    y_in = [core.sem(f"co_y_in{b}") for b in range(NB)]
    y_view = core.y_dram.rearrange("(pr i ch b) t -> pr ch i b t", b=NB, i=NI, ch=2)
    with ExitStack() as st:
        sb = lambda n, sh, d=F32: st.enter_context(nc.sbuf_tensor("co_" + n, sh, d))
        wo, bo, gbo, fb = sb("wo", [P, DC, D]), sb("bo", [P, DC]), sb("gbo", [P, DC, NB]), sb("fb", [P, DC])
        z = [sb(f"z{b}", [P, DC, T]) for b in range(NB)]
        y = [sb(f"y{b}", [P, DC, T]) for b in range(NB)]
        with nc.Block() as block:

            @block.sync
            def _(sp):
                sp.dma_start(wo[:], io["h_wout"].rearrange("(k p) o -> p k o", p=P)).then_inc(w_in, 16)
                sp.dma_start(bo[:], io["h_bout"]).then_inc(w_in, 16)
                sp.dma_start(fb[:], io["h_fb"]).then_inc(w_in, 16)
                with sp.Fori(0, TPB) as i:
                    for b in range(NB):
                        sp.wait_ge(o_ps, NB * i + b + 1)
                        for c in range(DC):
                            for k in range(T // OW):
                                src = y_view[c * P // 2:(c + 1) * P // 2, :, bass.ds(i * (T // OW) + k, 1), b]
                                sp.dma_start(z[b][:, c, k * OW:(k + 1) * OW], src.rearrange("pr ch o t -> pr ch (o t)")).then_inc(y_in[b], 16)

            @block.vector
            def _(dve):
                dve.wait_ge(w_in, 48)
                for b in range(NB):
                    nc.vector.tensor_tensor(gbo[:, :, b], core.mod[:, 1, GA, :, b], bo[:], ALU.mult).then_inc(gbo_s, 1)
                with dve.Fori(0, TPB) as i:
                    for b in range(NB):
                        dve.wait_ge(y_in[b], 16 * DC * T // OW * (i + 1))
                        for c in range(DC):
                            op = nc.vector.scalar_tensor_tensor(z[b][:, c], V[:, c, tok(b, i)], fb[:, c:c + 1], z[b][:, c],
                                                                ALU.mult, ALU.add)
                        op.then_inc(z_s, 1)
                        dve.wait_ge(z_s, 2 * (NB * i + b) + 1)
                        nc.vector.tensor_tensor(z[b][:], z[b][:], X0[:, :, tok(b, i)], ALU.mult).then_inc(z_s, 1)
                    for b in range(NB):
                        dve.wait_ge(o_sb, NB * i + b + 2)
                        nc.vector.tensor_tensor(X[:, :, tok(b, i)], X[:, :, tok(b, i)], y[b][:], ALU.add).then_inc(x_done, 1)

            @block.tensor
            def _(pe):
                pe.sem_inc(o_ps, NB)
                pe.wait_ge(w_in, 48)
                pe.sem_inc(o_sb, 1)
                with pe.Fori(0, TPB) as i:
                    for b in range(NB):
                        pe.wait_ge(z_s, 2 * (NB * i + b + 1))
                        pe.wait_ge(o_sb, NB * i + 1)
                        for c in range(DC):
                            for k in range(DC):
                                mm = nc.tensor.matmul(PS[:, 2 * b + c], wo[:, k, c * P:(c + 1) * P], z[b][:, k],
                                                      start=(k == 0), stop=(k == DC - 1))
                        mm.then_inc(o_ps, 1)

            @block.scalar
            def _(act):
                act.wait_ge(gbo_s, NB)
                act.sem_inc(x_done, 1)
                with act.Fori(0, TPB) as i:
                    for b in range(NB):
                        act.wait_ge(o_ps, NB * i + b + 1 + NB)
                        act.wait_ge(x_done, NB * i + 1)
                        for c in range(DC):
                            op = nc.scalar.activation(y[b][:, c], PS[:, 2 * b + c], ACT.Identity,
                                                      bias=gbo[:, c, b:b + 1], scale=core.mod[:, 1, GA, c, b:b + 1])
                        op.then_inc(o_sb, 1)



NH1 = 8
HD1 = 64
INNER = NH1 * HD1
IC = INNER // P
WPT = T // P
HID = 682
HCS = [min(P, HID - o) for o in range(0, HID, P)]
HC = len(HCS)
NORM2_MIN = 1e-24
LN_SCALE = 2.0 ** 20


def shifted(Y, c, b, i):
    return Y[:, c, b, bass.ds(i * T + (0 if c else 1), T)]


def plain(Y, c, b, i):
    return Y[:, c, b, bass.ds(i * T + 1, T)]


QK = 2 * IC
UNITS = WPT * NH1 // 2
TR_LAG, OUT_LAG = 3, 5
SLOTS = UNITS - 1 + OUT_LAG
V_PIECE = QK + 2
PIECES = V_PIECE + WPT
PIECE_SLOT = (0, 1, 3, 5, 7, 8, 10, 12, 14, 15, 16, 17, 18, 19)


def attn1(core, layer, Y, Yn):
    nc, io, PS = core.nc, core.io, core.PS
    tag = f"a1{layer}_"
    w_in, tab_in, hs, pj_ps, raw_s, sqr_s, kss_ps, qss_ps, t1_s, t2_s, kmax, klog, krn, ksum, roped, qmax, qlog, rq_s = (
        core.sem(tag + n) for n in
        "w_in tab_in hs pj_ps raw sqr kss_ps qss_ps t1 t2 kmax klog krn ksum roped qmax qlog rq".split())
    v_ps, v_sb, hist, s_ps, mx_s, nb_s, exp_s, rsum_s, norm_s, tr_ps, pt_s, pv_ps, o_sb, wo_ps, y_done = (
        core.sem(tag + n) for n in
        "v_ps v_sb hist s_ps mx nb exp rsum norm tr_ps pt pv_ps o_sb wo_ps y_done".split())
    swapped_in = [core.sem(tag + f"swapped{k}") for k in range(2)]
    n_w = DC + 4
    SC, TR, OB, PJ, V2, SS = (0, 1), (2, 3), 4, 5, 6, 7
    with ExitStack() as st:
        sb = lambda n, sh, d=F32: st.enter_context(nc.sbuf_tensor(tag + n, sh, d))
        wqkv = sb("wqkv", [P, DC, 3 * INNER])
        wo = sb("wo", [P, IC, D])
        sc = sb("sc", [P, 2, 2])
        pairsum = sb("pairsum", [P, P])
        headsum = sb("headsum", [P, 2])
        tab = sb("tab", [P, 4, T])
        Hs = sb("Hs", [P, DC, T])
        raw = [sb(f"raw{k}", [P, T]) for k in range(2)]
        swapped = [sb(f"swapped{k}", [P, T]) for k in range(2)]
        sqr = [sb(f"sqr{k}", [P, T]) for k in range(2)]
        t1, t2, kn = sb("t1", [P, T]), sb("t2", [P, T]), sb("kn", [P, T])
        rn = [sb(f"rn{k}", [P, T]) for k in range(2)]
        QT = [sb(f"QT{b}", [P, IC, T]) for b in range(NB)]
        KT = [sb(f"KT{b}", [P, IC, P + T]) for b in range(NB)]
        V = [sb(f"V{b}", [P, 1 + WPT, INNER]) for b in range(NB)]
        rq = [sb(f"rq{b}", [P, WPT, NH1]) for b in range(NB)]
        mx, nb, sums, rsum = (sb(n, [P, WPT, NH1]) for n in ("mx", "nb", "sums", "rsum"))
        Pb = [sb(f"P{k}", [P, 2, 2 * P]) for k in range(4)]
        PTb = [sb(f"PT{k}", [P, 2, 2, P]) for k in range(4)]
        OT = sb("OT", [P, IC, T])

        def steps(eng, step):
            step(None, False, (0, 0, 0))
            step((0, 0, 0), True, (0, 1, 1))
            step((0, 1, 1), True, (1, 0, 2))
            with eng.Fori(1, TPB - 1) as i:
                step((i, 0, NB * i), False, (i, 1, NB * i + 1))
                step((i, 1, NB * i + 1), False, (i + 1, 0, NB * i + 2))
            i = TPB - 1
            step((i, 0, NB * i), False, (i, 1, NB * i + 1))
            step((i, 1, NB * i + 1), False, None)

        def slots(att, prj, attend, project, after=None):
            for s in range(SLOTS):
                if att:
                    attend(s)
                if prj:
                    for x in range(PIECES):
                        if PIECE_SLOT[x] == s:
                            project(x)
                if att and after:
                    after(s)

        def unit(s):
            return s // 4, s // 2 % 2, s % 2

        def heads(buf, s):
            w, g, h = unit(s)
            return buf[:, w, 4 * g:4 * g + 4].rearrange("p (j h) -> p j h", h=2)[:, :, h]

        def keys(s, first):
            return slice(P, 2 * P) if first and s < 4 else slice(0, 2 * P)

        def scores(s, ks):
            return PS[:, SC[s % 2]].rearrange("p (j t) -> p j t", j=2)[:, :, ks]

        with nc.Block() as block:

            @block.sync
            def _(sp):
                for k in range(DC):
                    sp.dma_start(wqkv[:, k], io["wqkv"][layer, k * P:(k + 1) * P]).then_inc(w_in, 16)
                sp.dma_start(wo[:], io["wo"][layer].rearrange("(k p) o -> p k o", p=P)).then_inc(w_in, 16)
                sp.dma_start(sc[:], io["qk_scale"][layer]).then_inc(w_in, 16)
                for t, name in ((pairsum, "pairsum"), (headsum, "headsum")):
                    sp.dma_start(t[:], io[name]).then_inc(w_in, 16)
                tables = io["tables"].rearrange("a p t -> p a t")
                sp.dma_start(tab[:], tables[:, :, 0:T]).then_inc(tab_in, 16)
                half = HD1 // 2

                def step(att, first, prj):
                    if not prj:
                        return
                    i, b, u = prj
                    if b == 0 and not (isinstance(i, int) and i == 0):
                        sp.wait_ge(roped, QK * u)
                        sp.dma_start(tab[:], tables[:, :, bass.ds(i * T, T)]).then_inc(tab_in, 16)
                    for x in range(QK):
                        sp.wait_ge(raw_s, QK * u + x + 1)
                        if x >= 2:
                            sp.wait_ge(t2_s, QK * u + x - 1)
                        for r in range(0, P, half):
                            src = r + half if r % HD1 == 0 else r - half
                            sp.dma_start(swapped[x % 2][r:r + half, :], raw[x % 2][src:src + half, :]).then_inc(swapped_in[x % 2], 16)

                steps(sp, step)

            @block.gpsimd
            def _(pool):
                def step(att, first, prj):
                    if prj:
                        i, b, u = prj
                        if att:
                            pool.wait_ge(v_ps, WPT * u)
                            pool.sem_inc(core.tick, 1)
                        for c in range(DC):
                            op = nc.gpsimd.tensor_copy(Hs[:, c], shifted(Y, c, b, i))
                        op.then_inc(hs, 1)

                steps(pool, step)

            @block.tensor
            def _(pe):
                pe.wait_ge(w_in, 16 * n_w)
                masks = core.mask[:].rearrange("p a t -> p (a t)")

                def step(att, first, prj):
                    def attend(s):
                        _, b, u = att
                        if s == 0:
                            pe.wait_ge(roped, QK * (u + 1))
                            pe.wait_ge(v_sb, WPT * (u + 1))
                        if s < UNITS:
                            if s >= 2:
                                pe.wait_ge(exp_s, UNITS * u + s - 1)
                            w, g, h = unit(s)
                            ks, rows = keys(s, first), slice(HD1 * h, HD1 * (h + 1))
                            for j in range(2):
                                c = 2 * g + j
                                out = scores(s, ks)[:, j]
                                nc.tensor.matmul(out, core.lower[:], masks[:, ks], start=True, stop=True)
                                mm = nc.tensor.matmul(out, QT[b][rows, c, w * P:(w + 1) * P],
                                                      KT[b][rows, c, w * P + ks.start:w * P + ks.stop],
                                                      start=False, stop=True, skip_group_check=True)
                            mm.then_inc(s_ps, 1)
                        y = s - TR_LAG
                        if 0 <= y < UNITS:
                            pe.wait_ge(norm_s, UNITS * u + y + 1)
                            if y >= 2:
                                pe.wait_ge(pt_s, UNITS * u + y - 1)
                            elif not (isinstance(u, int) and u == 0):
                                pe.wait_ge(y_done, u)
                            for j in range(2):
                                for kb in range(keys(y, first).start // P, 2):
                                    mm = nc.tensor.transpose(PS[:, TR[y % 2], (2 * j + kb) * P:(2 * j + kb + 1) * P],
                                                             Pb[y % 4][:, j, kb * P:(kb + 1) * P], core.ident[:])
                            mm.then_inc(tr_ps, 1)

                    def project(x):
                        i, b, u = prj
                        again = not (isinstance(u, int) and u == 0)
                        y = x - 1
                        if 0 <= y < IC:
                            pe.wait_ge(sqr_s, QK * u + y + 1)
                            for w in range(WPT):
                                col = w * NH1 + 2 * y
                                mm = nc.tensor.matmul(PS[:, SS, col:col + 2], sqr[y % 2][:, w * P:(w + 1) * P], headsum[:],
                                                      start=True, stop=True)
                            mm.then_inc(qss_ps, 1)
                        elif IC <= y < QK:
                            pe.wait_ge(sqr_s, QK * u + y + 1)
                            if y == IC:
                                pe.wait_ge(qmax, u + 1)
                            else:
                                pe.wait_ge(kmax, IC * u + y - IC)
                            nc.tensor.matmul(PS[:, SS], pairsum[:], sqr[y % 2][:], start=True, stop=True).then_inc(kss_ps, 1)
                        if x < QK:
                            if x >= 1:
                                pe.wait_ge(sqr_s, QK * u + x)
                            elif again:
                                pe.wait_ge(v_sb, WPT * u)
                            for k in range(DC):
                                mm = nc.tensor.matmul(PS[:, PJ], wqkv[:, k, x * P:(x + 1) * P], shifted(Y, k, b, i),
                                                      start=(k == 0), stop=(k == DC - 1))
                            mm.then_inc(pj_ps, 1)
                        if x >= V_PIECE:
                            w = x - V_PIECE
                            if w == 0:
                                pe.wait_ge(hs, u + 1)
                            if w >= 2:
                                pe.wait_ge(v_sb, WPT * u + w - 1)
                            for k in range(DC):
                                mm = nc.tensor.matmul(PS[:, (PJ, V2)[w % 2]], Hs[:, k, w * P:(w + 1) * P], wqkv[:, k, 2 * INNER:],
                                                      start=(k == 0), stop=(k == DC - 1))
                            mm.then_inc(v_ps, 1)

                    def after(s):
                        _, b, u = att
                        if (s - OUT_LAG) % 2 or s < OUT_LAG:
                            return
                        q = (s - OUT_LAG) // 2
                        w, g, _ = unit(2 * q)
                        pe.wait_ge(pt_s, UNITS * u + 2 * q + 2)
                        if g == 0 and w >= 1:
                            pe.wait_ge(o_sb, WPT * u + w)
                        kbs = range(keys(2 * q, first).start // P, 2)
                        for j in range(2):
                            c = 2 * g + j
                            for kb in kbs:
                                for h in range(2):
                                    mm = nc.tensor.matmul(PS[HD1 * h:HD1 * (h + 1), OB, c * P:(c + 1) * P],
                                                          V[b][:, w + kb, (2 * c + h) * HD1:(2 * c + h + 1) * HD1],
                                                          PTb[(2 * q + h) % 4][:, j, kb], start=(kb == kbs[0]), stop=(kb == 1))
                        mm.then_inc(pv_ps, 1)

                    slots(att, prj, attend, project, after)
                    if att:
                        _, _, u = att
                        pe.wait_ge(o_sb, WPT * (u + 1))
                        for c in range(DC):
                            for k in range(IC):
                                mm = nc.tensor.matmul(PS[:, TR[c]], wo[:, k, c * P:(c + 1) * P], OT[:, k], start=(k == 0), stop=(k == IC - 1))
                        mm.then_inc(wo_ps, 1)

                steps(pe, step)

            @block.scalar
            def _(act):
                nc.scalar.preload_act_table_set("natural_log_exp_and_others")

                def step(att, first, prj):
                    def attend(s):
                        _, b, u = att
                        if s < UNITS:
                            act.wait_ge(nb_s, UNITS * u + s + 1)
                            if s >= 4:
                                act.wait_ge(tr_ps, UNITS * u + s - 3)
                            ks = keys(s, first)
                            for j in range(2):
                                op = nc.scalar.activation(Pb[s % 4][:, j, ks], scores(s, ks)[:, j], ACT.Exp,
                                                          bias=heads(nb, s)[:, j:j + 1], scale=heads(rq[b], s)[:, j:j + 1],
                                                          accum_out=heads(sums, s)[:, j:j + 1])
                            op.then_inc(exp_s, 1)

                    def project(x):
                        i, b, u = prj
                        y = x - 2
                        if IC <= y < QK:
                            n = IC * u + y - IC
                            act.wait_ge(kmax, n + 1)
                            nc.scalar.activation(rn[y % 2][:], rn[y % 2][:], ACT.Ln, scale=LN_SCALE).then_inc(klog, 1)
                            act.wait_ge(klog, n + 1)
                            nc.scalar.activation(rn[y % 2][:], rn[y % 2][:], ACT.Exp, scale=-0.5).then_inc(krn, 1)
                        if y == IC:
                            act.wait_ge(qmax, u + 1)
                            nc.scalar.activation(rq[b][:], rq[b][:], ACT.Ln, scale=LN_SCALE).then_inc(qlog, 1)
                            act.wait_ge(qlog, u + 1)
                            nc.scalar.activation(rq[b][:], rq[b][:], ACT.Exp, scale=-0.5).then_inc(rq_s, 1)
                        if x < QK:
                            act.wait_ge(pj_ps, QK * u + x + 1)
                            if x >= 2:
                                act.wait_ge(t1_s, QK * u + x - 1)
                                if x - 2 < IC:
                                    act.wait_ge(qss_ps, IC * u + x - 1)
                                else:
                                    act.wait_ge(kss_ps, IC * u + x - 1 - IC)
                                act.wait_ge(swapped_in[x % 2], 64 * (QK // 2 * u + x // 2))
                            nc.scalar.copy(raw[x % 2][:], PS[:, PJ]).then_inc(raw_s, 1)
                            nc.scalar.activation(sqr[x % 2][:], PS[:, PJ], ACT.Square).then_inc(sqr_s, 1)
                        if x >= V_PIECE:
                            w = x - V_PIECE
                            act.wait_ge(v_ps, WPT * u + w + 1)
                            if w == 0:
                                act.wait_ge(hist, u + 1)
                            nc.scalar.copy(V[b][:, 1 + w], PS[:, (PJ, V2)[w % 2]]).then_inc(v_sb, 1)

                    def after(s):
                        _, b, u = att
                        if s >= OUT_LAG + 2 and (s - OUT_LAG - 2) % 4 == 0:
                            w = (s - OUT_LAG - 2) // 4
                            act.wait_ge(pv_ps, UNITS // 2 * u + 2 * (w + 1))
                            nc.scalar.copy(OT[:, :, w * P:(w + 1) * P], PS[:, OB].rearrange("p (c t) -> p c t", c=IC)).then_inc(o_sb, 1)

                    slots(att, prj, attend, project, after)

                steps(act, step)

            @block.vector
            def _(dve):
                dve.wait_ge(w_in, 16 * n_w)

                def step(att, first, prj):
                    def attend(s):
                        _, b, u = att
                        if s == 0:
                            dve.wait_ge(rq_s, u + 1)
                        if s < UNITS:
                            n = UNITS * u + s
                            dve.wait_ge(s_ps, n + 1)
                            nc.vector.tensor_reduce(heads(mx, s), scores(s, keys(s, first)), AX_X, ALU.max).then_inc(mx_s, 1)
                            dve.wait_ge(mx_s, n + 1)
                            nc.vector.scalar_tensor_tensor(heads(nb, s), heads(mx, s), -1.0, heads(rq[b], s), ALU.mult, ALU.mult
                                                           ).then_inc(nb_s, 1)
                        if 1 <= s <= UNITS:
                            dve.wait_ge(exp_s, UNITS * u + s)
                            nc.vector.reciprocal(heads(rsum, s - 1), heads(sums, s - 1)).then_inc(rsum_s, 1)
                            dve.wait_ge(rsum_s, UNITS * u + s)
                            p, ks = Pb[(s - 1) % 4], keys(s - 1, first)
                            for j in range(2):
                                op = nc.vector.tensor_scalar(p[:, j, ks], p[:, j, ks], heads(rsum, s - 1)[:, j:j + 1], None, ALU.mult)
                            op.then_inc(norm_s, 1)
                        z = s - TR_LAG
                        if 0 <= z < UNITS:
                            kb = keys(z, first).start // P
                            dve.wait_ge(tr_ps, UNITS * u + z + 1)
                            if z >= 4:
                                dve.wait_ge(pv_ps, UNITS // 2 * u + z // 2 - 1)
                            src = PS[:, TR[z % 2]].rearrange("p (j k t) -> p j k t", j=2, k=2)
                            nc.vector.tensor_copy(PTb[z % 4][:, :, kb:], src[:, :, kb:]).then_inc(pt_s, 1)

                    def project(x):
                        i, b, u = prj
                        if x == 0:
                            if isinstance(i, int) and i == 0:
                                dve.sem_inc(hist, 1)
                            else:
                                nc.vector.tensor_copy(KT[b][:, :, 0:P], KT[b][:, :, T:T + P])
                                nc.vector.tensor_copy(V[b][:, 0], V[b][:, WPT]).then_inc(hist, 1)
                            if b == 0:
                                dve.wait_ge(tab_in, 16 * (i + 1))
                        y = x - 1
                        if IC <= y < QK:
                            m = IC * u + y - IC
                            dve.wait_ge(kss_ps, m + 1)
                            dve.wait_ge(roped, QK * u + y - 1)
                            nc.vector.tensor_scalar(rn[y % 2][:], PS[:, SS], NORM2_MIN, None, ALU.max).then_inc(kmax, 1)
                        y = x - 2
                        if IC <= y < QK:
                            m = IC * u + y - IC
                            dve.wait_ge(krn, m + 1)
                            dve.wait_ge(ksum, m + 1)
                            dve.wait_ge(hist, u + 1)
                            nc.vector.tensor_tensor(KT[b][:, y - IC, P:], kn[:], rn[y % 2][:], ALU.mult).then_inc(roped, 1)
                        y = x - 1
                        if 0 <= y < QK:
                            a, c = divmod(y, IC)
                            n, m = QK * u + y, IC * u + c
                            dve.wait_ge(raw_s, n + 1)
                            if 1 <= y <= IC:
                                dve.wait_ge(roped, n)
                            elif y > IC or not (isinstance(u, int) and u == 0):
                                dve.wait_ge(ksum, IC * u + max(y - IC, 0))
                            nc.vector.scalar_tensor_tensor(t1[:], raw[y % 2][:], sc[:, a, 0:1], tab[:, 2 * a], ALU.mult, ALU.mult
                                                           ).then_inc(t1_s, 1)
                            dve.wait_ge(swapped_in[y % 2], 64 * (QK // 2 * u + y // 2 + 1))
                            nc.vector.scalar_tensor_tensor(t2[:], swapped[y % 2][:], sc[:, a, 1:2], tab[:, 2 * a + 1], ALU.mult,
                                                           ALU.mult).then_inc(t2_s, 1)
                            if y == IC - 1:
                                dve.wait_ge(qss_ps, IC * (u + 1))
                                nc.vector.tensor_scalar(rq[b][:].rearrange("p w h -> p (w h)"), PS[:, SS, 0:WPT * NH1], NORM2_MIN,
                                                        None, ALU.max).then_inc(qmax, 1)
                            dve.wait_ge(t2_s, n + 1)
                            if a == 0:
                                nc.vector.tensor_tensor(QT[b][:, c], t1[:], t2[:], ALU.add).then_inc(roped, 1)
                            else:
                                if c >= 1:
                                    dve.wait_ge(roped, n)
                                nc.vector.tensor_tensor(kn[:], t1[:], t2[:], ALU.add).then_inc(ksum, 1)

                    slots(att, prj, attend, project)
                    if att:
                        i, b, u = att
                        dve.wait_ge(wo_ps, u + 1)
                        for c in range(DC):
                            op = nc.vector.tensor_tensor(plain(Yn, c, b, i), plain(Y, c, b, i), PS[:, TR[c]], ALU.add)
                        op.then_inc(y_done, 1)

                steps(dve, step)


def ffn1(core, layer, Y, H):
    nc, io, PS = core.nc, core.io, core.PS
    tag = f"f1{layer}_"
    w_in, ag_ps, gelu_s, hid_s, w2_ps, y_done = (core.sem(tag + n) for n in "w_in ag_ps gelu hid w2_ps y_done".split())
    lag = 2
    with ExitStack() as st:
        sb = lambda n, sh: st.enter_context(nc.sbuf_tensor(tag + n, sh, F32))
        w1, w2 = sb("w1", [P, DC, 2 * HID]), sb("w2", [P, HC, D])
        b1, b2 = sb("b1", [P, 2, HC]), sb("b2", [P, DC])
        gl = [sb(f"gl{k}", [P, T]) for k in range(2)]
        hid = [sb(f"hid{k}", [P, T]) for k in range(4)]
        with nc.Block() as block:

            @block.sync
            def _(sp):
                for k in range(DC):
                    sp.dma_start(w1[:, k], io["l_w1"][layer, k * P:(k + 1) * P]).then_inc(w_in, 16)
                sp.dma_start(w2[:], io["l_w2"][layer]).then_inc(w_in, 16)
                sp.dma_start(b1[:], io["l_b1"][layer]).then_inc(w_in, 16)
                sp.dma_start(b2[:], io["l_b2"][layer]).then_inc(w_in, 16)

            @block.tensor
            def _(pe):
                pe.wait_ge(w_in, 16 * (DC + 3))
                pe.sem_inc(y_done, 1)
                with pe.Fori(0, TPB) as i:
                    for b in range(NB):
                        u = NB * i + b
                        for x in range(HC + lag):
                            if x < HC:
                                if x >= 2:
                                    pe.wait_ge(hid_s, HC * u + x - 1)
                                    pe.sem_inc(core.tick, 1)
                                for half in range(2):
                                    o = half * HID + x * P
                                    for k in range(DC):
                                        mm = nc.tensor.matmul(PS[0:HCS[x], 2 * (x % 2) + half], w1[:, k, o:o + HCS[x]],
                                                              H[:, k, tok(b, i)], start=(k == 0), stop=(k == DC - 1))
                                    mm.then_inc(ag_ps, 1)
                            z = x - lag
                            if z >= 0:
                                pe.wait_ge(hid_s, HC * u + z + 1)
                                if z == 0 and b == 0:
                                    pe.wait_ge(y_done, NB * i + 1)
                                for c in range(DC):
                                    mm = nc.tensor.matmul(PS[:, 4 + 2 * b + c], w2[0:HCS[z], z, c * P:(c + 1) * P],
                                                          hid[z % 4][0:HCS[z]], start=(z == 0), stop=(z == HC - 1))
                                mm.then_inc(w2_ps, 1)

            @block.scalar
            def _(act):
                nc.scalar.preload_act_table_set("gelu_and_others")
                act.wait_ge(w_in, 16 * (DC + 3))
                with act.Fori(0, TPB) as i:
                    for b in range(NB):
                        u = NB * i + b
                        for x in range(HC):
                            g = HC * u + x
                            act.wait_ge(ag_ps, 2 * (g + 1))
                            nc.scalar.activation(gl[x % 2][0:HCS[x]], PS[0:HCS[x], 2 * (x % 2) + 1], ACT.Gelu,
                                                 bias=b1[0:HCS[x], 1, x:x + 1]).then_inc(gelu_s, 1)

            @block.vector
            def _(dve):
                dve.wait_ge(w_in, 16 * (DC + 3))
                with dve.Fori(0, TPB) as i:
                    for b in range(NB):
                        u = NB * i + b
                        for x in range(HC):
                            g = HC * u + x
                            dve.wait_ge(gelu_s, g + 1)
                            if x >= 4:
                                dve.wait_ge(w2_ps, g - 3)
                            nc.vector.scalar_tensor_tensor(hid[x % 4][0:HCS[x]], PS[0:HCS[x], 2 * (x % 2)], b1[0:HCS[x], 0, x:x + 1],
                                                           gl[x % 2][0:HCS[x]], ALU.add, ALU.mult).then_inc(hid_s, 1)
                        dve.wait_ge(w2_ps, HC * (u + 1))
                        for c in range(DC):
                            y = plain(Y, c, b, i)
                            op = nc.vector.scalar_tensor_tensor(y, PS[:, 4 + 2 * b + c], b2[:, c:c + 1], y, ALU.add, ALU.add)
                        op.then_inc(y_done, 1)


def local_layers(core):
    nc, io, mod = core.nc, core.io, core.mod
    saved, zeroed, zeroed_z, ln_in, x_in, out_s, written = (
        core.sem("ll_" + n) for n in "saved zeroed zeroed_z ln_in x_in out written".split())
    padded = lambda n: nc.sbuf_tensor(n, [P, DC, NB, 1 + S], F32)
    with ExitStack() as st:
        Y = st.enter_context(padded("Y"))
        lgb = st.enter_context(nc.sbuf_tensor("lgb", [P, 2, 2, DC], F32))
        with nc.Block() as block:
            @block.sync
            def _(sp):
                sp.dma_start(lgb[:], io["l_ln"]).then_inc(ln_in, 16)
                sp.dma_start(core.x_dram.rearrange("(k p) t -> p k t", p=P), core.X[:]).then_inc(saved, 16)
                sp.wait_ge(saved, 16)
                sp.wait_ge(ln_in, 16)

            @block.gpsimd
            def _(pool):
                nc.gpsimd.memset(Y[:, :, :, 0:1], 0.0).then_inc(zeroed, 1)
                pool.wait_ge(zeroed, 1)
        layernorm(core, "ln3", lambda c, b, i: core.X[:, c, tok(b, i)], lambda c, b, i: plain(Y, c, b, i),
                  lambda c, b: mod[:, 1, CB, c, b:b + 1], lambda c, b: mod[:, 1, SB_, c, b:b + 1])
        Z = core.XP[:].rearrange("p (c b t) -> p c b t", c=DC, b=NB)
        with nc.Block() as block:
            @block.gpsimd
            def _(pool):
                nc.gpsimd.memset(Z[:, :, :, 0:1], 0.0).then_inc(zeroed_z, 1)
                pool.wait_ge(zeroed_z, 1)
        for layer, (src, dst) in enumerate(((Y, Z), (Z, Y))):
            with nc.cleanup_on_exit():
                attn1(core, layer, src, dst)
                with nc.sbuf_tensor(f"H{3 + layer}", [P, DC, NB * S], F32) as H:
                    layernorm(core, f"ln{4 + layer}", lambda c, b, i: shifted(dst, c, b, i), lambda c, b, i: H[:, c, tok(b, i)],
                              lambda c, b: lgb[:, layer, 0, c:c + 1], lambda c, b: lgb[:, layer, 1, c:c + 1])
                    ffn1(core, layer, dst, H)
        xi = [st.enter_context(nc.sbuf_tensor(f"ll_x{b}", [P, DC, T], F32)) for b in range(NB)]
        with nc.Block() as block:
            @block.sync
            def _(sp):
                x_view = core.x_dram.rearrange("(k p) t -> p k t", p=P)
                out_view = io["out"].rearrange("(k p) t -> p k t", p=P)
                sp.sem_inc(written, 16)
                with sp.Fori(0, TPB) as i:
                    for b in range(NB):
                        sp.wait_ge(written, 16 * NB * i + 16)
                        sp.dma_start(xi[b][:], x_view[:, :, tok(b, i)]).then_inc(x_in, 16)
                        sp.wait_ge(x_in, 16 * (NB * i + b + 1))
                    for b in range(NB):
                        sp.wait_ge(out_s, NB * i + b + 1)
                        sp.dma_start(out_view[:, :, tok(b, i)], xi[b][:]).then_inc(written, 16)
                sp.wait_ge(written, 16 * NB * TPB + 16)

            @block.vector
            def _(dve):
                with dve.Fori(0, TPB) as i:
                    for b in range(NB):
                        dve.wait_ge(x_in, 16 * (NB * i + b + 1))
                        for c in range(DC):
                            op = nc.vector.scalar_tensor_tensor(xi[b][:, c], plain(Y, c, b, i), mod[:, 1, GB, c, b:b + 1], xi[b][:, c],
                                                                ALU.mult, ALU.add)
                        op.then_inc(out_s, 1)


def program(nc, io):
    with ExitStack() as stack:
        core = Core(nc, stack, io)
        X, mod = core.X, core.mod
        setup(core)
        x_tile = lambda c, b, i: X[:, c, tok(b, i)]
        h_tile = lambda H: lambda c, b, i: H[:, c, tok(b, i)]
        modulated = lambda layer, w_scale, w_shift: (lambda c, b: mod[:, layer, w_scale, c, b:b + 1],
                                                     lambda c, b: mod[:, layer, w_shift, c, b:b + 1])
        with nc.cleanup_on_exit():
            with nc.sbuf_tensor("H", [P, DC, NB * S], F32) as H:
                layernorm(core, "ln0", x_tile, h_tile(H), *modulated(0, CA, SA))
                with nc.sbuf_tensor("VV", [P, NB, NBLK, NH0, HD0 + 1], F32) as VV:
                    attn0_project(core, H, VV)
                    attn0_scores(core, VV)
            attn0_out(core)
        with nc.cleanup_on_exit():
            with nc.sbuf_tensor("H1", [P, DC, NB * S], F32) as H:
                layernorm(core, "ln1", x_tile, h_tile(H), *modulated(0, CB, SB_))
                ffn0(core, H)
            filter_taps(core)
            with ExitStack() as st:
                V, X0 = (st.enter_context(nc.sbuf_tensor(n, [P, DC, NB * S], F32)) for n in ("V", "X0"))
                RR = st.enter_context(nc.sbuf_tensor("RR", [P, D // 2, BPO, NJ // BPO, NB], F32))
                with nc.sbuf_tensor("H2", [P, DC, NB * S], F32) as H:
                    layernorm(core, "ln2", x_tile, h_tile(H), *modulated(1, CA, SA))
                    conv_inputs(core, H, V, X0, RR)
                long_conv(core, RR)
                conv_out(core, V, X0)
        local_layers(core)




def columns(v):
    v = np.asarray(v)
    v = v.reshape(v.shape[:-1] + (-1, P))
    return np.moveaxis(v, -1, 0)


def filter_positions():
    f32 = np.float32
    t = np.linspace(0, 1, NT).astype(f32)
    w = (2 * np.pi * np.linspace(0, NT - 1, NT) / NT).astype(f32)
    fw = f32(1e-4) * w
    deltas = np.abs(np.linspace(np.log(0.01) / 1.5, np.log(0.01) / 0.3, D)).astype(f32)
    return {"f_z": np.stack([t, np.cos(fw), -np.sin(fw)]).astype(f32),
            "f_decay": (np.exp(-deltas[:, None] * t[None]) + f32(0.05)).astype(f32)}


def rotary_tables():
    f32 = np.float32
    half = np.arange(0, HD1, 2, dtype=f32)
    t = np.arange(S, dtype=f32)
    angle = t[:, None] * (1 / f32(10000) ** (half / f32(HD1))).astype(f32)[None]
    base = ((half + f32(0.4 * HD1)) / f32(1.4 * HD1)).astype(f32)
    power = ((t - S // 2) / f32(P // 2)).astype(f32)
    scale = base[None] ** power[:, None]
    cos, sin = np.cos(angle), np.sin(angle)
    up = f32(LN_SCALE ** 0.5)
    tables = np.stack([cos * scale * (8 * up), sin * scale * (8 * up), cos / scale * up, sin / scale * up]).transpose(0, 2, 1)
    sign = np.array([1, -1, 1, -1], f32)[:, None, None]
    return np.tile(np.concatenate([sign * tables, tables], 1), (1, P // HD1, 1)).astype(f32)


def head_matrices():
    head = np.arange(P) // HD1
    return {"pairsum": (head[:, None] == head[None]).astype(np.float32),
            "headsum": (head[:, None] == np.arange(2)[None]).astype(np.float32)}


def layout(d):
    d = {k: np.asarray(v) for k, v in d.items()}
    o = {"xT": d["L0_attn_x"].reshape(NB * S, D).T,
         "cT": np.stack([d["L0_c"], d["L1_c"]]).transpose(2, 0, 1),
         "wmod": np.stack([d["L0_wmod"], d["L1_wmod"]])}
    for n in ("Wq", "Wk", "Wv", "Wo"):
        o[n.lower() + "T"] = d["L0_attn_" + n].T
    for n in ("bq", "bk", "bv", "bo"):
        o[n] = columns(d["L0_attn_" + n])
    cross, shift = np.zeros((DC, P, P), np.float32), np.zeros((DC, P, P), np.float32)
    for h in range(NH0):
        c, r = h // HPC, h % HPC * HD0
        cross[c, r:r + HD0, r:r + HD0] = d["L0_attn_W_cross"][h]
        for f in range(HD0):
            n = min(MS0, HD0 - f)
            shift[c, r + f, r + f:r + f + n] = d["L0_attn_shift_weights"][h, :n]
    o["wc_bd"], o["shift_bd"] = cross, shift
    o["gate_rep"] = columns(np.repeat(d["L0_attn_gate"], HD0))
    for n in ("w1", "w2", "h1", "h2", "w3"):
        o[n + "T"] = d[f"L0_ffn_{n}_w"].T
        o[n + "s"] = columns(d[f"L0_ffn_{n}_s"])
    A = lambda n: d["L1_attn_" + n]
    o.update(filter_positions())
    for k in (1, 2, 3):
        o[f"f_w{k}"] = A(f"f_w{k}")
    o["f_bf"] = np.stack([np.stack([A(f"f_b{k}"), A(f"freq{k}")], -1) for k in (1, 2, 3)], 1)
    o["f_wout"], o["h_win"], o["h_wout"] = A("f_wout"), A("w_in"), A("w_out")
    o["h_bin"], o["h_sfb"], o["h_bout"], o["h_fb"] = (columns(A(n)) for n in ("b_in", "sf_b", "b_out", "filt_bias"))
    o["h_sfw"] = A("sf_w").reshape(UC, P, -1).transpose(1, 0, 2)
    F = lambda n: d["L1_ffn_" + n]
    depth = F("wqkv").shape[0]
    o["wqkv"], o["wo"], o["l_w1"] = F("wqkv"), F("wo"), F("w1")
    scale = np.stack([np.tile(F(n), (1, P // HD1)) for n in ("q_scale", "k_scale")], -1)
    halves = scale.reshape(depth, P // HD1, 2, HD1 // 2, 2)
    o["qk_scale"] = np.stack([scale, halves[:, :, ::-1].reshape(scale.shape)], -1)
    o["tables"] = rotary_tables()
    o.update(head_matrices())
    o["l_ln"] = columns(np.stack([F("ln_g"), F("ln_b")], 1))
    w2 = np.zeros((depth, HC * P, D), np.float32)
    w2[:, :HID] = F("w2")
    o["l_w2"] = w2.reshape(depth, HC, P, D).transpose(0, 2, 1, 3)
    b1 = np.zeros((depth, 2, HC * P), np.float32)
    b1[:, :, :HID] = F("b1").reshape(depth, 2, HID)
    o["l_b1"] = b1.reshape(depth, 2, HC, P).transpose(0, 3, 1, 2)
    o["l_b2"] = F("b2").reshape(depth, DC, P).transpose(0, 2, 1)
    return {k: np.ascontiguousarray(v) for k, v in o.items()}


def kernel(**inputs):
    import concourse.bacc as bacc
    from concourse.bass_utils import run_bass_kernel_spmd

    nc = bacc.Bacc("TRN2", target_bir_lowering=False, num_devices=1)
    arrays = {"in_" + k: v for k, v in layout(inputs).items()}
    io = {k[3:]: nc.dram_tensor(k, v.shape, mybir.dt.from_np(v.dtype), kind="ExternalInput").ap()
          for k, v in arrays.items()}
    io["out"] = nc.dram_tensor("out", (D, NB * S), F32, kind="ExternalOutput").ap()
    program(nc, io)
    r = run_bass_kernel_spmd(nc, [arrays], core_ids=[0])
    return np.ascontiguousarray(r.results[0]["out"].T).reshape(NB, S, D)
```

```python
from contextlib import ExitStack

import numpy as np

import concourse.bass as bass
from concourse import mybir
from concourse.alu_op_type import AluOpType as ALU

F32 = mybir.dt.float32
BF16 = mybir.dt.bfloat16
ACT = mybir.ActivationFunctionType
AX_X = mybir.AxisListType.X

P = 128
D = 256
DC = D // P
NB = 2
S = 2048
T = 512
TPB = S // T
EPS = 1e-5
BIG = 1e30

BELOW, ABOVE = 0, 1

SA, CA, GA, SB_, CB, GB = range(6)


def tok(b, i):
    return bass.ds(i * T + b * S, T)


class Core:

    def __init__(self, nc, stack, io):
        self.nc, self.io, self.stack = nc, io, stack
        self.XP = stack.enter_context(nc.sbuf_tensor("X", [P, DC * NB * (1 + S)], F32))
        self.X = self.XP[:, 0:DC * NB * S].rearrange("p (c t) -> p c t", c=DC)
        self.ones = stack.enter_context(nc.sbuf_tensor("ones", [P, P], F32))
        self.ident = stack.enter_context(nc.sbuf_tensor("ident", [P, P], F32))
        self.identb = stack.enter_context(nc.sbuf_tensor("identb", [P, P], BF16))
        self.lower = stack.enter_context(nc.sbuf_tensor("lower", [P, P], BF16))
        self.mask = stack.enter_context(nc.sbuf_tensor("mask", [P, 2, P], BF16))
        self.eps = stack.enter_context(nc.sbuf_tensor("eps", [P, 1], F32))
        self.mod = stack.enter_context(nc.sbuf_tensor("mod", [P, 2, 6, DC, NB], F32))
        self.PS = stack.enter_context(nc.psum_tensor("PS", [P, 8, 512], F32))
        self.tick = self.sem("tick")
        self.qk_parts = nc.dram_tensor("qk_parts", [2, NB, 3, D, S], BF16, kind="Internal").ap()
        self.o_dram = nc.dram_tensor("o_dram", [NB, NH0, HD0, S], F32, kind="Internal").ap()
        self.sum_dram = nc.dram_tensor("sum_dram", [NB, NH0, S], F32, kind="Internal").ap()
        self.kpad = nc.dram_tensor("kpad", [D, KW], F32, kind="Internal").ap()
        self.x_dram = nc.dram_tensor("x_dram", [D, NB * S], F32, kind="Internal").ap()
        self.y_dram = nc.dram_tensor("y_dram", [D * NB * NI, OW], F32, kind="Internal").ap()
        self.recip_dram = nc.dram_tensor("recip_dram", [NB, NH0, S], F32, kind="Internal").ap()

    def sem(self, name):
        return self.nc.alloc_semaphore(name=name)


class Weights:

    def __init__(self, core, stack, tag, arrays, place=None):
        self.loaded = core.sem(tag + "loaded")
        self.buf, self.moves = {}, []
        for name, shape, sources in arrays:
            buf = place.buf[name] if place else stack.enter_context(core.nc.sbuf_tensor(tag + name, shape, F32))
            self.buf[name] = buf
            self.moves += [(buf[index], src) for index, src in sources]
        self.all = 16 * len(self.moves)

    def start(self, sp):
        for dst, src in self.moves:
            sp.dma_start(dst, src).then_inc(self.loaded, 16)


WHOLE = slice(None)
by_chunk = lambda ap: ap.rearrange("(k p) o -> p k o", p=P)


def setup(core):
    nc, io, mod = core.nc, core.io, core.mod
    loaded, x_in = core.sem("su_loaded"), core.sem("su_x_in")
    filled, picked = core.sem("su_filled"), core.sem("su_picked")
    c_act, mod_ps, mod_sb, gate_parts = (core.sem("su_" + n) for n in ("c_act", "mod_ps", "mod_sb", "gate_parts"))
    done = core.sem("su_done")
    with ExitStack() as st:
        sb = lambda n, s, d=F32: st.enter_context(nc.sbuf_tensor(n, s, d))
        cT = sb("cT", [P, DC, 2, NB])
        cs = sb("cs", [P, DC, 2, NB])
        wm = sb("wm", [P, 2, DC, 6 * D])
        sgn = sb("sgn", [P, 2, 2, DC, NB])
        mag = sb("mag", [P, 2, 2, DC, NB])
        ps = core.PS[:, 0]
        with nc.Block() as block:

            @block.sync
            def _(sp):
                sp.dma_start(cT[:], io["cT"].rearrange("(k p) l b -> p k l b", p=P)).then_inc(loaded, 16)
                for layer in range(2):
                    sp.dma_start(wm[:, layer], io["wmod"][layer].rearrange("(k p) n -> p k n", p=P)).then_inc(loaded, 16)
                sp.dma_start(core.X[:], io["xT"].rearrange("(k p) t -> p k t", p=P)).then_inc(x_in, 16)
                sp.wait_ge(x_in, 16)

            @block.gpsimd
            def _(pool):
                nc.gpsimd.memset(core.eps[:], EPS)
                nc.gpsimd.memset(core.ones[:], 1.0 / D)
                nc.gpsimd.memset(core.ident[:], 0.0)
                nc.gpsimd.memset(core.identb[:], 0.0)
                nc.gpsimd.memset(core.lower[:], 0.0)
                nc.gpsimd.memset(core.mask[:], 0.0).then_inc(filled, 1)
                pool.wait_ge(filled, 1)
                eye = [[-1, P]]
                nc.gpsimd.affine_select(out=core.ident[:], in_=core.ident[:], compare_op=ALU.not_equal, fill=1.0,
                                        base=0, pattern=eye, channel_multiplier=1)
                nc.gpsimd.affine_select(out=core.identb[:], in_=core.identb[:], compare_op=ALU.not_equal, fill=1.0,
                                        base=0, pattern=eye, channel_multiplier=1)
                nc.gpsimd.affine_select(out=core.lower[:], in_=core.lower[:], compare_op=ALU.not_equal, fill=-BIG,
                                        base=0, pattern=eye, channel_multiplier=1)
                nc.gpsimd.affine_select(out=core.mask[:, BELOW], in_=core.mask[:, BELOW], compare_op=ALU.is_ge, fill=1.0,
                                        base=0, pattern=[[1, P]], channel_multiplier=-1)
                nc.gpsimd.affine_select(out=core.mask[:, ABOVE], in_=core.mask[:, ABOVE], compare_op=ALU.is_ge, fill=1.0,
                                        base=0, pattern=[[-1, P]], channel_multiplier=1).then_inc(picked, 1)
                pool.wait_ge(picked, 1)

            @block.scalar
            def _(act):
                act.wait_ge(loaded, 16 * 3)
                nc.scalar.activation(cs[:], cT[:], ACT.Silu).then_inc(c_act, 1)

            @block.tensor
            def _(pe):
                pe.wait_ge(c_act, 1)
                for layer in range(2):
                    for o in range(6 * DC):
                        col = (layer * 6 * DC + o) * NB
                        for k in range(DC):
                            mm = nc.tensor.matmul(ps[:, col:col + NB], wm[:, layer, k, o * P:(o + 1) * P],
                                                  cs[:, k, layer, :], start=(k == 0), stop=(k == DC - 1))
                mm.then_inc(mod_ps, 1)

            @block.vector
            def _(dve):
                dve.wait_ge(mod_ps, 1)
                nc.vector.tensor_copy(mod[:].rearrange("p l w k b -> p (l w k b)"),
                                      ps[:, 0:2 * 6 * DC * NB]).then_inc(mod_sb, 1)
                dve.wait_ge(mod_sb, 1)
                for j, w in enumerate((GA, GB)):
                    nc.vector.tensor_scalar(sgn[:, j], mod[:, :, w], 0.0, 2.0, ALU.is_ge, ALU.mult).then_inc(gate_parts, 1)
                    for layer in range(2):
                        nc.vector.scalar_tensor_tensor(mag[:, j, layer], mod[:, layer, w], -1.0, mod[:, layer, w],
                                                       ALU.mult, ALU.max).then_inc(gate_parts, 1)
                dve.wait_ge(gate_parts, 6)
                nc.vector.tensor_scalar(mag[:], mag[:], 0.25, None, ALU.max).then_inc(gate_parts, 1)
                dve.wait_ge(gate_parts, 7)
                for j, w in enumerate((GA, GB)):
                    for layer in range(2):
                        nc.vector.scalar_tensor_tensor(mod[:, layer, w], sgn[:, j, layer], -1.0, mag[:, j, layer],
                                                       ALU.add, ALU.mult).then_inc(done, 1)
                for w in (CA, CB):
                    nc.vector.tensor_scalar(mod[:, :, w], mod[:, :, w], 1.0, None, ALU.add).then_inc(done, 1)
                dve.wait_ge(done, 6)


def layernorm(core, tag, src, dst, scale, bias, ahead):
    nc, PS = core.nc, core.PS
    mean, centred, squared, var, logged, rstd, normed, done = (
        core.sem(f"{tag}_{n}") for n in ("mean", "centred", "squared", "var", "logged", "rstd", "normed", "done"))
    with ExitStack() as st:
        sb = lambda n, sh: st.enter_context(nc.sbuf_tensor(f"{tag}_{n}", sh, F32))
        xc = [[sb(f"xc{k}{b}", [P, DC, T]) for b in range(NB)] for k in range(2)]
        sq = [sb(f"sq{b}", [P, DC, T]) for b in range(NB)]
        ln = [sb(f"ln{b}", [P, T]) for b in range(NB)]
        rs = [sb(f"rs{b}", [P, T]) for b in range(NB)]
        with nc.Block() as block:

            @block.sync
            def _(sp):
                ahead.start(sp)

            def pipeline(eng, first, behind, behind_first=False):
                def both(i, b, k):
                    if behind_first:
                        behind(i - 1, b, 1 - k)
                    first(i, b, k)
                    if not behind_first:
                        behind(i - 1, b, 1 - k)

                for b in range(NB):
                    first(0, b, 0)
                for b in range(NB):
                    both(1, b, 1)
                with eng.Fori(1, TPB // 2) as it:
                    for k in range(2):
                        for b in range(NB):
                            both(2 * it + k, b, k)
                for b in range(NB):
                    behind(TPB - 1, b, 1)

            def later(i, rounds):
                return not (isinstance(i, int) and i < rounds)

            @block.tensor
            def _(pe):
                def means(i, b, k):
                    if later(i, 2):
                        pe.wait_ge(centred, NB * (i - 2) + b + 1)
                    for c in range(DC):
                        mm = nc.tensor.matmul(PS[:, 2 * k + b], core.ones[:], src(c, b, i), start=(c == 0), stop=(c == DC - 1))
                    mm.then_inc(mean, 1)

                def variances(i, b, k):
                    pe.wait_ge(squared, NB * i + b + 1)
                    if later(i, 2):
                        pe.wait_ge(logged, NB * (i - 2) + b + 1)
                    for c in range(DC):
                        mm = nc.tensor.matmul(PS[:, 4 + 2 * k + b], core.ones[:], sq[b][:, c], start=(c == 0), stop=(c == DC - 1))
                    mm.then_inc(var, 1)

                pipeline(pe, means, variances)

            @block.vector
            def _(dve):
                def centre(i, b, k):
                    dve.wait_ge(mean, NB * i + b + 1)
                    if later(i, 2):
                        dve.wait_ge(done, NB * (i - 2) + b + 1)
                    for c in range(DC):
                        op = nc.vector.tensor_tensor(xc[k][b][:, c], src(c, b, i), PS[:, 2 * k + b], ALU.subtract)
                    op.then_inc(centred, 1)

                def scale_shift(i, b, k):
                    x = xc[k][b]
                    dve.wait_ge(rstd, NB * i + b + 1)
                    for c in range(DC):
                        op = nc.vector.tensor_tensor(x[:, c], x[:, c], rs[b][:], ALU.mult)
                    op.then_inc(normed, 1)
                    dve.wait_ge(normed, NB * i + b + 1)
                    for c in range(DC):
                        op = nc.vector.tensor_scalar(dst(c, b, i), x[:, c], scale(c, b), bias(c, b), ALU.mult, ALU.add)
                    op.then_inc(done, 1)

                pipeline(dve, centre, scale_shift)

            @block.scalar
            def _(act):
                nc.scalar.preload_act_table_set("natural_log_exp_and_others")

                def square(i, b, k):
                    act.wait_ge(centred, NB * i + b + 1)
                    if later(i, 1):
                        act.wait_ge(var, NB * (i - 1) + b + 1)
                    nc.scalar.activation(sq[b][:], xc[k][b][:], ACT.Square).then_inc(squared, 1)

                def root(i, b, k):
                    act.wait_ge(var, NB * i + b + 1)
                    nc.scalar.activation(ln[b][:], PS[:, 4 + 2 * k + b], ACT.Ln, bias=core.eps[:]).then_inc(logged, 1)
                    act.wait_ge(logged, NB * i + b + 1)
                    if later(i, 1):
                        act.wait_ge(normed, NB * (i - 1) + b + 1)
                    nc.scalar.activation(rs[b][:], ln[b][:], ACT.Exp, scale=-0.5).then_inc(rstd, 1)

                pipeline(act, square, root, behind_first=True)



NH0 = 16
HD0 = D // NH0
HPC = P // HD0
MS0 = HD0 // 2
NBLK = S // P
TB = T // P
Q_PARTS = (0, 0, 0, 1, 2, 1)
K_PARTS = (0, 1, 2, 0, 0, 1)
STK = len(Q_PARTS) * HD0
AUG = STK + 3
RING = 3
P1_TO, O_COST, S_FIX = 0.92, 0.85, 0.2


def attn0_project_weights(core, st):
    io = core.io
    square = [P, DC, D]
    return Weights(core, st, "a0p_", [
        ("wq", square, [(WHOLE, by_chunk(io["wqT"]))]), ("wk", square, [(WHOLE, by_chunk(io["wkT"]))]),
        ("wv", square, [(WHOLE, by_chunk(io["wvT"]))]),
        ("wc", [P, DC, P], [(WHOLE, io["wc_bd"].rearrange("k p o -> p k o"))]),
        ("wm", [P, DC, P], [(WHOLE, io["shift_bd"].rearrange("k p o -> p k o"))]),
        ("bq", [P, DC], [(WHOLE, io["bq"])]), ("bk", [P, DC], [(WHOLE, io["bk"])]), ("gate", [P, DC], [(WHOLE, io["gate_rep"])])])


def attn0_project(core, H, VV, W):
    nc, io, PS = core.nc, core.io, core.PS
    names = ("sig mixed hs_ready q_ps k_ps qt_ps v_ps q_sb k_sb hi_q hi_k rest_q rest_k mid_q mid_k lo_q lo_k "
             "v_sb zeroed table")
    sig, mixed, hs_ready, q_ps, k_ps, qt_ps, v_ps, q_sb, k_sb, hi_q, hi_k, rest_q, rest_k, mid_q, mid_k, lo_q, \
        lo_k, v_sb, zeroed, table = (core.sem("a0p_" + n) for n in names.split())
    parts_out = [core.sem(f"a0p_parts_out{b}") for b in range(NB)]
    tick = core.sem("a0p_tick")
    with ExitStack() as st:
        sb = lambda n, sh, d=F32: st.enter_context(nc.sbuf_tensor("a0p_" + n, sh, d))
        wq, wk, wv, bq, bk, gate, wc, wm = (W.buf[n] for n in "wq wk wv bq bk gate wc wm".split())
        g = sb("g", [P, DC])
        A = sb("A", [P, DC, P])
        Hs = [sb(f"Hs{b}", [P, DC, T]) for b in range(NB)]
        qsb = [sb(f"qsb{b}", [P, DC, T]) for b in range(NB)]
        ksb = [sb(f"ksb{b}", [P, DC, T]) for b in range(NB)]
        rest = [sb(f"rest{b}", [P, 2, DC, T]) for b in range(NB)]
        parts = [sb(f"parts{b}", [P, 2, 3, DC, T], BF16) for b in range(NB)]
        with nc.Block() as block:

            @block.sync
            def _(sp):
                with sp.Fori(0, TPB) as i:
                    for b in range(NB):
                        for w, ready in ((0, lo_q), (1, lo_k)):
                            sp.wait_ge(ready, NB * i + b + 1)
                            for part in range(3):
                                dst = core.qk_parts[w, b, part].rearrange("(c p) s -> p c s", p=P)[:, :, bass.ds(i * T, T)]
                                sp.dma_start(dst, parts[b][:, w, part]).then_inc(parts_out[b], 16)
                for b in range(NB):
                    sp.wait_ge(parts_out[b], 96 * (TPB + 1))

            @block.gpsimd
            def _(pool):
                nc.gpsimd.memset(VV[:], 1.0).then_inc(zeroed, 1)
                def copy_h(i, b):
                    pool.wait_ge(v_sb, NB * i + b + 1)
                    pool.sem_inc(tick, 1)
                    nc.gpsimd.tensor_copy(Hs[b][:], H[:, :, tok(b, i)]).then_inc(hs_ready, 1)

                def middle(i, b):
                    for w, r, m in ((1, rest_k, mid_k), (0, rest_q, mid_q)):
                        pool.wait_ge(r, NB * i + b + 2)
                        pool.sem_inc(tick, 1)
                        nc.gpsimd.tensor_copy(parts[b][:, w, 1], rest[b][:, w]).then_inc(m, 1)

                pool.sem_inc(rest_k, 1)
                copy_h(0, 0)
                with pool.Fori(0, TPB - 1) as i:
                    copy_h(i, 1)
                    middle(i, 0)
                    copy_h(i + 1, 0)
                    middle(i, 1)
                copy_h(TPB - 1, 1)
                middle(TPB - 1, 0)
                middle(TPB - 1, 1)

            @block.scalar
            def _(act):
                for b in range(NB):
                    act.sem_inc(parts_out[b], 96)
                act.wait_ge(W.loaded, W.all)
                nc.scalar.activation(g[:], gate[:], ACT.Sigmoid).then_inc(sig, 1)
                with act.Fori(0, TPB) as i:
                    for b in range(NB):
                        act.wait_ge(q_ps, NB * i + b + 1)
                        for c in range(DC):
                            op = nc.scalar.activation(qsb[b][:, c], PS[:, c], ACT.Identity, bias=bq[:, c:c + 1])
                        op.then_inc(q_sb, 1)
                        act.wait_ge(k_ps, NB * i + b + 1)
                        for c in range(DC):
                            op = nc.scalar.activation(ksb[b][:, c], PS[:, 2 + c], ACT.Identity, bias=bk[:, c:c + 1])
                        op.then_inc(k_sb, 1)
                        act.wait_ge(parts_out[b], 96 * (i + 1))
                        act.wait_ge(k_sb, NB * i + b + 2)
                        nc.scalar.copy(parts[b][:, 1, 0], ksb[b][:]).then_inc(hi_k, 1)
                        act.wait_ge(qt_ps, NB * i + b + 1)
                        nc.scalar.copy(parts[b][:, 0, 0], PS[:, 4:6]).then_inc(hi_q, 1)

            @block.vector
            def _(dve):
                dve.sem_inc(v_sb, NB)
                dve.wait_ge(sig, 1)
                nc.vector.tensor_tensor(wc[:], wc[:], wm[:], ALU.subtract).then_inc(mixed, 1)
                dve.wait_ge(mixed, 1)
                for c in range(DC):
                    nc.vector.scalar_tensor_tensor(A[:, c], wc[:, c], g[:, c:c + 1], wm[:, c], ALU.mult, ALU.add).then_inc(mixed, 1)
                dve.wait_ge(mixed, 1 + DC)
                nc.vector.tensor_scalar(A[:], A[:], float(HD0) ** -0.5, None, ALU.mult).then_inc(mixed, 1)
                dve.wait_ge(zeroed, 1)
                with dve.Fori(0, TPB) as i:
                    for b in range(NB):
                        dve.wait_ge(hi_k, NB * i + b + 1)
                        nc.vector.tensor_tensor(rest[b][:, 1], ksb[b][:], parts[b][:, 1, 0], ALU.subtract).then_inc(rest_k, 1)
                        dve.wait_ge(v_ps, NB * i + b + 1)
                        for j in range(2):
                            dst = VV[:, b, bass.ds(i * TB + 2 * j, 2), :, 0:HD0]
                            op = nc.vector.tensor_copy(dst, PS[:, 6 + j].rearrange("p (k h f) -> p k h f", k=2, h=NH0))
                        op.then_inc(v_sb, 1)
                        dve.wait_ge(hi_q, NB * i + b + 1)
                        nc.vector.tensor_tensor(rest[b][:, 0], PS[:, 4:6], parts[b][:, 0, 0], ALU.subtract).then_inc(rest_q, 1)
                        dve.wait_ge(mid_k, NB * i + b + 1)
                        nc.vector.tensor_tensor(parts[b][:, 1, 2], rest[b][:, 1], parts[b][:, 1, 1], ALU.subtract).then_inc(lo_k, 1)
                        dve.wait_ge(mid_q, NB * i + b + 1)
                        nc.vector.tensor_tensor(parts[b][:, 0, 2], rest[b][:, 0], parts[b][:, 0, 1], ALU.subtract).then_inc(lo_q, 1)

            @block.tensor
            def _(pe):
                pe.wait_ge(W.loaded, W.all)
                pe.wait_ge(mixed, 2 + DC)
                pe.sem_inc(k_sb, 1)
                pe.sem_inc(rest_q, 1)
                with pe.Fori(0, TPB) as i:
                    for b in range(NB):
                        for c in range(DC):
                            for k in range(DC):
                                mm = nc.tensor.matmul(PS[:, c], wq[:, k, c * P:(c + 1) * P], H[:, k, tok(b, i)],
                                                      start=(k == 0), stop=(k == DC - 1))
                        mm.then_inc(q_ps, 1)
                        pe.wait_ge(k_sb, NB * i + b + 1)
                        for c in range(DC):
                            for k in range(DC):
                                mm = nc.tensor.matmul(PS[:, 2 + c], wk[:, k, c * P:(c + 1) * P], H[:, k, tok(b, i)],
                                                      start=(k == 0), stop=(k == DC - 1))
                        mm.then_inc(k_ps, 1)
                        pe.wait_ge(hs_ready, NB * i + b + 1)
                        pe.wait_ge(v_sb, NB * i + b + NB)
                        for j in range(TB):
                            for k in range(DC):
                                mm = nc.tensor.matmul(PS[:, 6 + j // 2, (j % 2) * D:(j % 2 + 1) * D],
                                                      Hs[b][:, k, j * P:(j + 1) * P], wv[:, k],
                                                      start=(k == 0), stop=(k == DC - 1))
                        mm.then_inc(v_ps, 1)
                        pe.wait_ge(q_sb, NB * i + b + 1)
                        pe.wait_ge(rest_q, NB * i + b + 1)
                        for c in range(DC):
                            mm = nc.tensor.matmul(PS[:, 4 + c], A[:, c], qsb[b][:, c], start=True, stop=True)
                        mm.then_inc(qt_ps, 1)


def attn0_scores(core, VV):
    nc, PS = core.nc, core.PS
    ST = NH0
    names = "ones_set vu mx_set p1_ps p1_read mx neg part m_ps m_sb m_in s_ps exp_done pv_done o_sb"
    ones_set, vu, mx_set, p1_ps, p1_read, mx_s, neg_s, part_s, m_ps, m_sb, m_in, s_ps, exp_done, pv_done, o_sb = (
        core.sem("a0s_" + n) for n in names.split())
    stack_in = [[core.sem(f"a0s_stack_in{p}{b}") for b in range(NB)] for p in range(RING)]
    o_out = core.sem("a0s_o_out")
    tick = core.sem("a0s_tick")
    N_IN = 16 * 6
    N_P1 = NB * (sum((q // 4 + 1) for q in range(NBLK)) + 1)
    N_S2 = NB * (NBLK + NBLK // 2)
    N_PV = NB * NBLK
    N_OUT = 16 * NB * 8
    with ExitStack() as st:
        sb = lambda n, sh, d=F32: st.enter_context(nc.sbuf_tensor("a0s_" + n, sh, d))
        QS = [[sb(f"QS{p}{b}", [AUG, S], BF16) for b in range(NB)] for p in range(RING)]
        KS = [[sb(f"KS{p}{b}", [AUG, S], BF16) for b in range(NB)] for p in range(RING)]
        VU = [[sb(f"VU{p}{b}", [P, NBLK, HD0 + 1]) for b in range(NB)] for p in range(RING)]
        PT = [[sb(f"PT{b}{k}", [P, S]) for k in range(2)] for b in range(NB)]
        mx = [sb(f"mx{b}", [P, NBLK, 4]) for b in range(NB)]
        rowmax = [sb(f"rowmax{b}", [P, NBLK]) for b in range(NB)]
        rest = [sb(f"rest{b}", [P, NBLK]) for b in range(NB)]
        mparts = [sb(f"mparts{b}", [P, P // NBLK, NBLK], BF16) for b in range(NB)]
        mrow = [sb(f"mrow{b}", [3 * NBLK, P], BF16) for b in range(NB)]
        O = [sb(f"O{b}", [P, T]) for b in range(NB)]

        rounds = (ST - RING) // RING

        def stages(eng, stage):
            with eng.Fori(0, rounds) as it:
                for r in range(RING):
                    stage(RING * it + r, r, it, True, True)
            for n in range(rounds * RING, ST):
                stage(n, n % RING, n // RING, n + 1 < ST, n + RING < ST)

        def pass1_blocks():
            for b in range(NB):
                for q in range(NBLK):
                    for j in range(q // 4 + 1):
                        yield b, q, j
                    if b == 1 and q == 3:
                        yield 0, None, None
            yield 1, None, None

        P1 = list(pass1_blocks())
        assert len(P1) == N_P1

        def p2_groups(kt):
            return [g for g in range(2) if 1024 * (g + 1) > kt * P]

        def group(b, qc):
            return qc if b == 0 else 3 - qc

        G2 = {}
        for kt in range(NBLK):
            for b in range(NB):
                for g in p2_groups(kt):
                    G2[kt, b, g] = len(G2)
        assert len(G2) == N_S2

        def order(more):
            main = [("s", (0, b, g)) for b in range(NB) for g in range(2)]
            for kt in range(NBLK):
                groups = [("s", (kt + 1, b, g)) for b in range(NB) for g in p2_groups(kt + 1)] if kt + 1 < NBLK else []
                main += groups[:len(groups) // 2] + [("o", kt)] + groups[len(groups) // 2:]

            def weight(what, key):
                if what == "o":
                    return O_COST * (2 if key < 8 else 1)
                if what == "s":
                    kt, b, g = key
                    return S_FIX + (1024 * (g + 1) - max(kt * P, 1024 * g)) / 1200
                b, q, j = P1[key]
                return 0.15 + (P if q is None else min(T, (q + 1) * P - j * T)) / 960

            total, total_p = sum(weight(*m) for m in main), sum(weight("p", x) for x in range(N_P1))
            done = done_p = 0.0
            x = 0
            for m in main:
                while more and x < N_P1 and done_p / total_p <= done / total / P1_TO:
                    yield "p", x
                    done_p += weight("p", x)
                    x += 1
                yield m
                done += weight(*m)
            assert not more or x == N_P1

        def load(dma, par, b, h):
            rows = bass.ds(h * HD0, HD0)
            q, k = core.qk_parts[0, b], core.qk_parts[1, b]
            qs, ks, done = QS[par][b], KS[par][b], stack_in[par][b]
            dma(qs[0:3 * HD0, :], q[0:1, rows, :].broadcast_to([3, HD0, S])).then_inc(done, 16)
            dma(qs[3 * HD0:5 * HD0, :], q[1:3, rows, :]).then_inc(done, 16)
            dma(qs[5 * HD0:6 * HD0, :], q[1, rows, :]).then_inc(done, 16)
            dma(ks[0:3 * HD0, :], k[:, rows, :]).then_inc(done, 16)
            dma(ks[3 * HD0:4 * HD0, :], k[0, rows, :]).then_inc(done, 16)
            dma(ks[4 * HD0:6 * HD0, :], k[0:2, rows, :]).then_inc(done, 16)

        with nc.Block() as block:

            @block.sync
            def _(sp):
                def maxima(n, par):
                    for b in range(NB):
                        sp.wait_ge(m_sb, NB * n + b + 1)
                        for j in range(3):
                            dst = QS[par][b][STK + j:STK + j + 1, :].rearrange("o (q c) -> o q c", c=P)
                            src = mrow[b][j * NBLK:(j + 1) * NBLK, :]
                            sp.dma_start(dst, src).then_inc(m_in, 16)

                for r in range(RING):
                    load(sp.dma_start, r, 0, r)
                maxima(0, 0)

                def stage(n, r, it, more, ahead):
                    if more:
                        maxima(n + 1, (r + 1) % RING)
                    if ahead:
                        sp.wait_ge(pv_done, N_PV * (n + 1) + 4)
                        load(sp.dma_start, r, 0, n + RING)
                    for b in range(NB):
                        sp.wait_ge(o_sb, NB * n + b + 2)
                        for qc in range(4):
                            row = 32 * group(b, qc)
                            sp.dma_start(core.o_dram[b, bass.ds(n, 1), :, qc * T:(qc + 1) * T].rearrange("o f t -> (o f) t"),
                                         O[b][row:row + HD0, :]).then_inc(o_out, 16)
                            sp.dma_start(core.sum_dram[b, bass.ds(n, 1), qc * T:(qc + 1) * T],
                                         O[b][row + HD0:row + HD0 + 1, :]).then_inc(o_out, 16)

                stages(sp, stage)
                sp.wait_ge(o_out, N_OUT * ST + 1)

            @block.gpsimd
            def _(pool):
                for r in range(RING):
                    load(pool.dma_start, r, 1, r)
                for b in range(NB):
                    nc.gpsimd.tensor_copy(VU[0][b][:], VV[:, b, :, 0, :]).then_inc(vu, 1)

                def stage(n, r, it, more, ahead):
                    if more:
                        pool.wait_ge(pv_done, N_PV * n + 4)
                        pool.sem_inc(tick, 1)
                        for b in range(NB):
                            nc.gpsimd.tensor_copy(VU[(r + 1) % RING][b][:], VV[:, b, :, bass.ds(n + 1, 1), :].rearrange("p k o f -> p k (o f)")).then_inc(vu, 1)
                    if ahead:
                        pool.wait_ge(pv_done, N_PV * (n + 1) + 4)
                        load(pool.dma_start, r, 1, n + RING)

                stages(pool, stage)

            @block.vector
            def _(dve):
                for b in range(NB):
                    nc.vector.memset(mx[b][:], -3e38).then_inc(mx_set, 1)
                    nc.vector.memset(mparts[b][:], 0.0).then_inc(ones_set, 1)
                    for p in range(RING):
                        nc.vector.memset(KS[p][b][96:AUG, :], 1.0).then_inc(ones_set, 1)
                dve.wait_ge(mx_set, NB)
                dve.wait_ge(ones_set, (1 + RING) * NB)
                dve.sem_inc(p1_read, 2)
                dve.sem_inc(o_out, 1)

                def row_maxima(b, n):
                    nc.vector.tensor_reduce(rowmax[b][:], mx[b][:], AX_X, ALU.max).then_inc(mx_s, 1)
                    dve.wait_ge(mx_s, NB * n + b + 1)
                    nc.vector.tensor_scalar(mparts[b][:, 0], rowmax[b][:], -1.0, None, ALU.mult).then_inc(part_s, 1)
                    dve.wait_ge(part_s, 3 * (NB * n + b) + 1)
                    nc.vector.scalar_tensor_tensor(rest[b][:], rowmax[b][:], -1.0, mparts[b][:, 0], ALU.mult, ALU.subtract).then_inc(neg_s, 1)
                    dve.wait_ge(neg_s, NB * n + b + 1)
                    nc.vector.tensor_copy(mparts[b][:, 1], rest[b][:]).then_inc(part_s, 1)
                    dve.wait_ge(part_s, 3 * (NB * n + b) + 2)
                    nc.vector.tensor_tensor(mparts[b][:, 2], rest[b][:], mparts[b][:, 1], ALU.subtract).then_inc(part_s, 1)

                def pass1(n):
                    for x, (b, q, j) in enumerate(P1):
                        dve.wait_ge(p1_ps, N_P1 * n + x + 1)
                        ps = PS[:, 6 + x % 2]
                        if q is None:
                            nc.vector.tensor_copy(mrow[b][:], ps.bitcast(BF16)[0:3 * NBLK, 0:P]).then_inc(m_sb, 1)
                            dve.wait_ge(m_sb, NB * n + b + 1)
                            dve.sem_inc(p1_read, 1)
                            continue
                        w = min(T, (q + 1) * P - j * T)
                        nc.vector.tensor_reduce(mx[b][:, q, j:j + 1], ps[:, 0:w], AX_X, ALU.max).then_inc(p1_read, 1)
                        if q == NBLK - 1 and j == 3:
                            dve.wait_ge(p1_read, N_P1 * n + x + 1 + 2)
                            row_maxima(b, n)

                pass1(0)

                def stage(n, r, it, more, ahead):
                    if more:
                        pass1(n + 1)
                    for b in range(NB):
                        dve.wait_ge(pv_done, N_PV * (n + 1) - NB + b + 1 + 4)
                        if b == 0:
                            dve.wait_ge(o_out, N_OUT * n + 1)
                        nc.vector.tensor_copy(O[b][:], PS[:, b]).then_inc(o_sb, 1)

                stages(dve, stage)

            @block.scalar
            def _(act):
                nc.scalar.preload_act_table_set("exp_and_others")
                act.sem_inc(exp_done, 2)

                def stage(n, r, it, more, ahead):
                    for kt in range(NBLK):
                        for b in range(NB):
                            act.wait_ge(pv_done, N_PV * n + 2 * kt + b + 1)
                            for g in p2_groups(kt):
                                x = G2[kt, b, g]
                                act.wait_ge(s_ps, N_S2 * n + x + 1)
                                lo = max(kt * P - 1024 * g, 0)
                                src = PS[:, 2 + 2 * (x % 2):4 + 2 * (x % 2)].rearrange("p a t -> p (a t)")
                                nc.scalar.activation(PT[b][kt % 2][:, 1024 * g + lo:1024 * (g + 1)], src[:, lo:1024],
                                                     ACT.Exp).then_inc(exp_done, 1)

                stages(act, stage)

            @block.tensor
            def _(pe):
                pe.sem_inc(pv_done, 4)
                pe.sem_inc(o_sb, 1)

                def pass1(n, par, x):
                    b, q, j = P1[x]
                    pe.wait_ge(p1_read, N_P1 * n + x + 1)
                    ps = PS[:, 6 + x % 2]
                    if q is None:
                        pe.wait_ge(part_s, 3 * (NB * n + b + 1))
                        nc.tensor.transpose(ps.bitcast(BF16)[:, 0:P], mparts[b][:].rearrange("p a q -> p (a q)"),
                                            core.identb[:]).then_inc(p1_ps, 1)
                        return
                    w = min(T, (q + 1) * P - j * T)
                    diag = j == q // 4
                    if diag:
                        nc.tensor.matmul(ps[:, w - P:w], core.lower[:], core.mask[:, ABOVE], start=True, stop=True)
                    nc.tensor.matmul(ps[:, 0:w], QS[par][b][0:STK, q * P:(q + 1) * P], KS[par][b][0:STK, j * T:j * T + w],
                                     start=not diag, stop=True, skip_group_check=diag).then_inc(p1_ps, 1)

                def pass2(n, par, kt, b, g):
                    x = G2[kt, b, g]
                    pe.wait_ge(exp_done, N_S2 * n + x + 1)
                    for qc in (2 * g, 2 * g + 1):
                        lo = max(kt * P, qc * T)
                        if lo >= (qc + 1) * T:
                            continue
                        ps = PS[:, 2 + 2 * (x % 2) + qc % 2]
                        diag = kt // 4 == qc
                        if diag:
                            nc.tensor.matmul(ps[:, lo - qc * T:lo - qc * T + P], core.lower[:], core.mask[:, BELOW],
                                             start=True, stop=True)
                        mm = nc.tensor.matmul(ps[:, lo - qc * T:T], KS[par][b][:, kt * P:(kt + 1) * P],
                                              QS[par][b][:, lo:(qc + 1) * T], start=not diag, stop=True,
                                              skip_group_check=diag)
                    mm.then_inc(s_ps, 1)

                def pv(n, par, kt):
                    for b in range(NB):
                        pe.wait_ge(exp_done, N_S2 * n + G2[kt, b, 1] + 1 + 2)
                        if kt == 0:
                            pe.wait_ge(o_sb, NB * n + 1)
                        for qc in range(kt // 4, 4):
                            lo = max(kt * P, qc * T)
                            r = 32 * group(b, qc)
                            mm = nc.tensor.matmul(PS[r:r + HD0 + 1, b, lo - qc * T:T], VU[par][b][:, kt],
                                                  PT[b][kt % 2][:, lo:(qc + 1) * T], start=(kt == 0), stop=(kt >= 4 * qc),
                                                  skip_group_check=(kt > 4 * qc))
                        mm.then_inc(pv_done, 1)

                for b in range(NB):
                    pe.wait_ge(stack_in[0][b], N_IN)
                pe.wait_ge(ones_set, (1 + RING) * NB)
                for x in range(N_P1):
                    pass1(0, 0, x)

                def stage(n, r, it, more, ahead):
                    pe.wait_ge(m_in, 16 * 3 * NB * (n + 1))
                    pe.wait_ge(vu, NB * (n + 1))
                    for what, key in order(more):
                        if what == "s":
                            pass2(n, r, *key)
                        elif what == "o":
                            pv(n, r, key)
                        else:
                            b = P1[key][0]
                            if key in (0, P1.index((1, 0, 0))):
                                pe.wait_ge(stack_in[(r + 1) % RING][b], N_IN * (it + 1 + (r + 1) // RING))
                            pass1(n + 1, (r + 1) % RING, key)

                stages(pe, stage)


def attn0_out(core):
    nc, io, PS, X = core.nc, core.io, core.PS, core.X
    w_in, sums_in, recip, recip_out, gbo_s, o_ready, o_ps, o_sb, x_done = (
        core.sem("a0o_" + n) for n in "w_in sums_in recip recip_out gbo normed o_ps o_sb x_done".split())
    tile_in = [core.sem(f"a0o_tile_in{b}") for b in range(NB)]
    with ExitStack() as st:
        sb = lambda n, sh, d=F32: st.enter_context(nc.sbuf_tensor("a0o_" + n, sh, d))
        wo, bv, bo, gbo = sb("wo", [P, DC, D]), sb("bv", [P, DC]), sb("bo", [P, DC]), sb("gbo", [P, DC, NB])
        sums = sb("sums", [P, NB * NH0 * S // P])
        oh = [sb(f"oh{b}", [P, DC, T]) for b in range(NB)]
        o = [sb(f"o{b}", [P, DC, T]) for b in range(NB)]
        r = [sb(f"r{b}", [P, DC, T]) for b in range(NB)]
        y = [sb(f"y{b}", [P, DC, T]) for b in range(NB)]
        with nc.Block() as block:

            @block.sync
            def _(sp):
                sp.dma_start(sums[:], core.sum_dram.rearrange("b h (a t) -> (b h a) t", a=4)).then_inc(sums_in, 16)
                sp.dma_start(wo[:], io["woT"].rearrange("(k p) o -> p k o", p=P)).then_inc(w_in, 16)
                sp.dma_start(bv[:], io["bv"]).then_inc(w_in, 16)
                sp.dma_start(bo[:], io["bo"]).then_inc(w_in, 16)
                sp.wait_ge(recip, 1)
                sp.dma_start(core.recip_dram.rearrange("b h (a t) -> (b h a) t", a=4), sums[:]).then_inc(recip_out, 16)
                sp.wait_ge(recip_out, 16)

                def load(i, b):
                    for c in range(DC):
                        heads = slice(c * HPC, (c + 1) * HPC)
                        src = core.o_dram[b, heads].rearrange("h f s -> (h f) s")[:, bass.ds(i * T, T)]
                        sp.dma_start(oh[b][:, c], src).then_inc(tile_in[b], 16)
                        src = core.recip_dram[b, heads, bass.ds(i * T, T)].unsqueeze(1).broadcast_to([HPC, HD0, T])
                        sp.dma_start(r[b][:, c], src).then_inc(tile_in[b], 16)

                for b in range(NB):
                    load(0, b)
                with sp.Fori(1, TPB) as i:
                    for b in range(NB):
                        sp.wait_ge(o_ready, 2 * (NB * (i - 1) + b) + 1)
                        load(i, b)

            @block.vector
            def _(dve):
                dve.wait_ge(sums_in, 16)
                nc.vector.reciprocal(sums[:], sums[:]).then_inc(recip, 1)
                dve.wait_ge(w_in, 48)
                for b in range(NB):
                    nc.vector.tensor_tensor(gbo[:, :, b], core.mod[:, 0, GA, :, b], bo[:], ALU.mult).then_inc(gbo_s, 1)

                def prepare(i, b):
                    dve.wait_ge(tile_in[b], 64 * (i + 1))
                    dve.wait_ge(o_ps, NB * i + b + 1)
                    nc.vector.tensor_tensor(o[b][:], oh[b][:], r[b][:], ALU.mult).then_inc(o_ready, 1)
                    dve.wait_ge(o_ready, 2 * (NB * i + b) + 1)
                    for c in range(DC):
                        op = nc.vector.tensor_scalar(o[b][:, c], o[b][:, c], bv[:, c:c + 1], None, ALU.add)
                    op.then_inc(o_ready, 1)

                def add(i, b):
                    dve.wait_ge(o_sb, NB * i + b + 2)
                    nc.vector.tensor_tensor(X[:, :, tok(b, i)], X[:, :, tok(b, i)], y[b][:], ALU.add).then_inc(x_done, 1)

                prepare(0, 0)
                with dve.Fori(0, TPB - 1) as i:
                    prepare(i, 1)
                    add(i, 0)
                    prepare(i + 1, 0)
                    add(i, 1)
                prepare(TPB - 1, 1)
                add(TPB - 1, 0)
                add(TPB - 1, 1)

            @block.tensor
            def _(pe):
                pe.sem_inc(o_ps, NB)
                pe.wait_ge(w_in, 48)
                pe.sem_inc(o_sb, 1)
                with pe.Fori(0, TPB) as i:
                    for b in range(NB):
                        pe.wait_ge(o_ready, 2 * (NB * i + b + 1))
                        pe.wait_ge(o_sb, NB * i + 1)
                        for c in range(DC):
                            for k in range(DC):
                                mm = nc.tensor.matmul(PS[:, 2 * b + c], wo[:, k, c * P:(c + 1) * P], o[b][:, k],
                                                      start=(k == 0), stop=(k == DC - 1))
                        mm.then_inc(o_ps, 1)

            @block.scalar
            def _(act):
                act.wait_ge(gbo_s, NB)
                act.sem_inc(x_done, 1)
                with act.Fori(0, TPB) as i:
                    for b in range(NB):
                        act.wait_ge(o_ps, NB * i + b + 1 + NB)
                        act.wait_ge(x_done, NB * i + 1)
                        for c in range(DC):
                            op = nc.scalar.activation(y[b][:, c], PS[:, 2 * b + c], ACT.Identity,
                                                      bias=gbo[:, c, b:b + 1], scale=core.mod[:, 0, GA, c, b:b + 1])
                        op.then_inc(o_sb, 1)



FH = 1024
FC = FH // P


def ffn0_weights(core, st):
    io = core.io
    return Weights(core, st, "f0_", [
        ("w1", [P, DC, FH], [(WHOLE, by_chunk(io["w1T"]))]), ("w2", [P, DC, FH], [(WHOLE, by_chunk(io["w2T"]))]),
        ("s1", [P, FC], [(WHOLE, io["w1s"])]), ("s2", [P, FC], [(WHOLE, io["w2s"])]), ("sh1", [P, FC], [(WHOLE, io["h1s"])]),
        ("sh2", [P, FC], [(WHOLE, io["h2s"])]), ("s3", [P, DC], [(WHOLE, io["w3s"])])])


def ffn0(core, H, W):
    nc, io, PS, X = core.nc, core.io, core.PS, core.X
    scales, pair_ps, tanh_s, half_s, gate_s, h1_ps, h1_s, h2_ps, h2_s, w3_ps, x_done = (
        core.sem("f0_" + n) for n in
        "scales pair_ps tanh half gate h1_ps h1 h2_ps h2 w3_ps x_done".split())
    in_h1, in_h2, in_w3 = (core.sem("f0_in_" + n) for n in ("h1", "h2", "w3"))
    with ExitStack() as st:
        sb = lambda n, sh, d=F32: st.enter_context(nc.sbuf_tensor("f0_" + n, sh, d))
        w1, w2, s1, s2, sh1, sh2, s3 = (W.buf[n] for n in "w1 w2 s1 s2 sh1 sh2 s3".split())
        h1, h2 = sb("h1", [P, FC, FH]), sb("h2", [P, FC, FH])
        w3 = sb("w3", [P, FC, D])
        s1h, s12 = sb("s1h", [P, FC]), sb("s12", [P, FC])
        g3 = sb("g3", [P, DC, NB])
        hA, hB = sb("hA", [P, FC, T]), sb("hB", [P, FC, T])
        th = [sb(f"th{k}", [P, T]) for k in range(2)]
        hf = [sb(f"hf{k}", [P, T]) for k in range(2)]
        with nc.Block() as block:

            @block.sync
            def _(sp):
                for t, name, ready in ((h1, "h1T", in_h1), (h2, "h2T", in_h2), (w3, "w3T", in_w3)):
                    sp.dma_start(t[:], io[name].rearrange("(k p) o -> p k o", p=P)).then_inc(ready, 16)

            @block.tensor
            def _(pe):
                def dense(bank, w, x, o, n_k, done):
                    for k in range(n_k):
                        mm = nc.tensor.matmul(PS[:, bank], w[:, k, o * P:(o + 1) * P], x[:, k], start=(k == 0), stop=(k == n_k - 1))
                    mm.then_inc(done, 1)

                pe.wait_ge(W.loaded, W.all)
                pe.sem_inc(x_done, 1)
                with pe.Fori(0, TPB) as i:
                    for b in range(NB):
                        u = NB * i + b
                        h = H[:, :, tok(b, i)]
                        for o in range(FC):
                            if o >= 2:
                                pe.wait_ge(gate_s, FC * u + o - 1)
                            dense(2 * (o % 2), w1, h, o, DC, pair_ps)
                            dense(2 * (o % 2) + 1, w2, h, o, DC, pair_ps)
                        pe.wait_ge(gate_s, FC * (u + 1))
                        pe.wait_ge(in_h1, 16)
                        pe.wait_ge(x_done, u + 1)
                        for o in range(FC):
                            if o >= 2:
                                pe.wait_ge(h1_s, FC * u + o - 1)
                            dense(4 + o % 2, h1, hA, o, FC, h1_ps)
                        pe.wait_ge(h1_s, FC * (u + 1))
                        pe.wait_ge(in_h2, 16)
                        for o in range(FC):
                            if o >= 2:
                                pe.wait_ge(h2_s, FC * u + o - 1)
                            dense(6 + o % 2, h2, hB, o, FC, h2_ps)
                        pe.wait_ge(h2_s, FC * (u + 1))
                        pe.wait_ge(in_w3, 16)
                        for o in range(DC):
                            dense(4 + o, w3, hA, o, FC, w3_ps)

            @block.scalar
            def _(act):
                nc.scalar.preload_act_table_set("gelu_and_others")
                act.wait_ge(scales, 1)
                with act.Fori(0, TPB) as i:
                    for b in range(NB):
                        u = NB * i + b
                        for o in range(FC):
                            act.wait_ge(pair_ps, 2 * (FC * u + o) + 1)
                            nc.scalar.activation(th[o % 2][:], PS[:, 2 * (o % 2)], ACT.Tanh, scale=s1h[:, o:o + 1]).then_inc(tanh_s, 1)
                        for o in range(FC):
                            act.wait_ge(h1_ps, FC * u + o + 1)
                            nc.scalar.activation(hB[:, o], PS[:, 4 + o % 2], ACT.Gelu, scale=sh1[:, o:o + 1]).then_inc(h1_s, 1)
                        for o in range(FC):
                            act.wait_ge(h2_ps, FC * u + o + 1)
                            nc.scalar.activation(hA[:, o], PS[:, 6 + o % 2], ACT.Gelu, scale=sh2[:, o:o + 1]).then_inc(h2_s, 1)

            @block.vector
            def _(dve):
                dve.wait_ge(W.loaded, W.all)
                for b in range(NB):
                    nc.vector.tensor_tensor(g3[:, :, b], core.mod[:, 0, GB, :, b], s3[:], ALU.mult)
                nc.vector.scalar_tensor_tensor(s12[:], s1[:], 0.5, s2[:], ALU.mult, ALU.mult)
                nc.vector.tensor_scalar(s1h[:], s1[:], 0.5, None, ALU.mult).then_inc(scales, 1)
                with dve.Fori(0, TPB) as i:
                    for b in range(NB):
                        u = NB * i + b
                        for o in range(FC):
                            dve.wait_ge(tanh_s, FC * u + o + 1)
                            g1, g2 = PS[:, 2 * (o % 2)], PS[:, 2 * (o % 2) + 1]
                            nc.vector.scalar_tensor_tensor(hf[o % 2][:], th[o % 2][:], 1.0, g1, ALU.add, ALU.mult).then_inc(half_s, 1)
                            dve.wait_ge(half_s, FC * u + o + 1)
                            dve.wait_ge(pair_ps, 2 * (FC * u + o + 1))
                            nc.vector.scalar_tensor_tensor(hA[:, o], hf[o % 2][:], s12[:, o:o + 1], g2, ALU.mult, ALU.mult).then_inc(gate_s, 1)
                        dve.wait_ge(w3_ps, DC * (u + 1))
                        for c in range(DC):
                            op = nc.vector.scalar_tensor_tensor(X[:, c, tok(b, i)], PS[:, 4 + c], g3[:, c, b:b + 1],
                                                                X[:, c, tok(b, i)], ALU.mult, ALU.add)
                        op.then_inc(x_done, 1)



NT = 1024
FO = 64
UC = 3 * D // P
BS = 64
NJ = S // BS
OW = 256
NI = S // OW
BPO = OW // BS
PAIRS = 4
LAG0 = -(BPO - 1)
LAG1 = NT // BS
LAGS = range(LAG0, LAG1 + 1)
JPAD = LAG1
HW = (len(LAGS) - 1) * BS + OW
KOFF = -LAG0 * BS + BS
KW = BS + HW
TWO_PI = 2.0 * np.pi
PI2_HI = float(np.float32(6.28125))
PI2_LO = float(TWO_PI - 6.28125)
ROUND = 1.5 * 2.0 ** 23
PI_IN = float(np.nextafter(np.float32(np.pi), np.float32(0)))


def filter_taps(core):
    nc, io, PS = core.nc, core.io, core.PS
    w_in, zeroed, ps_done, arg_s, sin_s, tap_ps, taps_s, out_s = (
        core.sem("ft_" + n) for n in "w_in zeroed ps arg sin tap_ps taps out".split())
    with ExitStack() as st:
        sb = lambda n, sh, d=F32: st.enter_context(nc.sbuf_tensor("ft_" + n, sh, d))
        z = sb("z", [3, NT])
        w = [sb("w1", [3, FO]), sb("w2", [FO, FO]), sb("w3", [FO, FO])]
        bf = sb("bf", [FO, 3, 2])
        wout = sb("wout", [FO, D])
        decay = sb("decay", [P, DC, NT])
        arg, turns, h = sb("arg", [FO, NT]), sb("turns", [FO, NT]), sb("h", [FO, NT])
        taps = sb("taps", [P, DC, KW])
        NH = NT // 512
        with nc.Block() as block:

            @block.sync
            def _(sp):
                loads = [(z[:], io["f_z"]), (bf[:], io["f_bf"]), (wout[:], io["f_wout"]),
                         (decay[:], io["f_decay"].rearrange("(c p) t -> p c t", p=P))]
                loads += [(w[k][:], io[f"f_w{k + 1}"]) for k in range(3)]
                for dst, src in loads:
                    sp.dma_start(dst, src).then_inc(w_in, 16)
                sp.wait_ge(taps_s, DC * NH)
                sp.wait_ge(zeroed, 1)
                sp.dma_start(core.kpad.rearrange("(c p) w -> p c w", p=P), taps[:]).then_inc(out_s, 16)
                sp.wait_ge(out_s, 16)

            @block.gpsimd
            def _(pool):
                nc.gpsimd.memset(taps[:], 0.0).then_inc(zeroed, 1)

            @block.tensor
            def _(pe):
                pe.wait_ge(w_in, 16 * 7)
                for layer in range(3):
                    x = z if layer == 0 else h
                    if layer:
                        pe.wait_ge(sin_s, layer)
                    for n in range(NH):
                        mm = nc.tensor.matmul(PS[0:FO, n], w[layer][:], x[:, n * 512:(n + 1) * 512], start=True, stop=True)
                    mm.then_inc(ps_done, 1)
                pe.wait_ge(sin_s, 3)
                for c in range(DC):
                    for n in range(NH):
                        mm = nc.tensor.matmul(PS[:, 2 + NH * c + n], wout[:, c * P:(c + 1) * P], h[:, n * 512:(n + 1) * 512],
                                              start=True, stop=True)
                mm.then_inc(tap_ps, 1)

            @block.vector
            def _(dve):
                dve.wait_ge(w_in, 16 * 7)
                n = 0

                def then(op):
                    nonlocal n
                    n += 1
                    op.then_inc(arg_s, 1)
                    dve.wait_ge(arg_s, n)

                for layer in range(3):
                    dve.wait_ge(ps_done, layer + 1)
                    ps = PS[0:FO, 0:NH].rearrange("p a t -> p (a t)")
                    then(nc.vector.tensor_scalar(arg[:], ps, bf[:, layer, 0:1], bf[:, layer, 1:2], ALU.add, ALU.mult))
                    then(nc.vector.tensor_scalar(turns[:], arg[:], 1.0 / TWO_PI, ROUND, ALU.mult, ALU.add))
                    then(nc.vector.tensor_scalar(turns[:], turns[:], ROUND, None, ALU.subtract))
                    then(nc.vector.scalar_tensor_tensor(arg[:], turns[:], -PI2_HI, arg[:], ALU.mult, ALU.add))
                    then(nc.vector.scalar_tensor_tensor(arg[:], turns[:], -PI2_LO, arg[:], ALU.mult, ALU.add))
                    then(nc.vector.tensor_scalar(arg[:], arg[:], PI_IN, -PI_IN, ALU.min, ALU.max))
                dve.wait_ge(tap_ps, 1)
                dve.wait_ge(zeroed, 1)
                for c in range(DC):
                    for k in range(NH):
                        at = slice(KOFF + k * 512, KOFF + (k + 1) * 512)
                        nc.vector.tensor_tensor(taps[:, c, at], PS[:, 2 + NH * c + k], decay[:, c, k * 512:(k + 1) * 512],
                                                ALU.mult).then_inc(taps_s, 1)

            @block.scalar
            def _(act):
                for layer in range(3):
                    act.wait_ge(arg_s, 6 * (layer + 1))
                    nc.scalar.activation(h[:], arg[:], ACT.Sin).then_inc(sin_s, 1)


def backwards(ap, start, n):
    return bass.AP(ap.tensor, ap.offset + start + n - 1, [list(ap.ap[0]), [-1, n]])


def conv_inputs_weights(core, st):
    io = core.io
    return Weights(core, st, "ci_", [
        ("wi", [P, DC, 3 * D], [(WHOLE, by_chunk(io["h_win"]))]), ("bi", [P, UC], [(WHOLE, io["h_bin"])]),
        ("fb", [P, UC], [(WHOLE, io["h_sfb"])]), ("fw", [P, UC, 3], [(WHOLE, io["h_sfw"])])])


def conv_inputs(core, H, V, X0, RR, W):
    nc, io, PS = core.nc, core.io, core.PS
    zeroed, pj_ps, pj_sb, tap_s, uc_s, v_s, tr_ps, rr_s, hist, v_free, turned = (
        core.sem("ci_" + n) for n in "zeroed pj_ps pj_sb tap uc v tr_ps rr hist v_free turned".split())
    with ExitStack() as st:
        sb = lambda n, sh, d=F32: st.enter_context(nc.sbuf_tensor("ci_" + n, sh, d))
        wi, bi, fb, fw = (W.buf[n] for n in "wi bi fb fw".split())
        U = [sb(f"U{b}", [P, UC, 2 + T]) for b in range(NB)]
        C = sb("C", [P, T])
        X1 = sb("X1", [P, DC, T])
        Vt = [sb(f"Vt{b}", [P, DC, T]) for b in range(NB)]
        NTR = DC * T // BS // 4

        with nc.Block() as block:

            @block.tensor
            def _(pe):
                pe.sem_inc(pj_sb, 1)
                def project(i, b, u):
                    for o in range(UC):
                        pe.wait_ge(pj_sb, UC * u + 1)
                        for k in range(DC):
                            mm = nc.tensor.matmul(PS[:, o], wi[:, k, o * P:(o + 1) * P], H[:, k, tok(b, i)],
                                                  start=(k == 0), stop=(k == DC - 1))
                        mm.then_inc(pj_ps, 1)

                def turn(b, u):
                    pe.wait_ge(v_s, DC * (u + 1))
                    for n in range(NTR):
                        pe.wait_ge(rr_s, NTR * u + n + 1)
                        pe.sem_inc(core.tick, 1)
                        for j in range(4):
                            c, blk = divmod(4 * n + j, T // BS)
                            mm = nc.tensor.transpose(PS[0:BS, 6 + n % 2, j * P:(j + 1) * P],
                                                     Vt[b][:, c, T - (blk + 1) * BS:T - blk * BS], core.ident[:])
                        mm.then_inc(tr_ps, 1)
                    pe.wait_ge(tr_ps, NTR * (u + 1))
                    pe.sem_inc(turned, NTR)

                pe.sem_inc(rr_s, 2)
                pe.sem_inc(turned, NTR * NB)
                pe.wait_ge(W.loaded, W.all)
                project(0, 0, 0)
                with pe.Fori(0, TPB - 1) as i:
                    project(i, 1, NB * i + 1)
                    turn(0, NB * i)
                    project(i + 1, 0, NB * i + 2)
                    turn(1, NB * i + 1)
                last = TPB - 1
                project(last, 1, NB * last + 1)
                turn(0, NB * last)
                turn(1, NB * last + 1)

            @block.scalar
            def _(act):
                act.wait_ge(W.loaded, W.all)
                act.wait_ge(zeroed, 1)

                def take(i, b, u):
                    act.wait_ge(hist, u + 1)
                    for o in range(UC):
                        act.wait_ge(pj_ps, UC * u + o + 1)
                        nc.scalar.activation(U[b][:, o, 2:2 + T], PS[:, o], ACT.Identity, bias=bi[:, o:o + 1]).then_inc(pj_sb, 1)

                def spread(i, b, u):
                    for n in range(NTR):
                        act.wait_ge(tr_ps, NTR * u + n + 1)
                        c, blk = divmod(4 * n, T // BS)
                        for half in range(2):
                            src = PS[0:BS, 6 + n % 2].rearrange("p (r d two) -> p d r two", r=BPO, two=2)[:, :, :, half]
                            dst = RR[half * BS:(half + 1) * BS, c * 64:(c + 1) * 64, :, bass.ds(i * (T // OW) + blk // BPO, 1), b]
                            dst = dst.rearrange("p d r o -> p d (r o)")
                            op = nc.scalar.copy(dst, src)
                        op.then_inc(rr_s, 1)

                take(0, 0, 0)
                with act.Fori(0, TPB - 1) as i:
                    take(i, 1, NB * i + 1)
                    spread(i, 0, NB * i)
                    take(i + 1, 0, NB * i + 2)
                    spread(i, 1, NB * i + 1)
                last = TPB - 1
                take(last, 1, NB * last + 1)
                spread(last, 0, NB * last)
                spread(last, 1, NB * last + 1)

            @block.vector
            def _(dve):
                dve.wait_ge(W.loaded, W.all)
                for b in range(NB):
                    op = nc.vector.memset(U[b][:, :, 0:2], 0.0)
                op.then_inc(zeroed, 1)
                dve.wait_ge(zeroed, 1)
                dve.sem_inc(hist, NB)
                with dve.Fori(0, TPB) as i:
                    for b in range(NB):
                        u = NB * i + b
                        for n, o in enumerate((2, 3, 4, 5, 0, 1)):
                            dve.wait_ge(pj_sb, UC * u + o + 2)
                            c = o % DC
                            a = C[:]
                            at = 2 * (UC * u + n)
                            dve.wait_ge(uc_s, UC * u + n)
                            if n >= 3:
                                dve.wait_ge(v_s, DC * u + min(n - 2, DC))
                            nc.vector.tensor_scalar(a, U[b][:, o, 2:2 + T], fw[:, o, 2:3], fb[:, o:o + 1], ALU.mult, ALU.add).then_inc(tap_s, 1)
                            dve.wait_ge(tap_s, at + 1)
                            nc.vector.scalar_tensor_tensor(a, U[b][:, o, 1:1 + T], fw[:, o, 1:2], a, ALU.mult, ALU.add).then_inc(tap_s, 1)
                            dve.wait_ge(tap_s, at + 2)
                            dst = X0[:, c, tok(b, i)] if o < DC else X1[:, c] if o < 2 * DC else a
                            nc.vector.scalar_tensor_tensor(dst, U[b][:, o, 0:T], fw[:, o, 0:1], a, ALU.mult, ALU.add).then_inc(uc_s, 1)
                            if o >= 2 * DC:
                                dve.wait_ge(uc_s, UC * u + n + 1)
                                if c == 0:
                                    dve.wait_ge(v_free, u + 1)
                                    dve.wait_ge(turned, NTR * (u + 1))
                                nc.vector.tensor_tensor(backwards(Vt[b][:, c], 0, T), a, X1[:, c], ALU.mult).then_inc(v_s, 1)
                        dve.wait_ge(uc_s, UC * (u + 1))
                        nc.vector.tensor_copy(U[b][:, :, 0:2], U[b][:, :, T:T + 2]).then_inc(hist, 1)

            @block.gpsimd
            def _(pool):
                pool.sem_inc(v_free, NB)
                with pool.Fori(0, TPB) as i:
                    for b in range(NB):
                        pool.wait_ge(v_s, DC * (NB * i + b + 1))
                        pool.sem_inc(core.tick, 1)
                        for c in range(DC):
                            op = nc.gpsimd.tensor_copy(V[:, c, tok(b, i)], backwards(Vt[b][:, c], 0, T))
                        op.then_inc(v_free, 1)


def long_conv(core, RR):
    nc, PS = core.nc, core.PS
    zeroed, spread_s, y_ps, y_sb, y_done = (core.sem("lc_" + n) for n in "zeroed spread y_ps y_sb all".split())
    strip_in = [core.sem(f"lc_strip_in{k}") for k in range(2)]
    y_out = [core.sem(f"lc_y_out{k}") for k in range(2)]
    G = D // (2 * PAIRS)
    with ExitStack() as st:
        sb = lambda n, sh, d=F32: st.enter_context(nc.sbuf_tensor("lc_" + n, sh, d))
        strip = [sb(f"strip{k}", [P, PAIRS, HW]) for k in range(2)]
        blocks = [sb(f"blocks{k}", [P, PAIRS, BPO, (JPAD + NJ) // BPO, 2, NB]) for k in range(2)]
        Y = [sb(f"Y{k}", [P, OW]) for k in range(2)]
        with nc.Block() as block:

            @block.sync
            def _(sp):
                with sp.Fori(0, G // 2) as i:
                    for k in range(2):
                        g = 2 * i + k
                        sp.wait_ge(y_ps, g + 1)
                        for j in range(PAIRS):
                            src = bass.AP(core.kpad.tensor, (g * PAIRS + j) * 2 * KW + 1, [[KW, 2], [1, BS], [1, HW]])
                            sp.dma_start(strip[k][:, j], src).then_inc(strip_in[k], 16)

            @block.vector
            def _(dve):
                for k in range(2):
                    op = nc.vector.memset(blocks[k][:], 0.0)
                op.then_inc(zeroed, 1)
                dve.wait_ge(zeroed, 1)
                with dve.Fori(0, G // 2) as i:
                    for k in range(2):
                        g = 2 * i + k
                        dve.wait_ge(y_ps, g + 1)
                        for half in range(2):
                            rows = slice(half * BS, (half + 1) * BS)
                            for b in range(NB):
                                op = nc.vector.tensor_copy(blocks[k][rows, :, :, JPAD // BPO:, half, b],
                                                           RR[rows, bass.ds(g * PAIRS, PAIRS), :, :, b])
                        op.then_inc(spread_s, 1)

            @block.tensor
            def _(pe):
                pe.sem_inc(y_ps, 2)
                pe.sem_inc(y_sb, 1)
                with pe.Fori(0, G // 2) as i:
                    for k in range(2):
                        g = 2 * i + k
                        pe.wait_ge(spread_s, g + 1)
                        pe.wait_ge(strip_in[k], 16 * PAIRS * (i + 1))
                        pe.wait_ge(y_sb, g + 1)
                        for lag in LAGS:
                            for j in range(PAIRS):
                                q, r = divmod(JPAD - lag, BPO)
                                lhsT = blocks[k][:, j, r, q:q + NI].rearrange("p q c b -> p (q c b)")
                                mm = nc.tensor.matmul(PS[32 * j:32 * j + 32, k, 0:OW], lhsT,
                                                      strip[k][:, j, (lag - LAG0) * BS:(lag - LAG0) * BS + OW],
                                                      start=(lag == LAG0), stop=(lag == LAG1))
                        mm.then_inc(y_ps, 1)

            @block.scalar
            def _(act):
                for k in range(2):
                    act.sem_inc(y_out[k], 16)
                with act.Fori(0, G // 2) as i:
                    for k in range(2):
                        g = 2 * i + k
                        act.wait_ge(y_ps, g + 1 + 2)
                        act.wait_ge(y_out[k], 16 * (i + 1))
                        nc.scalar.copy(Y[k][:], PS[:, k, 0:OW]).then_inc(y_sb, 1)
                        act.wait_ge(y_sb, g + 2)
                        act.dma_start(core.y_dram[bass.ds(g * P, P)], Y[k][:]).then_inc(y_out[k], 16)
                for k in range(2):
                    act.wait_ge(y_out[k], 16 * (G // 2 + 1))


def conv_out(core, V, X0):
    nc, io, PS, X = core.nc, core.io, core.PS, core.X
    w_in, gbo_s, z_s, o_ps, o_sb, x_done = (core.sem("co_" + n) for n in "w_in gbo z o_ps o_sb x_done".split())
    y_in = [core.sem(f"co_y_in{b}") for b in range(NB)]
    y_view = core.y_dram.rearrange("(pr i ch b) t -> pr ch i b t", b=NB, i=NI, ch=2)
    with ExitStack() as st:
        sb = lambda n, sh, d=F32: st.enter_context(nc.sbuf_tensor("co_" + n, sh, d))
        wo, bo, gbo, fb = sb("wo", [P, DC, D]), sb("bo", [P, DC]), sb("gbo", [P, DC, NB]), sb("fb", [P, DC])
        yc = [sb(f"yc{b}", [P, DC, T]) for b in range(NB)]
        z = [sb(f"z{b}", [P, DC, T]) for b in range(NB)]
        y = [sb(f"y{b}", [P, DC, T]) for b in range(NB)]
        with nc.Block() as block:

            @block.sync
            def _(sp):
                sp.dma_start(wo[:], io["h_wout"].rearrange("(k p) o -> p k o", p=P)).then_inc(w_in, 16)
                sp.dma_start(bo[:], io["h_bout"]).then_inc(w_in, 16)
                sp.dma_start(fb[:], io["h_fb"]).then_inc(w_in, 16)

                def load(i, b):
                    for c in range(DC):
                        for k in range(T // OW):
                            src = y_view[c * P // 2:(c + 1) * P // 2, :, bass.ds(i * (T // OW) + k, 1), b]
                            sp.dma_start(yc[b][:, c, k * OW:(k + 1) * OW], src.rearrange("pr ch o t -> pr ch (o t)")).then_inc(y_in[b], 16)

                for b in range(NB):
                    load(0, b)
                with sp.Fori(1, TPB) as i:
                    for b in range(NB):
                        sp.wait_ge(z_s, 2 * (NB * (i - 1) + b) + 1)
                        load(i, b)

            @block.vector
            def _(dve):
                dve.wait_ge(w_in, 48)
                for b in range(NB):
                    nc.vector.tensor_tensor(gbo[:, :, b], core.mod[:, 1, GA, :, b], bo[:], ALU.mult).then_inc(gbo_s, 1)

                def prepare(i, b):
                    dve.wait_ge(y_in[b], 16 * DC * T // OW * (i + 1))
                    dve.wait_ge(o_ps, NB * i + b + 1)
                    for c in range(DC):
                        op = nc.vector.scalar_tensor_tensor(z[b][:, c], V[:, c, tok(b, i)], fb[:, c:c + 1], yc[b][:, c],
                                                            ALU.mult, ALU.add)
                    op.then_inc(z_s, 1)
                    dve.wait_ge(z_s, 2 * (NB * i + b) + 1)
                    nc.vector.tensor_tensor(z[b][:], z[b][:], X0[:, :, tok(b, i)], ALU.mult).then_inc(z_s, 1)

                def add(i, b):
                    dve.wait_ge(o_sb, NB * i + b + 2)
                    nc.vector.tensor_tensor(X[:, :, tok(b, i)], X[:, :, tok(b, i)], y[b][:], ALU.add).then_inc(x_done, 1)

                prepare(0, 0)
                with dve.Fori(0, TPB - 1) as i:
                    prepare(i, 1)
                    add(i, 0)
                    prepare(i + 1, 0)
                    add(i, 1)
                prepare(TPB - 1, 1)
                add(TPB - 1, 0)
                add(TPB - 1, 1)

            @block.tensor
            def _(pe):
                pe.sem_inc(o_ps, NB)
                pe.wait_ge(w_in, 48)
                pe.sem_inc(o_sb, 1)
                with pe.Fori(0, TPB) as i:
                    for b in range(NB):
                        pe.wait_ge(z_s, 2 * (NB * i + b + 1))
                        pe.wait_ge(o_sb, NB * i + 1)
                        for c in range(DC):
                            for k in range(DC):
                                mm = nc.tensor.matmul(PS[:, 2 * b + c], wo[:, k, c * P:(c + 1) * P], z[b][:, k],
                                                      start=(k == 0), stop=(k == DC - 1))
                        mm.then_inc(o_ps, 1)

            @block.scalar
            def _(act):
                act.wait_ge(gbo_s, NB)
                act.sem_inc(x_done, 1)
                with act.Fori(0, TPB) as i:
                    for b in range(NB):
                        act.wait_ge(o_ps, NB * i + b + 1 + NB)
                        act.wait_ge(x_done, NB * i + 1)
                        for c in range(DC):
                            op = nc.scalar.activation(y[b][:, c], PS[:, 2 * b + c], ACT.Identity,
                                                      bias=gbo[:, c, b:b + 1], scale=core.mod[:, 1, GA, c, b:b + 1])
                        op.then_inc(o_sb, 1)



NH1 = 8
HD1 = 64
INNER = NH1 * HD1
IC = INNER // P
WPT = T // P
HID = 682
HCS = [min(P, HID - o) for o in range(0, HID, P)]
HC = len(HCS)
NORM2_MIN = 1e-24
LN_SCALE = 2.0 ** 20


def shifted(Y, c, b, i):
    return Y[:, c, b, bass.ds(i * T + (0 if c else 1), T)]


def plain(Y, c, b, i):
    return Y[:, c, b, bass.ds(i * T + 1, T)]


QK = 2 * IC
UNITS = WPT * NH1 // 2
TR_LAG, OUT_LAG = 3, 5
SLOTS = UNITS - 1 + OUT_LAG
V_PIECE = QK + 2
PIECES = V_PIECE + WPT
PIECE_SLOT = (0, 1, 3, 5, 7, 8, 10, 12, 14, 15, 16, 17, 18, 19)


def attn1_weights(core, st, layer, place=None):
    io = core.io
    return Weights(core, st, f"a1{layer}_", [
        ("wqkv", [P, DC, 3 * INNER], [(WHOLE, by_chunk(io["wqkv"][layer]))]),
        ("wo", [P, IC, D], [(WHOLE, by_chunk(io["wo"][layer]))]),
        ("sc", [P, 2, 2], [(WHOLE, io["qk_scale"][layer])]),
        ("pairsum", [P, P], [(WHOLE, io["pairsum"])]),
        ("headsum", [P, 2], [(WHOLE, io["headsum"])]),
        ("tab", [P, 4, T], [(WHOLE, io["tables"].rearrange("a p t -> p a t")[:, :, 0:T])])], place)


def attn1(core, layer, Y, Yn, W):
    nc, io, PS = core.nc, core.io, core.PS
    tag = f"a1{layer}_"
    tab_in, hs, pj_ps, raw_s, sqr_s, kss_ps, qss_ps, t1_s, t2_s, kmax, klog, krn, ksum, roped, qmax, qlog, rq_s = (
        core.sem(tag + n) for n in
        "tab_in hs pj_ps raw sqr kss_ps qss_ps t1 t2 kmax klog krn ksum roped qmax qlog rq".split())
    v_ps, v_sb, hist, s_ps, mx_s, nb_s, exp_s, rsum_s, norm_s, tr_ps, pt_s, pv_ps, o_sb, wo_ps, y_done = (
        core.sem(tag + n) for n in
        "v_ps v_sb hist s_ps mx nb exp rsum norm tr_ps pt pv_ps o_sb wo_ps y_done".split())
    swapped_in = [core.sem(tag + f"swapped{k}") for k in range(2)]
    SC, TR, OB, PJ, V2, SS = (0, 1), (2, 3), 4, 5, 6, 7
    with ExitStack() as st:
        sb = lambda n, sh, d=F32: st.enter_context(nc.sbuf_tensor(tag + n, sh, d))
        wqkv, wo, sc, pairsum, headsum, tab = (W.buf[n] for n in "wqkv wo sc pairsum headsum tab".split())
        Hs = sb("Hs", [P, DC, T])
        raw = [sb(f"raw{k}", [P, T]) for k in range(2)]
        swapped = [sb(f"swapped{k}", [P, T]) for k in range(2)]
        sqr = [sb(f"sqr{k}", [P, T]) for k in range(2)]
        t1, t2, kn = sb("t1", [P, T]), sb("t2", [P, T]), sb("kn", [P, T])
        rn = [sb(f"rn{k}", [P, T]) for k in range(2)]
        QT = [sb(f"QT{b}", [P, IC, T]) for b in range(NB)]
        KT = [sb(f"KT{b}", [P, IC, P + T]) for b in range(NB)]
        V = [sb(f"V{b}", [P, 1 + WPT, INNER]) for b in range(NB)]
        rq = [sb(f"rq{b}", [P, WPT, NH1]) for b in range(NB)]
        mx, nb, sums, rsum = (sb(n, [P, WPT, NH1]) for n in ("mx", "nb", "sums", "rsum"))
        Pb = [sb(f"P{k}", [P, 2, 2 * P]) for k in range(4)]
        PTb = [sb(f"PT{k}", [P, 2, 2, P]) for k in range(4)]
        OT = sb("OT", [P, IC, T])

        def steps(eng, step):
            step(None, False, (0, 0, 0))
            step((0, 0, 0), True, (0, 1, 1))
            step((0, 1, 1), True, (1, 0, 2))
            with eng.Fori(1, TPB - 1) as i:
                step((i, 0, NB * i), False, (i, 1, NB * i + 1))
                step((i, 1, NB * i + 1), False, (i + 1, 0, NB * i + 2))
            i = TPB - 1
            step((i, 0, NB * i), False, (i, 1, NB * i + 1))
            step((i, 1, NB * i + 1), False, None)

        def slots(att, prj, attend, project, after=None):
            for s in range(SLOTS):
                if att:
                    attend(s)
                if prj:
                    for x in range(PIECES):
                        if PIECE_SLOT[x] == s:
                            project(x)
                if att and after:
                    after(s)

        def unit(s):
            return s // 4, s // 2 % 2, s % 2

        def heads(buf, s):
            w, g, h = unit(s)
            return buf[:, w, 4 * g:4 * g + 4].rearrange("p (j h) -> p j h", h=2)[:, :, h]

        def keys(s, first):
            return slice(P, 2 * P) if first and s < 4 else slice(0, 2 * P)

        def scores(s, ks):
            return PS[:, SC[s % 2]].rearrange("p (j t) -> p j t", j=2)[:, :, ks]

        with nc.Block() as block:

            @block.sync
            def _(sp):
                tables = io["tables"].rearrange("a p t -> p a t")
                half = HD1 // 2

                def step(att, first, prj):
                    if not prj:
                        return
                    i, b, u = prj
                    if b == 0 and not (isinstance(i, int) and i == 0):
                        sp.wait_ge(roped, QK * u)
                        sp.dma_start(tab[:], tables[:, :, bass.ds(i * T, T)]).then_inc(tab_in, 16)
                    for x in range(QK):
                        sp.wait_ge(raw_s, QK * u + x + 1)
                        if x >= 2:
                            sp.wait_ge(t2_s, QK * u + x - 1)
                        for r in range(0, P, half):
                            src = r + half if r % HD1 == 0 else r - half
                            sp.dma_start(swapped[x % 2][r:r + half, :], raw[x % 2][src:src + half, :]).then_inc(swapped_in[x % 2], 16)

                steps(sp, step)

            @block.gpsimd
            def _(pool):
                def step(att, first, prj):
                    if prj:
                        i, b, u = prj
                        if att:
                            pool.wait_ge(v_ps, WPT * u)
                            pool.sem_inc(core.tick, 1)
                        for c in range(DC):
                            op = nc.gpsimd.tensor_copy(Hs[:, c], shifted(Y, c, b, i))
                        op.then_inc(hs, 1)

                steps(pool, step)

            @block.tensor
            def _(pe):
                pe.wait_ge(W.loaded, W.all)
                masks = core.mask[:].rearrange("p a t -> p (a t)")

                def step(att, first, prj):
                    def attend(s):
                        _, b, u = att
                        if s == 0:
                            pe.wait_ge(roped, QK * (u + 1))
                            pe.wait_ge(v_sb, WPT * (u + 1))
                        if s < UNITS:
                            if s >= 2:
                                pe.wait_ge(exp_s, UNITS * u + s - 1)
                            w, g, h = unit(s)
                            ks, rows = keys(s, first), slice(HD1 * h, HD1 * (h + 1))
                            for j in range(2):
                                c = 2 * g + j
                                out = scores(s, ks)[:, j]
                                nc.tensor.matmul(out, core.lower[:], masks[:, ks], start=True, stop=True)
                                mm = nc.tensor.matmul(out, QT[b][rows, c, w * P:(w + 1) * P],
                                                      KT[b][rows, c, w * P + ks.start:w * P + ks.stop],
                                                      start=False, stop=True, skip_group_check=True)
                            mm.then_inc(s_ps, 1)
                        y = s - TR_LAG
                        if 0 <= y < UNITS:
                            pe.wait_ge(norm_s, UNITS * u + y + 1)
                            if y >= 2:
                                pe.wait_ge(pt_s, UNITS * u + y - 1)
                            elif not (isinstance(u, int) and u == 0):
                                pe.wait_ge(y_done, u)
                            for j in range(2):
                                for kb in range(keys(y, first).start // P, 2):
                                    mm = nc.tensor.transpose(PS[:, TR[y % 2], (2 * j + kb) * P:(2 * j + kb + 1) * P],
                                                             Pb[y % 4][:, j, kb * P:(kb + 1) * P], core.ident[:])
                            mm.then_inc(tr_ps, 1)

                    def project(x):
                        i, b, u = prj
                        again = not (isinstance(u, int) and u == 0)
                        y = x - 1
                        if 0 <= y < IC:
                            pe.wait_ge(sqr_s, QK * u + y + 1)
                            for w in range(WPT):
                                col = w * NH1 + 2 * y
                                mm = nc.tensor.matmul(PS[:, SS, col:col + 2], sqr[y % 2][:, w * P:(w + 1) * P], headsum[:],
                                                      start=True, stop=True)
                            mm.then_inc(qss_ps, 1)
                        elif IC <= y < QK:
                            pe.wait_ge(sqr_s, QK * u + y + 1)
                            if y == IC:
                                pe.wait_ge(qmax, u + 1)
                            else:
                                pe.wait_ge(kmax, IC * u + y - IC)
                            nc.tensor.matmul(PS[:, SS], pairsum[:], sqr[y % 2][:], start=True, stop=True).then_inc(kss_ps, 1)
                        if x < QK:
                            if x >= 1:
                                pe.wait_ge(sqr_s, QK * u + x)
                            elif again:
                                pe.wait_ge(v_sb, WPT * u)
                            for k in range(DC):
                                mm = nc.tensor.matmul(PS[:, PJ], wqkv[:, k, x * P:(x + 1) * P], shifted(Y, k, b, i),
                                                      start=(k == 0), stop=(k == DC - 1))
                            mm.then_inc(pj_ps, 1)
                        if x >= V_PIECE:
                            w = x - V_PIECE
                            if w == 0:
                                pe.wait_ge(hs, u + 1)
                            if w >= 2:
                                pe.wait_ge(v_sb, WPT * u + w - 1)
                            for k in range(DC):
                                mm = nc.tensor.matmul(PS[:, (PJ, V2)[w % 2]], Hs[:, k, w * P:(w + 1) * P], wqkv[:, k, 2 * INNER:],
                                                      start=(k == 0), stop=(k == DC - 1))
                            mm.then_inc(v_ps, 1)

                    def after(s):
                        _, b, u = att
                        if (s - OUT_LAG) % 2 or s < OUT_LAG:
                            return
                        q = (s - OUT_LAG) // 2
                        w, g, _ = unit(2 * q)
                        pe.wait_ge(pt_s, UNITS * u + 2 * q + 2)
                        if g == 0 and w >= 1:
                            pe.wait_ge(o_sb, WPT * u + w)
                        kbs = range(keys(2 * q, first).start // P, 2)
                        for j in range(2):
                            c = 2 * g + j
                            for kb in kbs:
                                for h in range(2):
                                    mm = nc.tensor.matmul(PS[HD1 * h:HD1 * (h + 1), OB, c * P:(c + 1) * P],
                                                          V[b][:, w + kb, (2 * c + h) * HD1:(2 * c + h + 1) * HD1],
                                                          PTb[(2 * q + h) % 4][:, j, kb], start=(kb == kbs[0]), stop=(kb == 1))
                        mm.then_inc(pv_ps, 1)

                    slots(att, prj, attend, project, after)
                    if att:
                        _, _, u = att
                        pe.wait_ge(o_sb, WPT * (u + 1))
                        for c in range(DC):
                            for k in range(IC):
                                mm = nc.tensor.matmul(PS[:, TR[c]], wo[:, k, c * P:(c + 1) * P], OT[:, k], start=(k == 0), stop=(k == IC - 1))
                        mm.then_inc(wo_ps, 1)

                steps(pe, step)

            @block.scalar
            def _(act):
                nc.scalar.preload_act_table_set("natural_log_exp_and_others")

                def step(att, first, prj):
                    def attend(s):
                        _, b, u = att
                        if s < UNITS:
                            act.wait_ge(nb_s, UNITS * u + s + 1)
                            if s >= 4:
                                act.wait_ge(tr_ps, UNITS * u + s - 3)
                            ks = keys(s, first)
                            for j in range(2):
                                op = nc.scalar.activation(Pb[s % 4][:, j, ks], scores(s, ks)[:, j], ACT.Exp,
                                                          bias=heads(nb, s)[:, j:j + 1], scale=heads(rq[b], s)[:, j:j + 1],
                                                          accum_out=heads(sums, s)[:, j:j + 1])
                            op.then_inc(exp_s, 1)

                    def project(x):
                        i, b, u = prj
                        y = x - 2
                        if IC <= y < QK:
                            n = IC * u + y - IC
                            act.wait_ge(kmax, n + 1)
                            nc.scalar.activation(rn[y % 2][:], rn[y % 2][:], ACT.Ln, scale=LN_SCALE).then_inc(klog, 1)
                            act.wait_ge(klog, n + 1)
                            nc.scalar.activation(rn[y % 2][:], rn[y % 2][:], ACT.Exp, scale=-0.5).then_inc(krn, 1)
                        if y == IC:
                            act.wait_ge(qmax, u + 1)
                            nc.scalar.activation(rq[b][:], rq[b][:], ACT.Ln, scale=LN_SCALE).then_inc(qlog, 1)
                            act.wait_ge(qlog, u + 1)
                            nc.scalar.activation(rq[b][:], rq[b][:], ACT.Exp, scale=-0.5).then_inc(rq_s, 1)
                        if x < QK:
                            act.wait_ge(pj_ps, QK * u + x + 1)
                            if x >= 2:
                                act.wait_ge(t1_s, QK * u + x - 1)
                                if x - 2 < IC:
                                    act.wait_ge(qss_ps, IC * u + x - 1)
                                else:
                                    act.wait_ge(kss_ps, IC * u + x - 1 - IC)
                                act.wait_ge(swapped_in[x % 2], 64 * (QK // 2 * u + x // 2))
                            nc.scalar.copy(raw[x % 2][:], PS[:, PJ]).then_inc(raw_s, 1)
                            nc.scalar.activation(sqr[x % 2][:], PS[:, PJ], ACT.Square).then_inc(sqr_s, 1)
                        if x >= V_PIECE:
                            w = x - V_PIECE
                            act.wait_ge(v_ps, WPT * u + w + 1)
                            if w == 0:
                                act.wait_ge(hist, u + 1)
                            nc.scalar.copy(V[b][:, 1 + w], PS[:, (PJ, V2)[w % 2]]).then_inc(v_sb, 1)

                    def after(s):
                        _, b, u = att
                        if s >= OUT_LAG + 2 and (s - OUT_LAG - 2) % 4 == 0:
                            w = (s - OUT_LAG - 2) // 4
                            act.wait_ge(pv_ps, UNITS // 2 * u + 2 * (w + 1))
                            nc.scalar.copy(OT[:, :, w * P:(w + 1) * P], PS[:, OB].rearrange("p (c t) -> p c t", c=IC)).then_inc(o_sb, 1)

                    slots(att, prj, attend, project, after)

                steps(act, step)

            @block.vector
            def _(dve):
                dve.wait_ge(W.loaded, W.all)

                def step(att, first, prj):
                    def attend(s):
                        _, b, u = att
                        if s == 0:
                            dve.wait_ge(rq_s, u + 1)
                        if s < UNITS:
                            n = UNITS * u + s
                            dve.wait_ge(s_ps, n + 1)
                            nc.vector.tensor_reduce(heads(mx, s), scores(s, keys(s, first)), AX_X, ALU.max).then_inc(mx_s, 1)
                            dve.wait_ge(mx_s, n + 1)
                            nc.vector.scalar_tensor_tensor(heads(nb, s), heads(mx, s), -1.0, heads(rq[b], s), ALU.mult, ALU.mult
                                                           ).then_inc(nb_s, 1)
                        if 1 <= s <= UNITS:
                            dve.wait_ge(exp_s, UNITS * u + s)
                            nc.vector.reciprocal(heads(rsum, s - 1), heads(sums, s - 1)).then_inc(rsum_s, 1)
                            dve.wait_ge(rsum_s, UNITS * u + s)
                            p, ks = Pb[(s - 1) % 4], keys(s - 1, first)
                            for j in range(2):
                                op = nc.vector.tensor_scalar(p[:, j, ks], p[:, j, ks], heads(rsum, s - 1)[:, j:j + 1], None, ALU.mult)
                            op.then_inc(norm_s, 1)
                        z = s - TR_LAG
                        if 0 <= z < UNITS:
                            kb = keys(z, first).start // P
                            dve.wait_ge(tr_ps, UNITS * u + z + 1)
                            if z >= 4:
                                dve.wait_ge(pv_ps, UNITS // 2 * u + z // 2 - 1)
                            src = PS[:, TR[z % 2]].rearrange("p (j k t) -> p j k t", j=2, k=2)
                            nc.vector.tensor_copy(PTb[z % 4][:, :, kb:], src[:, :, kb:]).then_inc(pt_s, 1)

                    def project(x):
                        i, b, u = prj
                        if x == 0:
                            if isinstance(i, int) and i == 0:
                                dve.sem_inc(hist, 1)
                            else:
                                nc.vector.tensor_copy(KT[b][:, :, 0:P], KT[b][:, :, T:T + P])
                                nc.vector.tensor_copy(V[b][:, 0], V[b][:, WPT]).then_inc(hist, 1)
                            if b == 0 and not (isinstance(i, int) and i == 0):
                                dve.wait_ge(tab_in, 16 * i)
                        y = x - 1
                        if IC <= y < QK:
                            m = IC * u + y - IC
                            dve.wait_ge(kss_ps, m + 1)
                            dve.wait_ge(roped, QK * u + y - 1)
                            nc.vector.tensor_scalar(rn[y % 2][:], PS[:, SS], NORM2_MIN, None, ALU.max).then_inc(kmax, 1)
                        y = x - 2
                        if IC <= y < QK:
                            m = IC * u + y - IC
                            dve.wait_ge(krn, m + 1)
                            dve.wait_ge(ksum, m + 1)
                            dve.wait_ge(hist, u + 1)
                            nc.vector.tensor_tensor(KT[b][:, y - IC, P:], kn[:], rn[y % 2][:], ALU.mult).then_inc(roped, 1)
                        y = x - 1
                        if 0 <= y < QK:
                            a, c = divmod(y, IC)
                            n, m = QK * u + y, IC * u + c
                            dve.wait_ge(raw_s, n + 1)
                            if 1 <= y <= IC:
                                dve.wait_ge(roped, n)
                            elif y > IC or not (isinstance(u, int) and u == 0):
                                dve.wait_ge(ksum, IC * u + max(y - IC, 0))
                            nc.vector.scalar_tensor_tensor(t1[:], raw[y % 2][:], sc[:, a, 0:1], tab[:, 2 * a], ALU.mult, ALU.mult
                                                           ).then_inc(t1_s, 1)
                            dve.wait_ge(swapped_in[y % 2], 64 * (QK // 2 * u + y // 2 + 1))
                            nc.vector.scalar_tensor_tensor(t2[:], swapped[y % 2][:], sc[:, a, 1:2], tab[:, 2 * a + 1], ALU.mult,
                                                           ALU.mult).then_inc(t2_s, 1)
                            if y == IC - 1:
                                dve.wait_ge(qss_ps, IC * (u + 1))
                                nc.vector.tensor_scalar(rq[b][:].rearrange("p w h -> p (w h)"), PS[:, SS, 0:WPT * NH1], NORM2_MIN,
                                                        None, ALU.max).then_inc(qmax, 1)
                            dve.wait_ge(t2_s, n + 1)
                            if a == 0:
                                nc.vector.tensor_tensor(QT[b][:, c], t1[:], t2[:], ALU.add).then_inc(roped, 1)
                            else:
                                if c >= 1:
                                    dve.wait_ge(roped, n)
                                nc.vector.tensor_tensor(kn[:], t1[:], t2[:], ALU.add).then_inc(ksum, 1)

                    slots(att, prj, attend, project)
                    if att:
                        i, b, u = att
                        dve.wait_ge(wo_ps, u + 1)
                        for c in range(DC):
                            op = nc.vector.tensor_tensor(plain(Yn, c, b, i), plain(Y, c, b, i), PS[:, TR[c]], ALU.add)
                        op.then_inc(y_done, 1)

                steps(dve, step)


def ffn1_weights(core, st, layer):
    io = core.io
    return Weights(core, st, f"f1{layer}_", [
        ("w1", [P, DC, 2 * HID], [(WHOLE, by_chunk(io["l_w1"][layer]))]), ("w2", [P, HC, D], [(WHOLE, io["l_w2"][layer])]),
        ("b1", [P, 2, HC], [(WHOLE, io["l_b1"][layer])]), ("b2", [P, DC], [(WHOLE, io["l_b2"][layer])])])


def ffn1(core, layer, Y, H, W, ahead):
    nc, io, PS = core.nc, core.io, core.PS
    tag = f"f1{layer}_"
    ag_ps, gelu_s, hid_s, w2_ps, y_done = (core.sem(tag + n) for n in "ag_ps gelu hid w2_ps y_done".split())
    lag = 2
    with ExitStack() as st:
        sb = lambda n, sh: st.enter_context(nc.sbuf_tensor(tag + n, sh, F32))
        w1, w2, b1, b2 = (W.buf[n] for n in "w1 w2 b1 b2".split())
        gl = [sb(f"gl{k}", [P, T]) for k in range(2)]
        hid = [sb(f"hid{k}", [P, T]) for k in range(4)]
        x_in = [core.sem(tag + f"x_in{b}") for b in range(NB)]
        out_s = core.sem(tag + "out")
        written = [core.sem(tag + f"written{b}") for b in range(NB)]
        xt = [sb(f"x{b}", [P, DC, T]) for b in range(NB)]
        last = ahead is None
        with nc.Block() as block:

            @block.sync
            def _(sp):
                if not last:
                    ahead.start(sp)
                    return
                x_view = core.x_dram.rearrange("(k p) t -> p k t", p=P)
                out_view = io["out"].rearrange("(k p) t -> p k t", p=P)
                for b in range(NB):
                    sp.dma_start(xt[b][:], x_view[:, :, b * S:b * S + T]).then_inc(x_in[b], 16)

                def write(i, b):
                    sp.wait_ge(out_s, NB * i + b + 1)
                    sp.dma_start(out_view[:, :, tok(b, i)], xt[b][:]).then_inc(written[b], 16)

                with sp.Fori(0, TPB - 1) as i:
                    for b in range(NB):
                        write(i, b)
                        sp.wait_ge(written[b], 16 * (i + 1))
                        sp.dma_start(xt[b][:], x_view[:, :, tok(b, i + 1)]).then_inc(x_in[b], 16)
                for b in range(NB):
                    write(TPB - 1, b)
                for b in range(NB):
                    sp.wait_ge(written[b], 16 * TPB)

            @block.tensor
            def _(pe):
                pe.wait_ge(W.loaded, W.all)
                pe.sem_inc(y_done, 1)
                with pe.Fori(0, TPB) as i:
                    for b in range(NB):
                        u = NB * i + b
                        for x in range(HC + lag):
                            if x < HC:
                                if x >= 2:
                                    pe.wait_ge(hid_s, HC * u + x - 1)
                                    pe.sem_inc(core.tick, 1)
                                for half in range(2):
                                    o = half * HID + x * P
                                    for k in range(DC):
                                        mm = nc.tensor.matmul(PS[0:HCS[x], 2 * (x % 2) + half], w1[:, k, o:o + HCS[x]],
                                                              H[:, k, tok(b, i)], start=(k == 0), stop=(k == DC - 1))
                                    mm.then_inc(ag_ps, 1)
                            z = x - lag
                            if z >= 0:
                                pe.wait_ge(hid_s, HC * u + z + 1)
                                if z == 0 and b == 0:
                                    pe.wait_ge(y_done, NB * i + 1)
                                for c in range(DC):
                                    mm = nc.tensor.matmul(PS[:, 4 + 2 * b + c], w2[0:HCS[z], z, c * P:(c + 1) * P],
                                                          hid[z % 4][0:HCS[z]], start=(z == 0), stop=(z == HC - 1))
                                mm.then_inc(w2_ps, 1)

            @block.scalar
            def _(act):
                nc.scalar.preload_act_table_set("gelu_and_others")
                act.wait_ge(W.loaded, W.all)
                with act.Fori(0, TPB) as i:
                    for b in range(NB):
                        u = NB * i + b
                        for x in range(HC):
                            g = HC * u + x
                            act.wait_ge(ag_ps, 2 * (g + 1))
                            nc.scalar.activation(gl[x % 2][0:HCS[x]], PS[0:HCS[x], 2 * (x % 2) + 1], ACT.Gelu,
                                                 bias=b1[0:HCS[x], 1, x:x + 1]).then_inc(gelu_s, 1)

            @block.vector
            def _(dve):
                dve.wait_ge(W.loaded, W.all)
                with dve.Fori(0, TPB) as i:
                    for b in range(NB):
                        u = NB * i + b
                        for x in range(HC):
                            g = HC * u + x
                            dve.wait_ge(gelu_s, g + 1)
                            if x >= 4:
                                dve.wait_ge(w2_ps, g - 3)
                            nc.vector.scalar_tensor_tensor(hid[x % 4][0:HCS[x]], PS[0:HCS[x], 2 * (x % 2)], b1[0:HCS[x], 0, x:x + 1],
                                                           gl[x % 2][0:HCS[x]], ALU.add, ALU.mult).then_inc(hid_s, 1)
                        dve.wait_ge(w2_ps, HC * (u + 1))
                        for c in range(DC):
                            y = plain(Y, c, b, i)
                            op = nc.vector.scalar_tensor_tensor(y, PS[:, 4 + 2 * b + c], b2[:, c:c + 1], y, ALU.add, ALU.add)
                        op.then_inc(y_done, 1)
                        if last:
                            dve.wait_ge(y_done, u + 2)
                            dve.wait_ge(x_in[b], 16 * (i + 1))
                            for c in range(DC):
                                op = nc.vector.scalar_tensor_tensor(xt[b][:, c], plain(Y, c, b, i), core.mod[:, 1, GB, c, b:b + 1],
                                                                    xt[b][:, c], ALU.mult, ALU.add)
                            op.then_inc(out_s, 1)


def local_layers(core):
    nc, io, mod = core.nc, core.io, core.mod
    saved, zeroed, zeroed_z, ln_in = (core.sem("ll_" + n) for n in "saved zeroed zeroed_z ln_in".split())
    padded = lambda n: nc.sbuf_tensor(n, [P, DC, NB, 1 + S], F32)
    with ExitStack() as st:
        Y = st.enter_context(padded("Y"))
        lgb = st.enter_context(nc.sbuf_tensor("lgb", [P, 2, 2, DC], F32))
        attn_w = [attn1_weights(core, st, 0)]
        attn_w.append(attn1_weights(core, st, 1, attn_w[0]))
        with nc.Block() as block:
            @block.sync
            def _(sp):
                sp.dma_start(lgb[:], io["l_ln"]).then_inc(ln_in, 16)
                sp.dma_start(core.x_dram.rearrange("(k p) t -> p k t", p=P), core.X[:]).then_inc(saved, 16)

            @block.gpsimd
            def _(pool):
                nc.gpsimd.memset(Y[:, :, :, 0:1], 0.0).then_inc(zeroed, 1)
                pool.wait_ge(zeroed, 1)
        layernorm(core, "ln3", lambda c, b, i: core.X[:, c, tok(b, i)], lambda c, b, i: plain(Y, c, b, i),
                  lambda c, b: mod[:, 1, CB, c, b:b + 1], lambda c, b: mod[:, 1, SB_, c, b:b + 1], attn_w[0])
        Z = core.XP[:].rearrange("p (c b t) -> p c b t", c=DC, b=NB)
        with nc.Block() as block:
            @block.gpsimd
            def _(pool):
                pool.wait_ge(saved, 16)
                pool.wait_ge(ln_in, 16)
                nc.gpsimd.memset(Z[:, :, :, 0:1], 0.0).then_inc(zeroed_z, 1)
                pool.wait_ge(zeroed_z, 1)
        for layer, (src, dst) in enumerate(((Y, Z), (Z, Y))):
            with nc.cleanup_on_exit():
                attn1(core, layer, src, dst, attn_w[layer])
                with ExitStack() as inner:
                    W = ffn1_weights(core, inner, layer)
                    H = inner.enter_context(nc.sbuf_tensor(f"H{3 + layer}", [P, DC, NB * S], F32))
                    layernorm(core, f"ln{4 + layer}", lambda c, b, i: shifted(dst, c, b, i), lambda c, b, i: H[:, c, tok(b, i)],
                              lambda c, b: lgb[:, layer, 0, c:c + 1], lambda c, b: lgb[:, layer, 1, c:c + 1], W)
                    ffn1(core, layer, dst, H, W, attn_w[1] if layer == 0 else None)


def program(nc, io):
    with ExitStack() as stack:
        core = Core(nc, stack, io)
        X, mod = core.X, core.mod
        setup(core)
        x_tile = lambda c, b, i: X[:, c, tok(b, i)]
        h_tile = lambda H: lambda c, b, i: H[:, c, tok(b, i)]
        modulated = lambda layer, w_scale, w_shift: (lambda c, b: mod[:, layer, w_scale, c, b:b + 1],
                                                     lambda c, b: mod[:, layer, w_shift, c, b:b + 1])
        with nc.cleanup_on_exit():
            with ExitStack() as st:
                W = attn0_project_weights(core, st)
                H = st.enter_context(nc.sbuf_tensor("H", [P, DC, NB * S], F32))
                layernorm(core, "ln0", x_tile, h_tile(H), *modulated(0, CA, SA), W)
                VV = st.enter_context(nc.sbuf_tensor("VV", [P, NB, NBLK, NH0, HD0 + 1], F32))
                attn0_project(core, H, VV, W)
                attn0_scores(core, VV)
            attn0_out(core)
        with nc.cleanup_on_exit():
            with ExitStack() as st:
                W = ffn0_weights(core, st)
                H = st.enter_context(nc.sbuf_tensor("H1", [P, DC, NB * S], F32))
                layernorm(core, "ln1", x_tile, h_tile(H), *modulated(0, CB, SB_), W)
                ffn0(core, H, W)
            filter_taps(core)
            with ExitStack() as st:
                V, X0 = (st.enter_context(nc.sbuf_tensor(n, [P, DC, NB * S], F32)) for n in ("V", "X0"))
                RR = st.enter_context(nc.sbuf_tensor("RR", [P, D // 2, BPO, NJ // BPO, NB], F32))
                with ExitStack() as inner:
                    W = conv_inputs_weights(core, inner)
                    H = inner.enter_context(nc.sbuf_tensor("H2", [P, DC, NB * S], F32))
                    layernorm(core, "ln2", x_tile, h_tile(H), *modulated(1, CA, SA), W)
                    conv_inputs(core, H, V, X0, RR, W)
                long_conv(core, RR)
                conv_out(core, V, X0)
        local_layers(core)




def columns(v):
    v = np.asarray(v)
    v = v.reshape(v.shape[:-1] + (-1, P))
    return np.moveaxis(v, -1, 0)


def filter_positions():
    f32 = np.float32
    t = np.linspace(0, 1, NT).astype(f32)
    w = (2 * np.pi * np.linspace(0, NT - 1, NT) / NT).astype(f32)
    fw = f32(1e-4) * w
    deltas = np.abs(np.linspace(np.log(0.01) / 1.5, np.log(0.01) / 0.3, D)).astype(f32)
    return {"f_z": np.stack([t, np.cos(fw), -np.sin(fw)]).astype(f32),
            "f_decay": (np.exp(-deltas[:, None] * t[None]) + f32(0.05)).astype(f32)}


def rotary_tables():
    f32 = np.float32
    half = np.arange(0, HD1, 2, dtype=f32)
    t = np.arange(S, dtype=f32)
    angle = t[:, None] * (1 / f32(10000) ** (half / f32(HD1))).astype(f32)[None]
    base = ((half + f32(0.4 * HD1)) / f32(1.4 * HD1)).astype(f32)
    power = ((t - S // 2) / f32(P // 2)).astype(f32)
    scale = base[None] ** power[:, None]
    cos, sin = np.cos(angle), np.sin(angle)
    up = f32(LN_SCALE ** 0.5)
    tables = np.stack([cos * scale * (8 * up), sin * scale * (8 * up), cos / scale * up, sin / scale * up]).transpose(0, 2, 1)
    sign = np.array([1, -1, 1, -1], f32)[:, None, None]
    return np.tile(np.concatenate([sign * tables, tables], 1), (1, P // HD1, 1)).astype(f32)


def head_matrices():
    head = np.arange(P) // HD1
    return {"pairsum": (head[:, None] == head[None]).astype(np.float32),
            "headsum": (head[:, None] == np.arange(2)[None]).astype(np.float32)}


def layout(d):
    d = {k: np.asarray(v) for k, v in d.items()}
    o = {"xT": d["L0_attn_x"].reshape(NB * S, D).T,
         "cT": np.stack([d["L0_c"], d["L1_c"]]).transpose(2, 0, 1),
         "wmod": np.stack([d["L0_wmod"], d["L1_wmod"]])}
    for n in ("Wq", "Wk", "Wv", "Wo"):
        o[n.lower() + "T"] = d["L0_attn_" + n].T
    for n in ("bq", "bk", "bv", "bo"):
        o[n] = columns(d["L0_attn_" + n])
    cross, shift = np.zeros((DC, P, P), np.float32), np.zeros((DC, P, P), np.float32)
    for h in range(NH0):
        c, r = h // HPC, h % HPC * HD0
        cross[c, r:r + HD0, r:r + HD0] = d["L0_attn_W_cross"][h]
        for f in range(HD0):
            n = min(MS0, HD0 - f)
            shift[c, r + f, r + f:r + f + n] = d["L0_attn_shift_weights"][h, :n]
    o["wc_bd"], o["shift_bd"] = cross, shift
    o["gate_rep"] = columns(np.repeat(d["L0_attn_gate"], HD0))
    for n in ("w1", "w2", "h1", "h2", "w3"):
        o[n + "T"] = d[f"L0_ffn_{n}_w"].T
        o[n + "s"] = columns(d[f"L0_ffn_{n}_s"])
    A = lambda n: d["L1_attn_" + n]
    o.update(filter_positions())
    for k in (1, 2, 3):
        o[f"f_w{k}"] = A(f"f_w{k}")
    o["f_bf"] = np.stack([np.stack([A(f"f_b{k}"), A(f"freq{k}")], -1) for k in (1, 2, 3)], 1)
    o["f_wout"], o["h_win"], o["h_wout"] = A("f_wout"), A("w_in"), A("w_out")
    o["h_bin"], o["h_sfb"], o["h_bout"], o["h_fb"] = (columns(A(n)) for n in ("b_in", "sf_b", "b_out", "filt_bias"))
    o["h_sfw"] = A("sf_w").reshape(UC, P, -1).transpose(1, 0, 2)
    F = lambda n: d["L1_ffn_" + n]
    depth = F("wqkv").shape[0]
    o["wqkv"], o["wo"], o["l_w1"] = F("wqkv"), F("wo"), F("w1")
    scale = np.stack([np.tile(F(n), (1, P // HD1)) for n in ("q_scale", "k_scale")], -1)
    halves = scale.reshape(depth, P // HD1, 2, HD1 // 2, 2)
    o["qk_scale"] = np.stack([scale, halves[:, :, ::-1].reshape(scale.shape)], -1)
    o["tables"] = rotary_tables()
    o.update(head_matrices())
    o["l_ln"] = columns(np.stack([F("ln_g"), F("ln_b")], 1))
    w2 = np.zeros((depth, HC * P, D), np.float32)
    w2[:, :HID] = F("w2")
    o["l_w2"] = w2.reshape(depth, HC, P, D).transpose(0, 2, 1, 3)
    b1 = np.zeros((depth, 2, HC * P), np.float32)
    b1[:, :, :HID] = F("b1").reshape(depth, 2, HID)
    o["l_b1"] = b1.reshape(depth, 2, HC, P).transpose(0, 3, 1, 2)
    o["l_b2"] = F("b2").reshape(depth, DC, P).transpose(0, 2, 1)
    return {k: np.ascontiguousarray(v) for k, v in o.items()}


def kernel(**inputs):
    import concourse.bacc as bacc
    from concourse.bass_utils import run_bass_kernel_spmd

    nc = bacc.Bacc("TRN2", target_bir_lowering=False, num_devices=1)
    arrays = {"in_" + k: v for k, v in layout(inputs).items()}
    io = {k[3:]: nc.dram_tensor(k, v.shape, mybir.dt.from_np(v.dtype), kind="ExternalInput").ap()
          for k, v in arrays.items()}
    io["out"] = nc.dram_tensor("out", (D, NB * S), F32, kind="ExternalOutput").ap()
    program(nc, io)
    r = run_bass_kernel_spmd(nc, [arrays], core_ids=[0])
    return np.ascontiguousarray(r.results[0]["out"].T).reshape(NB, S, D)
```
